# Optimizing a Trainium2 kernel written in Bass

```python
import numpy as np
import jax
import jax.numpy as jnp

def _softmax(x, axis=-1):
    return jax.nn.softmax(x, axis=axis)

def _gelu(x):
    return jax.nn.gelu(x, approximate=True)

def _silu(x):
    return jax.nn.silu(x)

def _sigmoid(x):
    return jax.nn.sigmoid(x)

def _layernorm(x, axis=-1, eps=1e-05):
    m = jnp.mean(x, axis=axis, keepdims=True)
    v = jnp.var(x, axis=axis, keepdims=True)
    return (x - m) / jnp.sqrt(v + eps)

def _scatter_add(tgt, idx, src, axis=0):
    return tgt.at[idx].add(src)

def _segment_sum(src, seg, n):
    return jax.ops.segment_sum(src, seg, n)
kernel_name = 'mk_xattn_ffn_d4_seqx_r8_e5c9c8'

def setup_inputs(seed: int=0):
    np.random.seed(seed)
    _w = jnp.asarray

    def _rec_inputs():
        import jax
        import jax.numpy as jnp
        _rk = jax.random.key(seed)
        x = 7.22e-05 + 1 * jax.random.normal(jax.random.fold_in(_rk, 1), (8, 128, 256), jnp.float32)
        _lenS = 128 - jax.random.randint(jax.random.fold_in(_rk, 7), (8,), 0, max(1, 128 // 4) + 1, jnp.int32)
        _lenS2 = 128 - jax.random.randint(jax.random.fold_in(_rk, 8), (8,), 0, max(1, 128 // 4) + 1, jnp.int32)
        _ctx_1024P = jax.random.normal(jax.random.fold_in(_rk, 11), (8, 16, 128), jnp.float32)
        _ctx_1024c = jax.random.dirichlet(jax.random.fold_in(_rk, 511), 0.3 * jnp.ones((16,), jnp.float32), (8, 128))
        _ctx_1024t = jnp.einsum('bsk,bkd->bsd', _ctx_1024c, _ctx_1024P)
        _ctx_1024t = _ctx_1024t * jax.lax.rsqrt(jnp.mean(jnp.square(_ctx_1024t)) + 1e-12) * 0.953939
        ctx_1024 = -1.39393e-06 + 0.999914 * (_ctx_1024t + 0.3 * jax.random.normal(jax.random.fold_in(_rk, 611), (8, 128, 128), jnp.float32))
        fside_BxSx2_0 = jax.random.uniform(jax.random.fold_in(_rk, 12), (8, 128, 2), jnp.float32, 0.0, 0.999707)
        _validS = jnp.arange(128)[None, :] < _lenS[:, None]
        _validS2 = jnp.arange(128)[None, :] < _lenS2[:, None]
        _causal = jnp.tril(jnp.ones((128, 128), dtype=bool))
        mask_BxS2_bf1 = jnp.ones((8, 128), dtype=bool)
        return (x, ctx_1024, fside_BxSx2_0, mask_BxS2_bf1)
    x, ctx_1024, fside_BxSx2_0, mask_BxS2_bf1 = _rec_inputs()

    def _L0_xattn_setup():
        import jax, jax.numpy as jnp
        import numpy as np
        DIM = 256
        CTX_DIM = 128
        N_HEADS = 32
        HEAD_DIM = DIM // N_HEADS
        POS_DIM = 2
        B, N, CTXN = (2, 256, 256)
        ROPE_BASE = 10000.0

        def apply_axial_rope(x, pos):
            b, n, h, d = x.shape
            p = pos.shape[-1]
            dpa = d // p
            half = dpa // 2
            freqs = ROPE_BASE ** (-jnp.arange(half, dtype=x.dtype) / half)
            ang = pos[..., :, None] * freqs
            cos = jnp.cos(ang)[:, :, None, :, :]
            sin = jnp.sin(ang)[:, :, None, :, :]
            xr = x.reshape(b, n, h, p, half, 2)
            x1, x2 = (xr[..., 0], xr[..., 1])
            out = jnp.stack([x1 * cos - x2 * sin, x1 * sin + x2 * cos], axis=-1)
            return out.reshape(b, n, h, d)
        key = jax.random.key(seed)
        ks = jax.random.split(key, 8)
        x = jax.random.normal(ks[0], (B, N, DIM), jnp.float32)
        ctx = jax.random.normal(ks[1], (B, CTXN, CTX_DIM), jnp.float32)
        pos_map = jax.random.uniform(ks[2], (B, N, POS_DIM), jnp.float32)
        ctx_pos_map = jax.random.uniform(ks[3], (B, CTXN, POS_DIM), jnp.float32)
        Wq = jax.random.normal(ks[4], (DIM, DIM), jnp.float32) / np.sqrt(DIM)
        Wkv = jax.random.normal(ks[5], (CTX_DIM, 2 * DIM), jnp.float32) / np.sqrt(CTX_DIM)
        Wout = jax.random.normal(ks[6], (DIM, DIM), jnp.float32) / np.sqrt(DIM)
        bout = jnp.zeros((DIM,), jnp.float32)
        return {'x': x, 'ctx': ctx, 'pos_map': pos_map, 'ctx_pos_map': ctx_pos_map, 'Wq': Wq, 'Wkv': Wkv, 'Wout': Wout, 'bout': bout}
    _L0_xattn_all = _L0_xattn_setup()
    _L0_xattn_in = {k: v for k, v in _L0_xattn_all.items() if k in ('Wq', 'Wkv', 'Wout', 'bout')}
    del _L0_xattn_all

    def _L0_ffn_setup():
        import jax, jax.numpy as jnp
        import numpy as np
        TOP_K = 4
        key = jax.random.key(seed)
        ks = jax.random.split(key, 8)
        B, S, D, E, H, HS = (2, 256, 256, 16, 128, 512)
        scaled = lambda k, shape, fan: jax.random.normal(k, shape, jnp.float32) * fan ** (-0.5)
        return {'x': jax.random.normal(ks[0], (B, S, D), jnp.float32), 'w_router': scaled(ks[1], (D, E), D), 'we1': scaled(ks[2], (E, D, H), D), 'we3': scaled(ks[3], (E, D, H), D), 'we2': scaled(ks[4], (E, H, D), H), 'ws1': scaled(ks[5], (D, HS), D), 'ws3': scaled(ks[6], (D, HS), D), 'ws2': scaled(ks[7], (HS, D), HS)}
    _L0_ffn_all = _L0_ffn_setup()
    _L0_ffn_in = {k: v for k, v in _L0_ffn_all.items() if k in ('w_router', 'we1', 'we3', 'we2', 'ws1', 'ws3', 'ws2')}
    del _L0_ffn_all

    def _L1_xattn_setup():
        import jax, jax.numpy as jnp
        import numpy as np
        N_HEADS = 16
        N_KV_HEADS = 8
        HEAD_DIM = 128
        D_TEXT = 256
        D_VISION = 128
        GROUPS = N_HEADS // N_KV_HEADS
        key = jax.random.key(seed)
        ks = jax.random.split(key, 6)
        B, T_text, T_vis = (4, 256, 72)
        text_hidden = jax.random.normal(ks[0], (B, T_text, D_TEXT), dtype=jnp.float32)
        vision_tokens = jax.random.normal(ks[1], (B, T_vis, D_VISION), dtype=jnp.float32)
        vision_mask = jnp.ones((B, T_vis), dtype=bool)
        s = 0.02
        Wq = jax.random.normal(ks[2], (D_TEXT, N_HEADS * HEAD_DIM), dtype=jnp.float32) * s
        Wk = jax.random.normal(ks[3], (D_VISION, N_KV_HEADS * HEAD_DIM), dtype=jnp.float32) * s
        Wv = jax.random.normal(ks[4], (D_VISION, N_KV_HEADS * HEAD_DIM), dtype=jnp.float32) * s
        Wo = jax.random.normal(ks[5], (N_HEADS * HEAD_DIM, D_TEXT), dtype=jnp.float32) * s
        return {'text_hidden': text_hidden, 'vision_tokens': vision_tokens, 'vision_mask': vision_mask, 'Wq': Wq, 'Wk': Wk, 'Wv': Wv, 'Wo': Wo}
    _L1_xattn_all = _L1_xattn_setup()
    _L1_xattn_in = {k: v for k, v in _L1_xattn_all.items() if k in ('Wq', 'Wk', 'Wv', 'Wo')}
    del _L1_xattn_all

    def _L1_ffn_setup():
        import jax, jax.numpy as jnp
        import numpy as np
        _FP8_MAX = 448.0
        _BLOCK = 32
        _EPS = 1e-30

        def _mx_dequant(t):
            rows, feat = t.shape
            blocks = t.reshape(rows, feat // _BLOCK, _BLOCK)
            max_abs = jnp.max(jnp.abs(blocks), axis=-1)
            scales = jnp.maximum(max_abs / _FP8_MAX, _EPS)
            q = (blocks / scales[..., None]).astype(jnp.float8_e4m3fn).astype(jnp.float32)
            return (q * scales[..., None]).reshape(rows, feat)

        def _mx_linear(x2d, w):
            return _mx_dequant(x2d) @ _mx_dequant(w).T
        key = jax.random.key(seed)
        k1, k2, k3, k4 = jax.random.split(key, 4)
        B, S, H, I = (2, 128, 256, 1024)
        return {'x': jax.random.normal(k1, (B, S, H), dtype=jnp.float32), 'gate_w': jax.random.normal(k2, (I, H), dtype=jnp.float32) * 0.02, 'up_w': jax.random.normal(k3, (I, H), dtype=jnp.float32) * 0.02, 'down_w': jax.random.normal(k4, (H, I), dtype=jnp.float32) * 0.02}
    _L1_ffn_all = _L1_ffn_setup()
    _L1_ffn_in = {k: v for k, v in _L1_ffn_all.items() if k in ('gate_w', 'up_w', 'down_w')}
    del _L1_ffn_all

    def _L2_xattn_setup():
        import jax, jax.numpy as jnp
        import numpy as np
        DIM = 256
        CTX_DIM = 128
        N_HEADS = 32
        HEAD_DIM = DIM // N_HEADS
        POS_DIM = 2
        B, N, CTXN = (2, 256, 256)
        ROPE_BASE = 10000.0

        def apply_axial_rope(x, pos):
            b, n, h, d = x.shape
            p = pos.shape[-1]
            dpa = d // p
            half = dpa // 2
            freqs = ROPE_BASE ** (-jnp.arange(half, dtype=x.dtype) / half)
            ang = pos[..., :, None] * freqs
            cos = jnp.cos(ang)[:, :, None, :, :]
            sin = jnp.sin(ang)[:, :, None, :, :]
            xr = x.reshape(b, n, h, p, half, 2)
            x1, x2 = (xr[..., 0], xr[..., 1])
            out = jnp.stack([x1 * cos - x2 * sin, x1 * sin + x2 * cos], axis=-1)
            return out.reshape(b, n, h, d)
        key = jax.random.key(seed)
        ks = jax.random.split(key, 8)
        x = jax.random.normal(ks[0], (B, N, DIM), jnp.float32)
        ctx = jax.random.normal(ks[1], (B, CTXN, CTX_DIM), jnp.float32)
        pos_map = jax.random.uniform(ks[2], (B, N, POS_DIM), jnp.float32)
        ctx_pos_map = jax.random.uniform(ks[3], (B, CTXN, POS_DIM), jnp.float32)
        Wq = jax.random.normal(ks[4], (DIM, DIM), jnp.float32) / np.sqrt(DIM)
        Wkv = jax.random.normal(ks[5], (CTX_DIM, 2 * DIM), jnp.float32) / np.sqrt(CTX_DIM)
        Wout = jax.random.normal(ks[6], (DIM, DIM), jnp.float32) / np.sqrt(DIM)
        bout = jnp.zeros((DIM,), jnp.float32)
        return {'x': x, 'ctx': ctx, 'pos_map': pos_map, 'ctx_pos_map': ctx_pos_map, 'Wq': Wq, 'Wkv': Wkv, 'Wout': Wout, 'bout': bout}
    _L2_xattn_all = _L2_xattn_setup()
    _L2_xattn_in = {k: v for k, v in _L2_xattn_all.items() if k in ('Wq', 'Wkv', 'Wout', 'bout')}
    del _L2_xattn_all

    def _L2_ffn_setup():
        import jax, jax.numpy as jnp
        import numpy as np
        DIM_IN = 256
        DIM_HIDDEN = 1024
        key = jax.random.key(seed)
        k_x, k_g, k_u, k_d = jax.random.split(key, 4)
        s_in = 1.0 / np.sqrt(DIM_IN)
        s_hid = 1.0 / np.sqrt(DIM_HIDDEN)
        x = jax.random.normal(k_x, (4, 256, DIM_IN), dtype=jnp.float32)
        w_gate = jax.random.uniform(k_g, (DIM_HIDDEN, DIM_IN), jnp.float32, -s_in, s_in)
        w_up = jax.random.uniform(k_u, (DIM_HIDDEN, DIM_IN), jnp.float32, -s_in, s_in)
        w_down = jax.random.uniform(k_d, (DIM_IN, DIM_HIDDEN), jnp.float32, -s_hid, s_hid)
        return {'x': x, 'w_gate': w_gate, 'w_up': w_up, 'w_down': w_down}
    _L2_ffn_all = _L2_ffn_setup()
    _L2_ffn_in = {k: v for k, v in _L2_ffn_all.items() if k in ('w_gate', 'w_up', 'w_down')}
    del _L2_ffn_all

    def _L3_xattn_setup():
        import jax, jax.numpy as jnp
        import numpy as np
        DIM = 256
        CTX_DIM = 128
        N_HEADS = 32
        HEAD_DIM = DIM // N_HEADS
        POS_DIM = 2
        B, N, CTXN = (2, 256, 256)
        ROPE_BASE = 10000.0

        def apply_axial_rope(x, pos):
            b, n, h, d = x.shape
            p = pos.shape[-1]
            dpa = d // p
            half = dpa // 2
            freqs = ROPE_BASE ** (-jnp.arange(half, dtype=x.dtype) / half)
            ang = pos[..., :, None] * freqs
            cos = jnp.cos(ang)[:, :, None, :, :]
            sin = jnp.sin(ang)[:, :, None, :, :]
            xr = x.reshape(b, n, h, p, half, 2)
            x1, x2 = (xr[..., 0], xr[..., 1])
            out = jnp.stack([x1 * cos - x2 * sin, x1 * sin + x2 * cos], axis=-1)
            return out.reshape(b, n, h, d)
        key = jax.random.key(seed)
        ks = jax.random.split(key, 8)
        x = jax.random.normal(ks[0], (B, N, DIM), jnp.float32)
        ctx = jax.random.normal(ks[1], (B, CTXN, CTX_DIM), jnp.float32)
        pos_map = jax.random.uniform(ks[2], (B, N, POS_DIM), jnp.float32)
        ctx_pos_map = jax.random.uniform(ks[3], (B, CTXN, POS_DIM), jnp.float32)
        Wq = jax.random.normal(ks[4], (DIM, DIM), jnp.float32) / np.sqrt(DIM)
        Wkv = jax.random.normal(ks[5], (CTX_DIM, 2 * DIM), jnp.float32) / np.sqrt(CTX_DIM)
        Wout = jax.random.normal(ks[6], (DIM, DIM), jnp.float32) / np.sqrt(DIM)
        bout = jnp.zeros((DIM,), jnp.float32)
        return {'x': x, 'ctx': ctx, 'pos_map': pos_map, 'ctx_pos_map': ctx_pos_map, 'Wq': Wq, 'Wkv': Wkv, 'Wout': Wout, 'bout': bout}
    _L3_xattn_all = _L3_xattn_setup()
    _L3_xattn_in = {k: v for k, v in _L3_xattn_all.items() if k in ('Wq', 'Wkv', 'Wout', 'bout')}
    del _L3_xattn_all

    def _L3_ffn_setup():
        import jax, jax.numpy as jnp
        import numpy as np
        N_GROUPS = 4
        TOPK_GROUPS = 2
        TOPK = 4
        ROUTE_SCALE = 1.0

        def _gate(xt, gate_w):
            T = xt.shape[0]
            E = gate_w.shape[0]
            scores = jax.nn.sigmoid(xt @ gate_w.T)
            original_scores = scores
            sg = scores.reshape(T, N_GROUPS, E // N_GROUPS)
            group_scores = sg.max(axis=-1)
            _, gidx = jax.lax.top_k(group_scores, TOPK_GROUPS)
            gmask = jax.nn.one_hot(gidx, N_GROUPS, dtype=scores.dtype).sum(axis=1)
            masked = (sg * gmask[:, :, None]).reshape(T, E)
            _, idx = jax.lax.top_k(masked, TOPK)
            w = jnp.take_along_axis(original_scores, idx, axis=-1)
            w = w / w.sum(axis=-1, keepdims=True) * ROUTE_SCALE
            return (w, idx)
        key = jax.random.key(seed)
        ks = jax.random.split(key, 8)
        B, S, D = (1, 256, 256)
        E, I = (16, 176)
        SH = 2 * I
        s = 0.02
        return {'x': jax.random.normal(ks[0], (B, S, D), dtype=jnp.float32), 'gate_w': jax.random.normal(ks[1], (E, D), dtype=jnp.float32) * s, 'W1': jax.random.normal(ks[2], (E, I, D), dtype=jnp.float32) * s, 'W2': jax.random.normal(ks[3], (E, D, I), dtype=jnp.float32) * s, 'W3': jax.random.normal(ks[4], (E, I, D), dtype=jnp.float32) * s, 'Ws1': jax.random.normal(ks[5], (SH, D), dtype=jnp.float32) * s, 'Ws2': jax.random.normal(ks[6], (D, SH), dtype=jnp.float32) * s, 'Ws3': jax.random.normal(ks[7], (SH, D), dtype=jnp.float32) * s}
    _L3_ffn_all = _L3_ffn_setup()
    _L3_ffn_in = {k: v for k, v in _L3_ffn_all.items() if k in ('gate_w', 'W1', 'W2', 'W3', 'Ws1', 'Ws2', 'Ws3')}
    del _L3_ffn_all
    return {'x': x, 'ctx_1024': ctx_1024, 'fside_BxSx2_0': fside_BxSx2_0, 'mask_BxS2_bf1': mask_BxS2_bf1, 'L0_xattn_Wq': _L0_xattn_in['Wq'], 'L0_xattn_Wkv': _L0_xattn_in['Wkv'], 'L0_xattn_Wout': _L0_xattn_in['Wout'], 'L0_xattn_bout': _L0_xattn_in['bout'], 'L0_ffn_w_router': _L0_ffn_in['w_router'], 'L0_ffn_we1': _L0_ffn_in['we1'], 'L0_ffn_we3': _L0_ffn_in['we3'], 'L0_ffn_we2': _L0_ffn_in['we2'], 'L0_ffn_ws1': _L0_ffn_in['ws1'], 'L0_ffn_ws3': _L0_ffn_in['ws3'], 'L0_ffn_ws2': _L0_ffn_in['ws2'], 'L1_xattn_Wq': _L1_xattn_in['Wq'], 'L1_xattn_Wk': _L1_xattn_in['Wk'], 'L1_xattn_Wv': _L1_xattn_in['Wv'], 'L1_xattn_Wo': _L1_xattn_in['Wo'], 'L1_ffn_gate_w': _L1_ffn_in['gate_w'], 'L1_ffn_up_w': _L1_ffn_in['up_w'], 'L1_ffn_down_w': _L1_ffn_in['down_w'], 'L2_xattn_Wq': _L2_xattn_in['Wq'], 'L2_xattn_Wkv': _L2_xattn_in['Wkv'], 'L2_xattn_Wout': _L2_xattn_in['Wout'], 'L2_xattn_bout': _L2_xattn_in['bout'], 'L2_ffn_w_gate': _L2_ffn_in['w_gate'], 'L2_ffn_w_up': _L2_ffn_in['w_up'], 'L2_ffn_w_down': _L2_ffn_in['w_down'], 'L3_xattn_Wq': _L3_xattn_in['Wq'], 'L3_xattn_Wkv': _L3_xattn_in['Wkv'], 'L3_xattn_Wout': _L3_xattn_in['Wout'], 'L3_xattn_bout': _L3_xattn_in['bout'], 'L3_ffn_gate_w': _L3_ffn_in['gate_w'], 'L3_ffn_W1': _L3_ffn_in['W1'], 'L3_ffn_W2': _L3_ffn_in['W2'], 'L3_ffn_W3': _L3_ffn_in['W3'], 'L3_ffn_Ws1': _L3_ffn_in['Ws1'], 'L3_ffn_Ws2': _L3_ffn_in['Ws2'], 'L3_ffn_Ws3': _L3_ffn_in['Ws3']}

def reference(x, ctx_1024, fside_BxSx2_0, mask_BxS2_bf1, L0_xattn_Wq, L0_xattn_Wkv, L0_xattn_Wout, L0_xattn_bout, L0_ffn_w_router, L0_ffn_we1, L0_ffn_we3, L0_ffn_we2, L0_ffn_ws1, L0_ffn_ws3, L0_ffn_ws2, L1_xattn_Wq, L1_xattn_Wk, L1_xattn_Wv, L1_xattn_Wo, L1_ffn_gate_w, L1_ffn_up_w, L1_ffn_down_w, L2_xattn_Wq, L2_xattn_Wkv, L2_xattn_Wout, L2_xattn_bout, L2_ffn_w_gate, L2_ffn_w_up, L2_ffn_w_down, L3_xattn_Wq, L3_xattn_Wkv, L3_xattn_Wout, L3_xattn_bout, L3_ffn_gate_w, L3_ffn_W1, L3_ffn_W2, L3_ffn_W3, L3_ffn_Ws1, L3_ffn_Ws2, L3_ffn_Ws3):
    import jax
    import jax.numpy as jnp

    def _L0_xattn_ref(x, ctx, pos_map, ctx_pos_map, Wq, Wkv, Wout, bout):
        import jax, jax.numpy as jnp
        import numpy as np
        DIM = 256
        CTX_DIM = 128
        N_HEADS = 32
        HEAD_DIM = DIM // N_HEADS
        POS_DIM = 2
        B, N, CTXN = (2, 256, 256)
        ROPE_BASE = 10000.0

        def apply_axial_rope(x, pos):
            b, n, h, d = x.shape
            p = pos.shape[-1]
            dpa = d // p
            half = dpa // 2
            freqs = ROPE_BASE ** (-jnp.arange(half, dtype=x.dtype) / half)
            ang = pos[..., :, None] * freqs
            cos = jnp.cos(ang)[:, :, None, :, :]
            sin = jnp.sin(ang)[:, :, None, :, :]
            xr = x.reshape(b, n, h, p, half, 2)
            x1, x2 = (xr[..., 0], xr[..., 1])
            out = jnp.stack([x1 * cos - x2 * sin, x1 * sin + x2 * cos], axis=-1)
            return out.reshape(b, n, h, d)
        b, n, _ = x.shape
        ctx_n = ctx.shape[1]
        q = (x @ Wq).reshape(b, n, N_HEADS, HEAD_DIM)
        k, v = jnp.split(ctx @ Wkv, 2, axis=-1)
        k = k.reshape(b, ctx_n, N_HEADS, HEAD_DIM)
        v = v.reshape(b, ctx_n, N_HEADS, HEAD_DIM)
        q = apply_axial_rope(q, pos_map)
        k = apply_axial_rope(k, ctx_pos_map)
        scale = 1.0 / np.sqrt(HEAD_DIM).astype(np.float32)
        logits = jnp.einsum('bqhd,bkhd->bhqk', q, k) * scale
        w = jax.nn.softmax(logits, axis=-1)
        attn = jnp.einsum('bhqk,bkhd->bqhd', w, v)
        attn = attn.reshape(b, n, N_HEADS * HEAD_DIM)
        return attn @ Wout + bout

    def _L0_ffn_ref(x, w_router, we1, we3, we2, ws1, ws3, ws2):
        import jax, jax.numpy as jnp
        import numpy as np
        TOP_K = 4
        B, S, D = x.shape
        T = B * S
        E = w_router.shape[1]
        xt = x.reshape(T, D)
        probs = jax.nn.softmax(xt @ w_router, axis=-1)
        top_w, top_i = jax.lax.top_k(probs, TOP_K)
        top_w = top_w / jnp.sum(top_w, axis=-1, keepdims=True)
        cw = jnp.zeros((T, E), xt.dtype).at[jnp.arange(T)[:, None], top_i].add(top_w)
        g = jax.nn.silu(jnp.einsum('td,edh->teh', xt, we1)) * jnp.einsum('td,edh->teh', xt, we3)
        g = g * cw[:, :, None]
        moe_out = jnp.einsum('teh,ehd->td', g, we2)
        shared = jax.nn.silu(xt @ ws1) * (xt @ ws3) @ ws2
        k = TOP_K
        out = shared / (k + 1) + moe_out * (k / (k + 1))
        return out.reshape(B, S, D)

    def _L1_xattn_ref(text_hidden, vision_tokens, vision_mask, Wq, Wk, Wv, Wo):
        import jax, jax.numpy as jnp
        import numpy as np
        N_HEADS = 16
        N_KV_HEADS = 8
        HEAD_DIM = 128
        D_TEXT = 256
        D_VISION = 128
        GROUPS = N_HEADS // N_KV_HEADS
        B, T_text, _ = text_hidden.shape
        T_vis = vision_tokens.shape[1]
        scale = jnp.float32(np.sqrt(HEAD_DIM))
        q = (text_hidden @ Wq).reshape(B, T_text, N_HEADS, HEAD_DIM).transpose(0, 2, 1, 3)
        k = (vision_tokens @ Wk).reshape(B, T_vis, N_KV_HEADS, HEAD_DIM).transpose(0, 2, 1, 3)
        v = (vision_tokens @ Wv).reshape(B, T_vis, N_KV_HEADS, HEAD_DIM).transpose(0, 2, 1, 3)
        k = jnp.repeat(k, GROUPS, axis=1)
        v = jnp.repeat(v, GROUPS, axis=1)
        scores = jnp.einsum('bhtd,bhsd->bhts', q, k) / scale
        mask = vision_mask[:, None, None, :]
        scores = jnp.where(mask, scores, -jnp.inf)
        attn = jax.nn.softmax(scores, axis=-1)
        attn = jnp.nan_to_num(attn, nan=0.0)
        out = jnp.einsum('bhts,bhsd->bhtd', attn, v)
        out = out.transpose(0, 2, 1, 3).reshape(B, T_text, N_HEADS * HEAD_DIM)
        return out @ Wo

    def _L1_ffn_ref(x, gate_w, up_w, down_w):
        import jax, jax.numpy as jnp
        import numpy as np
        _FP8_MAX = 448.0
        _BLOCK = 32
        _EPS = 1e-30

        def _mx_dequant(t):
            rows, feat = t.shape
            blocks = t.reshape(rows, feat // _BLOCK, _BLOCK)
            max_abs = jnp.max(jnp.abs(blocks), axis=-1)
            scales = jnp.maximum(max_abs / _FP8_MAX, _EPS)
            q = (blocks / scales[..., None]).astype(jnp.float8_e4m3fn).astype(jnp.float32)
            return (q * scales[..., None]).reshape(rows, feat)

        def _mx_linear(x2d, w):
            return _mx_dequant(x2d) @ _mx_dequant(w).T
        B, S, H = x.shape
        x2d = x.reshape(B * S, H)
        gate = _mx_linear(x2d, gate_w)
        up = _mx_linear(x2d, up_w)
        h = jax.nn.silu(gate) * up
        out = _mx_linear(h, down_w)
        return out.reshape(B, S, H)

    def _L2_xattn_ref(x, ctx, pos_map, ctx_pos_map, Wq, Wkv, Wout, bout):
        import jax, jax.numpy as jnp
        import numpy as np
        DIM = 256
        CTX_DIM = 128
        N_HEADS = 32
        HEAD_DIM = DIM // N_HEADS
        POS_DIM = 2
        B, N, CTXN = (2, 256, 256)
        ROPE_BASE = 10000.0

        def apply_axial_rope(x, pos):
            b, n, h, d = x.shape
            p = pos.shape[-1]
            dpa = d // p
            half = dpa // 2
            freqs = ROPE_BASE ** (-jnp.arange(half, dtype=x.dtype) / half)
            ang = pos[..., :, None] * freqs
            cos = jnp.cos(ang)[:, :, None, :, :]
            sin = jnp.sin(ang)[:, :, None, :, :]
            xr = x.reshape(b, n, h, p, half, 2)
            x1, x2 = (xr[..., 0], xr[..., 1])
            out = jnp.stack([x1 * cos - x2 * sin, x1 * sin + x2 * cos], axis=-1)
            return out.reshape(b, n, h, d)
        b, n, _ = x.shape
        ctx_n = ctx.shape[1]
        q = (x @ Wq).reshape(b, n, N_HEADS, HEAD_DIM)
        k, v = jnp.split(ctx @ Wkv, 2, axis=-1)
        k = k.reshape(b, ctx_n, N_HEADS, HEAD_DIM)
        v = v.reshape(b, ctx_n, N_HEADS, HEAD_DIM)
        q = apply_axial_rope(q, pos_map)
        k = apply_axial_rope(k, ctx_pos_map)
        scale = 1.0 / np.sqrt(HEAD_DIM).astype(np.float32)
        logits = jnp.einsum('bqhd,bkhd->bhqk', q, k) * scale
        w = jax.nn.softmax(logits, axis=-1)
        attn = jnp.einsum('bhqk,bkhd->bqhd', w, v)
        attn = attn.reshape(b, n, N_HEADS * HEAD_DIM)
        return attn @ Wout + bout

    def _L2_ffn_ref(x, w_gate, w_up, w_down):
        import jax, jax.numpy as jnp
        import numpy as np
        DIM_IN = 256
        DIM_HIDDEN = 1024
        gate = jnp.einsum('bsd,hd->bsh', x, w_gate)
        up = jnp.einsum('bsd,hd->bsh', x, w_up)
        gated = jax.nn.silu(gate) * up
        return jnp.einsum('bsh,dh->bsd', gated, w_down)

    def _L3_xattn_ref(x, ctx, pos_map, ctx_pos_map, Wq, Wkv, Wout, bout):
        import jax, jax.numpy as jnp
        import numpy as np
        DIM = 256
        CTX_DIM = 128
        N_HEADS = 32
        HEAD_DIM = DIM // N_HEADS
        POS_DIM = 2
        B, N, CTXN = (2, 256, 256)
        ROPE_BASE = 10000.0

        def apply_axial_rope(x, pos):
            b, n, h, d = x.shape
            p = pos.shape[-1]
            dpa = d // p
            half = dpa // 2
            freqs = ROPE_BASE ** (-jnp.arange(half, dtype=x.dtype) / half)
            ang = pos[..., :, None] * freqs
            cos = jnp.cos(ang)[:, :, None, :, :]
            sin = jnp.sin(ang)[:, :, None, :, :]
            xr = x.reshape(b, n, h, p, half, 2)
            x1, x2 = (xr[..., 0], xr[..., 1])
            out = jnp.stack([x1 * cos - x2 * sin, x1 * sin + x2 * cos], axis=-1)
            return out.reshape(b, n, h, d)
        b, n, _ = x.shape
        ctx_n = ctx.shape[1]
        q = (x @ Wq).reshape(b, n, N_HEADS, HEAD_DIM)
        k, v = jnp.split(ctx @ Wkv, 2, axis=-1)
        k = k.reshape(b, ctx_n, N_HEADS, HEAD_DIM)
        v = v.reshape(b, ctx_n, N_HEADS, HEAD_DIM)
        q = apply_axial_rope(q, pos_map)
        k = apply_axial_rope(k, ctx_pos_map)
        scale = 1.0 / np.sqrt(HEAD_DIM).astype(np.float32)
        logits = jnp.einsum('bqhd,bkhd->bhqk', q, k) * scale
        w = jax.nn.softmax(logits, axis=-1)
        attn = jnp.einsum('bhqk,bkhd->bqhd', w, v)
        attn = attn.reshape(b, n, N_HEADS * HEAD_DIM)
        return attn @ Wout + bout

    def _L3_ffn_ref(x, gate_w, W1, W2, W3, Ws1, Ws2, Ws3):
        import jax, jax.numpy as jnp
        import numpy as np
        N_GROUPS = 4
        TOPK_GROUPS = 2
        TOPK = 4
        ROUTE_SCALE = 1.0

        def _gate(xt, gate_w):
            T = xt.shape[0]
            E = gate_w.shape[0]
            scores = jax.nn.sigmoid(xt @ gate_w.T)
            original_scores = scores
            sg = scores.reshape(T, N_GROUPS, E // N_GROUPS)
            group_scores = sg.max(axis=-1)
            _, gidx = jax.lax.top_k(group_scores, TOPK_GROUPS)
            gmask = jax.nn.one_hot(gidx, N_GROUPS, dtype=scores.dtype).sum(axis=1)
            masked = (sg * gmask[:, :, None]).reshape(T, E)
            _, idx = jax.lax.top_k(masked, TOPK)
            w = jnp.take_along_axis(original_scores, idx, axis=-1)
            w = w / w.sum(axis=-1, keepdims=True) * ROUTE_SCALE
            return (w, idx)
        shape = x.shape
        D = shape[-1]
        xt = x.reshape(-1, D)
        E = W1.shape[0]
        weights, indices = _gate(xt, gate_w)
        combine = jnp.einsum('tk,tke->te', weights, jax.nn.one_hot(indices, E, dtype=weights.dtype))
        h1 = jnp.einsum('td,eid->tei', xt, W1)
        h3 = jnp.einsum('td,eid->tei', xt, W3)
        g = jax.nn.silu(h1) * h3 * combine[:, :, None]
        y = jnp.einsum('tei,edi->td', g, W2)
        z = jax.nn.silu(xt @ Ws1.T) * (xt @ Ws3.T) @ Ws2.T
        return (y + z).reshape(shape)
    x = x + _L0_xattn_ref(_layernorm(x, axis=-1), ctx_1024, fside_BxSx2_0, fside_BxSx2_0, L0_xattn_Wq, L0_xattn_Wkv, L0_xattn_Wout, L0_xattn_bout)
    x = x + _L0_ffn_ref(_layernorm(x, axis=-1), L0_ffn_w_router, L0_ffn_we1, L0_ffn_we3, L0_ffn_we2, L0_ffn_ws1, L0_ffn_ws3, L0_ffn_ws2)
    x = x + _L1_xattn_ref(_layernorm(x, axis=-1), ctx_1024, mask_BxS2_bf1, L1_xattn_Wq, L1_xattn_Wk, L1_xattn_Wv, L1_xattn_Wo)
    x = x + _L1_ffn_ref(_layernorm(x, axis=-1), L1_ffn_gate_w, L1_ffn_up_w, L1_ffn_down_w)
    x = x + _L2_xattn_ref(_layernorm(x, axis=-1), ctx_1024, fside_BxSx2_0, fside_BxSx2_0, L2_xattn_Wq, L2_xattn_Wkv, L2_xattn_Wout, L2_xattn_bout)
    x = x + _L2_ffn_ref(_layernorm(x, axis=-1), L2_ffn_w_gate, L2_ffn_w_up, L2_ffn_w_down)
    x = x + _L3_xattn_ref(_layernorm(x, axis=-1), ctx_1024, fside_BxSx2_0, fside_BxSx2_0, L3_xattn_Wq, L3_xattn_Wkv, L3_xattn_Wout, L3_xattn_bout)
    x = x + _L3_ffn_ref(_layernorm(x, axis=-1), L3_ffn_gate_w, L3_ffn_W1, L3_ffn_W2, L3_ffn_W3, L3_ffn_Ws1, L3_ffn_Ws2, L3_ffn_Ws3)
    return x

_drawn_inputs = setup_inputs


def setup_inputs(seed=0):
    import zlib

    import numpy as np

    out = dict(_drawn_inputs(seed))
    spreads = {'L0_xattn_bout': (0.0, 0.1), 'L2_xattn_bout': (0.0, 0.1), 'L3_xattn_bout': (0.0, 0.1)}
    factors = {'L1_xattn_Wq': 8.0,
     'L1_xattn_Wk': 8.0,
     'L1_ffn_gate_w': 2.79,
     'L3_ffn_gate_w': 8.0,
     'L3_ffn_W1': 8.0,
     'L3_ffn_W2': 8.0,
     'L3_ffn_W3': 8.0,
     'L3_ffn_Ws1': 5.669,
     'L3_ffn_Ws2': 5.628,
     'L3_ffn_Ws3': 5.77}
    for name, (base, spread) in spreads.items():
        noise = np.random.default_rng([zlib.crc32(name.encode()), seed]).standard_normal(out[name].shape)
        drawn = base * np.exp(spread * noise) if base else spread * noise
        out[name] = jnp.asarray(drawn.astype(out[name].dtype))
    for name, factor in factors.items():
        out[name] = (out[name] * factor).astype(out[name].dtype)
    return out
```

```python
from contextlib import ExitStack

import concourse.bass as bass
from concourse import mybir

F32 = mybir.dt.float32
F32R = mybir.dt.float32r
I32 = mybir.dt.int32
U8 = mybir.dt.uint8
ALU = mybir.AluOpType
ACT = mybir.ActivationFunctionType
AX_X = mybir.AxisListType.X

P = 128
B, S, D = 8, 128, 256
T = B * S
H = T // 2
KC = D // P
NT = H // P
HEADS, HD = 32, 8
GL = 4
E = 16
TOPK = 4
G2, D2 = 8, 128
LN_EPS = 1e-5
RW = 2304
FW = 3 * D
LW = 2 * D + 2 * P + 2 * D
MASKED = 1e30
TWO_PI_INV = 0.15915494309189535
PI_HI, PI_LO = 6.28125, 0.0019353071795864769
ROUND = 12582912.0
FP8_ROUND = 1.5 * 2.0 ** 20

FFN_CHUNKS = [20, 8, 8, 25]
FFN_ROUTED = [True, False, False, True]
FFN_MX = [False, True, False, False]
CHUNK_BASE = [0, 20, 28, 36]
ROUTED_BASE = {0: 0, 3: 20}
ROW_BLOCK = 16
ROWS_PER_EXPERT = {0: 8, 3: 11}


def build(nc, x_t, ctx_t, pos_rows, mask_row, mask_col, rope_w, rope_b, router_w, ffn_w0, ffn_w1,
          ffn_w2, ffn_w3, gqa_w, cols, ident_in, tri_in, out, n_phases=8):
    ffn_w = [ffn_w0, ffn_w1, ffn_w2, ffn_w3]
    PHASES = [("rope", 0), ("ffn", 0), ("gqa", 0), ("ffn", 1), ("rope", 1), ("ffn", 2), ("rope", 2),
              ("ffn", 3)][:n_phases]

    with ExitStack() as ctx:
        def sb(name, shape, dt=F32):
            return ctx.enter_context(nc.sbuf_tensor(name, shape, dt))

        def sem(name):
            return ctx.enter_context(nc.semaphore(name))

        PS = ctx.enter_context(nc.psum_tensor("PS", [P, 8, 512], F32))
        cw_rows = {f: nc.dram_tensor(f"cw_rows{f}", [FFN_CHUNKS[f] * 8, T], F32, kind="Internal").ap()
                   for f in (0, 3)}

        X = sb("X", [P, KC, T])
        h_hi_t = sb("h_hi_t", [P, KC, T], F32R)
        h_lo_t = sb("h_lo_t", [P, KC, T], F32R)
        h_tok = sb("h_tok", [P, 2 * NT, D])
        ctx_hi = sb("ctx_hi", [P, T], F32R)
        ctx_lo = sb("ctx_lo", [P, T], F32R)
        cos_t = sb("cos_t", [P, T])
        sin_t = sb("sin_t", [P, T])
        ident = sb("ident", [P, P])
        tri = sb("tri", [P, E, E])
        col = sb("col", [P, 8])
        bias_o = sb("bias_o", [P, 3, KC])
        wr_raw = sb("wr_raw", [P, 2, KC, E])
        wr_hi = sb("wr_hi", [P, 2, KC, E], F32R)
        wr_lo = sb("wr_lo", [P, 2, KC, E], F32R)
        st6 = sb("st6", [P, NT, 6])
        mv = sb("mv", [P, 2 * NT, 2])
        sd = sb("sd", [P, 2 * NT])
        rstd = sb("rstd", [P, 2 * NT])
        mcol8 = sb("mcol8", [P, B], U8)
        mcol = sb("mcol", [P, B])
        ctx_raw = h_tok[:, 0:4, :].rearrange("p a b -> p (a b)")
        shared_c = sb("shared_c", [32, 2, 64])

        RSZ = 2 * RW + 2 * 8 * T + 4 * T + 2 * 512 + 2 * 2048
        FSZ = 9600
        AR = sb("AR", [P, RSZ], F32R)
        AF = sb("AF", [P, FSZ])

        def carve(arena):
            at = [0]

            def take(n):
                a = arena[:, at[0]:at[0] + n]
                at[0] += n
                return a
            return take

        r = carve(AR)
        rw_hi_t, rw_lo_t = r(RW), r(RW)
        K_all = r(8 * T).rearrange("p (g t) -> p g t", g=8)
        Q_all = r(8 * T).rearrange("p (g t) -> p g t", g=8)
        a_or_r = r(4 * T)
        rot_hi = a_or_r[:, 0:2 * T].rearrange("p (s t) -> p s t", s=2)
        rot_lo = a_or_r[:, 2 * T:4 * T].rearrange("p (s t) -> p s t", s=2)
        a_hi_t, a_lo_t = rot_hi, rot_lo
        q_fix = r(2 * 512).rearrange("p (c g t) -> p c g t", c=2, g=GL)
        k_msk = r(2 * 2048).rearrange("p (c g j t) -> p c g j t", c=2, g=GL, j=4)
        f = carve(AF)
        scores = f(4096).rearrange("p (s h t) -> p s h t", s=4, h=8)
        rw_raw = AF[:, 0:RW]
        pT_or_t = f(2048)
        pT = pT_or_t.rearrange("p (v h t) -> p v h t", v=2, h=8)
        rot_a = pT_or_t[:, 0:1024].rearrange("p (s t) -> p s t", s=2)
        rot_b = pT_or_t[:, 1024:2048].rearrange("p (s t) -> p s t", s=2)
        v_aug = f(B * HEADS * 9).rearrange("p (b h d) -> p b h d", b=B, h=HEADS)
        a_tok = f(2 * P).rearrange("p (c d) -> p c d", c=2)
        row_max = f(4 * 8).rearrange("p (s h) -> p s h", s=4)
        o_rcp = f(2 * 16).rearrange("p (c h) -> p c h", c=2)
        r = carve(AR)
        w_hi_t = r(2 * FW).rearrange("p (s n) -> p s n", s=2)
        w_lo_t = r(2 * FW).rearrange("p (s n) -> p s n", s=2)
        g_hi_t = r(2 * H).rearrange("p (u t) -> p u t", u=2)
        g_lo_t = r(2 * H).rearrange("p (u t) -> p u t", u=2)
        f = carve(AF)
        w_raw = f(2 * FW).rearrange("p (s n) -> p s n", s=2)
        cw_t = f(2 * T).rearrange("p (s t) -> p s t", s=2)
        sil_t = f(2 * H).rearrange("p (u t) -> p u t", u=2)
        g_t = f(2 * H).rearrange("p (u t) -> p u t", u=2)
        tmp_ab = f(2048)
        tmp_a, tmp_b = tmp_ab[:, 0:1024], tmp_ab[:, 1024:2048]
        amax, scl, rscl = f(32), f(32), f(32)
        cw_T = f(T)
        r_lg = f(2 * NT * E).rearrange("p (n e) -> p n e", e=E)
        r_ex = f(2 * NT * E).rearrange("p (n e) -> p n e", e=E)
        r_sel = f(2 * NT * E).rearrange("p (n e) -> p n e", e=E)
        r_m = f(2 * NT * E).rearrange("p (n e) -> p n e", e=E)
        r_g = f(2 * NT * 4).rearrange("p (n e) -> p n e", e=4)
        r_gs = f(2 * NT * 4).rearrange("p (n e) -> p n e", e=4)
        r_s = f(2 * NT)
        r_r = f(2 * NT)
        cmp_a = cw_t.rearrange("p s t -> p (s t)")
        cmp_b = tmp_ab
        h_q_t = [cw_t[:, u, :].rearrange("p (k t) -> p k t", k=KC) for u in range(2)]
        r = carve(AR)
        l_hi_t = r(2 * LW).rearrange("p (s n) -> p s n", s=2)
        l_lo_t = r(2 * LW).rearrange("p (s n) -> p s n", s=2)
        lq_hi_t = r(2 * T).rearrange("p (h t) -> p h t", h=2)
        lq_lo_t = r(2 * T).rearrange("p (h t) -> p h t", h=2)
        lk_hi_t, lk_lo_t = r(T), r(T)
        lo_hi_t = r(2 * T).rearrange("p (h t) -> p h t", h=2)
        lo_lo_t = r(2 * T).rearrange("p (h t) -> p h t", h=2)
        f = carve(AF)
        l_raw = f(2 * LW).rearrange("p (s n) -> p s n", s=2)
        lv_t = f(T).rearrange("p (b d) -> p b d", b=B)
        ls_t = f(2 * T).rearrange("p (u b h k) -> p u b h k", u=2, b=4, h=2)
        lp_t = f(2 * T).rearrange("p (u b h k) -> p u b h k", u=2, b=4, h=2)
        l_mx = f(16).rearrange("p (u b) -> p u b", u=2)
        l_sm = f(16).rearrange("p (u b) -> p u b", u=2)
        l_rc = f(16).rearrange("p (u b) -> p u b", u=2)
        mask8 = f(T // 4).bitcast(U8)
        mbias = f(T).rearrange("p (b k) -> p b k", b=B)

        s_const, s_x, s_ctx = sem("s_const"), sem("s_x"), sem("s_ctx")
        s_pool0, s_act0, s_dve0 = sem("s_pool0"), sem("s_act0"), sem("s_dve0")
        s_sin, s_ang = sem("s_sin"), sem("s_ang")
        x_out = sem("x_out")
        ln_xT, ln_st, ln_mv, ln_sd, ln_rs, ln_h, ln_hT = (
            sem(n) for n in ("ln_xT", "ln_st", "ln_mv", "ln_sd", "ln_rs", "ln_h", "ln_hT"))
        h_f32, h_q, h_hi, h_lo = sem("h_f32"), sem("h_q"), sem("h_hi"), sem("h_lo")
        rw_in, rw_hi, rw_lo = sem("rw_in"), sem("rw_hi"), sem("rw_lo")
        v_mm, v_one, v_ev = sem("v_mm"), sem("v_one"), sem("v_ev")
        rp_mm, rp_mul, rp_add, rp_hi, rp_lo = (
            sem(n) for n in ("rp_mm", "rp_mul", "rp_add", "rp_hi", "rp_lo"))
        rp_dma = [sem("rp_dma0"), sem("rp_dma1")]
        km, qf, lg_mm, at_mx, at_sub, at_exp, at_T, at_ev, at_av = (
            sem(n) for n in ("km", "qf", "lg_mm", "at_mx", "at_sub", "at_exp", "at_T", "at_ev", "at_av"))
        o_rc, a_ok, at_z, a_hi, a_lo, op_mm = (
            sem(n) for n in ("o_rc", "a_ok", "at_z", "a_hi", "a_lo", "op_mm"))
        w13_in, w2_in = [sem("w13_in0"), sem("w13_in1")], [sem("w2_in0"), sem("w2_in1")]
        cw_in = [sem("cw_in0"), sem("cw_in1")]
        w_q, w13_hi, w13_lo, w2_hi, w2_lo = (sem(n) for n in ("w_q", "w13_hi", "w13_lo", "w2_hi", "w2_lo"))
        ab, sil, gm, g_cw, g_q, g_hi, g_lo, o_mm = (
            sem(n) for n in ("ab", "sil", "gm", "g_cw", "g_q", "g_hi", "g_lo", "o_mm"))
        r_mm, r_sub, r_act, cw_ok, cw_tr, cw_ev, cw_wr, cw_sh = (
            sem(n) for n in ("r_mm", "r_sub", "r_act", "cw_ok", "cw_tr", "cw_ev", "cw_wr", "cw_sh"))
        q_step = sem("q_step")
        lw_in = [sem("lw_in0"), sem("lw_in1")]
        lw_hi, lw_lo = sem("lw_hi"), sem("lw_lo")
        lq_mm, lq_hi, lq_lo, lk_mm, lk_hi, lk_lo, lv_mm, lv_ev = (
            sem(n) for n in ("lq_mm", "lq_hi", "lq_lo", "lk_mm", "lk_hi", "lk_lo", "lv_mm", "lv_ev"))
        l_lg, l_add, l_max, l_sub, l_exp, l_sum, l_rcp, l_nrm, l_T, l_pT, l_av, l_ohi, l_olo, l_out = (
            sem(n) for n in ("l_lg", "l_add", "l_max", "l_sub", "l_exp", "l_sum", "l_rcp", "l_nrm", "l_T",
                             "l_pT", "l_av", "l_ohi", "l_olo", "l_out"))
        l_mk = sem("l_mk")
        s_out = sem("s_out")

        block = ctx.enter_context(nc.Block())

        def f32(ap):
            return ap.bitcast(F32)

        def half(u):
            return slice(u * H, (u + 1) * H)

        def wait_x(eng, p, u):
            if p == 0:
                eng.wait_ge(s_x, 16)
            else:
                eng.wait_ge(x_out, 2 * (p - 1) + u + 1)

        def pairs(n):
            return n // 2 - (1 if n % 2 == 0 else 0), range(n - (2 - n % 2), n)

        def product(pe, dst, sides, start=True, stop=True):
            for i, (wh, wl, mh, ml) in enumerate(sides):
                pe.matmul(dst, wh, mh, start=start and i == 0, stop=False)
                pe.matmul(dst, wh, ml, start=False, stop=False)
                last = pe.matmul(dst, wl, mh, start=False, stop=stop and i == len(sides) - 1)
            return last

        @block.sync
        def _(sp):
            sp.dma_start(X[:], x_t.rearrange("(k p) t -> p k t", p=P)).then_inc(s_x, 16)
            sp.dma_start(col[:], cols).then_inc(s_const, 16)
            sp.dma_start(cos_t[:], pos_rows).then_inc(s_const, 16)
            sp.dma_start(ident[:], ident_in).then_inc(s_const, 16)
            sp.dma_start(ctx_raw, ctx_t).then_inc(s_ctx, 16)
            sp.dma_start(tri[:], tri_in.rearrange("p (i j) -> p i j", i=E)).then_inc(s_const, 16)
            sp.dma_start(bias_o[:], rope_b.rearrange("l p k -> p l k")).then_inc(s_const, 16)
            sp.dma_start(wr_raw[:], router_w.rearrange("l p k e -> p l k e")).then_inc(s_const, 16)
            sp.dma_start(mcol8[:], mask_col).then_inc(s_const, 16)
            sp.wait_ge(s_dve0, 2)
            for i, (fi, n) in enumerate(((0, 32), (3, 24))):
                sp.dma_start(cw_rows[fi][FFN_CHUNKS[fi] * 8 - n:, :].rearrange("n (a c) -> n a c", c=64),
                             shared_c[0:n, i:i + 1, :].to_broadcast([n, T // 64, 64])).then_inc(cw_sh, 16)

            def rope_moves(a, p):
                if p > 0:
                    sp.wait_ge(x_out, 2 * p)
                sp.dma_start(rw_raw, rope_w[a]).then_inc(rw_in, 16)
                for j in range(4):
                    dst, m = (K_all, Q_all)[j // 2], j % 2
                    sp.wait_ge(rp_lo, 8 * a + 2 * j + 2)
                    for s in range(3):
                        src = (rot_hi, rot_hi, rot_lo)[s] if j < 2 else (rot_hi, rot_lo, rot_hi)[s]
                        for g in range(GL):
                            sp.dma_start(f32(dst[32 * s:32 * s + 32, GL * m + g, :]),
                                         f32(src[32 * g:32 * g + 32, j % 2, :])).then_inc(rp_dma[j % 2], 16)

            def ffn_loads(fi, p):
                n, cb = FFN_CHUNKS[fi], CHUNK_BASE[fi]
                routed, rb = FFN_ROUTED[fi], ROUTED_BASE.get(fi)
                sp.wait_ge(x_out, 2 * p)

                def w_load(c, s, first):
                    src = ffn_w[fi][c] if isinstance(c, int) else \
                        ffn_w[fi][bass.ds(c, 1)].rearrange("a p n -> (a p) n")
                    if not first:
                        sp.wait_ge(w13_lo, cb + c - 1)
                    sp.dma_start(w_raw[:, s, 0:2 * D], src[:, 0:2 * D]).then_inc(w13_in[s], 16)
                    if not first:
                        sp.wait_ge(w2_lo, cb + c - 1)
                    sp.dma_start(w_raw[:, s, 2 * D:FW], src[:, 2 * D:FW]).then_inc(w2_in[s], 16)

                def cw_load(c, s, src, first):
                    if not first:
                        sp.wait_ge(g_cw, 2 * (rb + c) - 2)
                    sp.dma_start(cw_t[:, s, :], src).then_inc(cw_in[s], 16)

                def cw_src(c):
                    v = cw_rows[fi].rearrange("(c r) t -> c r t", r=8)
                    v = v[c] if isinstance(c, int) else v[bass.ds(c, 1)].rearrange("a r t -> (a r) t")
                    return v.unsqueeze(1).to_broadcast([8, ROW_BLOCK, T])

                for c in range(2):
                    w_load(c, c, True)
                if routed:
                    e_rows = ROWS_PER_EXPERT[fi]
                    sp.wait_ge(cw_ev, 1 if fi == 0 else 2)
                    sp.dma_start(cw_rows[fi][0:E * e_rows, :].rearrange("(e r) t -> e r t", r=e_rows),
                                 cw_T[0:E, :].unsqueeze(1).to_broadcast([E, e_rows, T])).then_inc(cw_wr, 16)
                    sp.wait_ge(cw_wr, 16 if fi == 0 else 32)
                    sp.wait_ge(cw_sh, 32)
                    for c in range(2):
                        cw_load(c, c, cw_src(c), True)
                loop_end, tail = pairs(n)
                with sp.Fori(1, loop_end) as i:
                    for s in range(2):
                        w_load(2 * i + s, s, False)
                        if routed:
                            cw_load(2 * i + s, s, cw_src(2 * i + s), False)
                for c in tail:
                    w_load(c, c % 2, False)
                    if routed:
                        cw_load(c, c % 2, cw_src(c), False)

            def gqa_loads(p):
                sp.wait_ge(x_out, 2 * p)
                sp.dma_start(mask8, mask_row.to_broadcast([P, T])).then_inc(l_mk, 16)
                for g in range(2):
                    sp.dma_start(l_raw[:, g, :], gqa_w[g]).then_inc(lw_in[g], 16)
                with sp.Fori(1, 4) as i:
                    for s in range(2):
                        sp.wait_ge(lw_lo, 2 * i + s - 1)
                        sp.dma_start(l_raw[:, s, :], gqa_w[bass.ds(2 * i + s, 1)]
                                     .rearrange("a p n -> (a p) n")).then_inc(lw_in[s], 16)

            for p, (kind, i) in enumerate(PHASES):
                if kind == "rope":
                    rope_moves(i, p)
                elif kind == "ffn":
                    ffn_loads(i, p)
                else:
                    gqa_loads(p)
            for u in range(2):
                sp.wait_ge(x_out, 2 * (len(PHASES) - 1) + u + 1)
                sp.dma_start(out.rearrange("(k p) t -> p k t", p=P)[:, :, half(u)],
                             X[:, :, half(u)]).then_inc(s_out, 16)
            sp.wait_ge(s_out, 32)
            sp.wait_ge(cw_sh, 32)

        @block.gpsimd
        def _(pool):
            def rope(a):
                for j in range(2):
                    pool.wait_ge(rp_dma[j], 384 * (a + 1))

                def unit(b, c, free):
                    if not free:
                        pool.wait_ge(lg_mm, 2 * (16 * a + 2 * b + c - 1))
                    src = K_all[0:96, GL * c:GL * c + GL, bass.ds(b * S, S)]
                    pool.tensor_tensor(k_msk[0:96, c], f32(src).unsqueeze(2).to_broadcast([96, GL, 4, S]),
                                       col[0:96, 2:6].unsqueeze(1).unsqueeze(3).to_broadcast([96, GL, 4, S]),
                                       ALU.mult).then_inc(km, 1)

                for c in range(2):
                    unit(0, c, True)
                with pool.Fori(1, B) as b:
                    for c in range(2):
                        unit(b, c, False)

            def ffn(fi):
                n, cb = FFN_CHUNKS[fi], CHUNK_BASE[fi]
                routed, rb = FFN_ROUTED[fi], ROUTED_BASE.get(fi)

                def split(c, s, part, hi, lo):
                    pool.wait_ge(hi, cb + c + 1)
                    pool.tensor_tensor(w_lo_t[:, s, part], w_raw[:, s, part], f32(w_hi_t[:, s, part]),
                                       ALU.subtract).then_inc(lo, 1)

                def route(c, s, i, u):
                    if u == 0:
                        pool.wait_ge(cw_in[s], 16 * (rb // 2 + i + 1))
                    pool.wait_ge(gm, 2 * (cb + c) + u + 1)
                    pool.tensor_tensor(g_t[:, u, :], g_t[:, u, :], cw_t[:, s, half(u)],
                                       ALU.mult).then_inc(g_cw, 1)

                def chunk(c, s, i, last):
                    if routed:
                        route(c, s, i, 0)
                    if not last:
                        split(c + 1, 1 - s, slice(0, 2 * D), w13_hi, w13_lo)
                    if routed:
                        route(c, s, i, 1)
                    split(c, s, slice(2 * D, FW), w2_hi, w2_lo)

                split(0, 0, slice(0, 2 * D), w13_hi, w13_lo)
                chunk(0, 0, 0, False)
                chunk(1, 1, 0, False)
                loop_end, tail = pairs(n)
                with pool.Fori(1, loop_end) as i:
                    chunk(2 * i, 0, i, False)
                    chunk(2 * i + 1, 1, i, False)
                for c in tail:
                    chunk(c, c % 2, c // 2, c == n - 1)

            def gqa():
                def split(g, s):
                    pool.wait_ge(lw_hi, g + 1)
                    pool.tensor_tensor(l_lo_t[:, s, :], l_raw[:, s, :], f32(l_hi_t[:, s, :]),
                                       ALU.subtract).then_inc(lw_lo, 1)

                def norm(g):
                    for u in range(2):
                        pool.wait_ge(l_rcp, 2 * g + u + 1)
                        v = ls_t[:, u].rearrange("p b h k -> p (b h) k")
                        pool.tensor_tensor(v, v, l_rc[:, u, :].unsqueeze(2).to_broadcast([P, 8, S]),
                                           ALU.mult).then_inc(l_nrm, 1)

                split(0, 0)
                split(1, 1)
                norm(0)
                norm(1)
                with pool.Fori(1, 4) as i:
                    for s in range(2):
                        split(2 * i + s, s)
                        norm(2 * i + s)

            for p, (kind, i) in enumerate(PHASES):
                if kind == "rope":
                    rope(i)
                elif kind == "ffn":
                    ffn(i)
                else:
                    gqa()

        @block.scalar
        def _(act):
            act.wait_ge(s_ctx, 16)
            act.activation(ctx_hi[:], ctx_raw, ACT.Copy).then_inc(s_act0, 1)
            act.wait_ge(s_const, 7 * 16)
            act.activation(wr_hi[:], wr_raw[:], ACT.Copy).then_inc(s_act0, 1)
            act.wait_ge(s_ang, 13)
            act.activation(cos_t[:], cos_t[:], ACT.Sin).then_inc(s_sin, 1)
            act.activation(sin_t[:], sin_t[:], ACT.Sin).then_inc(s_sin, 1)

            def layernorm(p, mx):
                for u in range(2):
                    n = 2 * p + u
                    act.wait_ge(ln_mv, n + 1)
                    act.activation(sd[:, NT * u:NT * u + NT], mv[:, NT * u:NT * u + NT, 1], ACT.Sqrt,
                                   bias=col[:, 6:7]).then_inc(ln_sd, 1)
                for u in range(2):
                    n = 2 * p + u
                    act.wait_ge(ln_hT, n + 1)
                    src = PS[:, 4 + 2 * u:6 + 2 * u, :]
                    if mx:
                        dst = h_q_t[u]
                        act.activation(dst, src, ACT.Copy).then_inc(h_f32, 1)
                        act.wait_ge(h_q, u + 1)
                        src = dst
                    act.activation(h_hi_t[:, :, half(u)], src, ACT.Copy).then_inc(h_hi, 1)

            def rope(a, p):
                act.wait_ge(rw_in, 16 * (a + 1))
                act.activation(rw_hi_t, rw_raw, ACT.Copy).then_inc(rw_hi, 1)
                layernorm(p, False)
                act.wait_ge(v_mm, a + 1)
                for b in range(0, B, 2):
                    ev = act.activation(v_aug[:, b:b + 2, :, 0:8],
                                        PS[:, b // 2, :].rearrange("p (b h d) -> p b h d", b=2, h=HEADS),
                                        ACT.Copy)
                ev.then_inc(v_ev, 1)
                for i in range(8):
                    j, u, gi = i // 2, i % 2, 8 * a + i
                    act.wait_ge(rp_add, gi + 1)
                    if j >= 2 and u == 0:
                        act.wait_ge(rp_dma[j % 2], 384 * a + 192)
                    act.activation(rot_hi[:, j % 2, half(u)], rot_a[:, i % 2, :], ACT.Copy).then_inc(rp_hi, 1)

                def q_copy(b, c):
                    act.activation(q_fix[0:96, c], f32(Q_all[0:96, GL * c:GL * c + GL, bass.ds(b * S, S)]),
                                   ACT.Copy).then_inc(qf, 1)

                def attn_hi(b, c):
                    act.wait_ge(at_z, 16 * a + 2 * b + c + 1)
                    act.activation(a_hi_t[:, c, bass.ds(b * S, S)], PS[:, 3, c * P:c * P + P],
                                   ACT.Copy).then_inc(a_hi, 1)

                def probs(b, c, v):
                    act.wait_ge(at_sub, 32 * a + 4 * b + 2 * c + v + 1)
                    s = scores[:, 2 * c + v]
                    act.activation(s, s, ACT.Exp, scale=HD ** -0.5).then_inc(at_exp, 1)

                def evacuate(b, c, v, free):
                    w = 32 * a + 4 * b + 2 * c + v
                    act.wait_ge(at_T, w + 1)
                    if not free:
                        act.wait_ge(at_av, w - 1)
                    act.activation(pT[:, v].rearrange("p h t -> p (h t)"),
                                   PS[:, 0:2, :].rearrange("p a b -> p (a b)"), ACT.Copy).then_inc(at_ev, 1)

                def batch(b, first, last):
                    for c in range(2):
                        for v in range(2):
                            if v == 1 and not first:
                                attn_hi(b - 1, c)
                            probs(b, c, v)
                            if c == 1:
                                evacuate(b, 0, v, first)
                            elif not first:
                                evacuate(b - 1, 1, v, False)
                            if v == 1 and not last:
                                act.wait_ge(lg_mm, 2 * (16 * a + 2 * b + c + 1))
                                q_copy(b + 1, c)

                for j in range(2):
                    act.wait_ge(rp_dma[j], 384 * (a + 1))
                q_copy(0, 0)
                q_copy(0, 1)
                batch(0, True, False)
                with act.Fori(1, B - 1) as b:
                    batch(b, False, False)
                batch(B - 1, False, True)
                evacuate(B - 1, 1, 0, False)
                attn_hi(B - 1, 0)
                evacuate(B - 1, 1, 1, False)
                attn_hi(B - 1, 1)

            def ffn(fi, p):
                n, cb = FFN_CHUNKS[fi], CHUNK_BASE[fi]
                routed, mx = FFN_ROUTED[fi], FFN_MX[fi]

                def w13_split(c, s, i, free):
                    act.wait_ge(w13_in[s], 16 * (cb // 2 + i + 1))
                    if mx:
                        act.wait_ge(w_q, c + 1)
                    if not free:
                        act.wait_ge(ab, 2 * (cb + c) - 2)
                    act.activation(w_hi_t[:, s, 0:2 * D], w_raw[:, s, 0:2 * D], ACT.Copy).then_inc(w13_hi, 1)

                def w2_split(c, s, i, free):
                    act.wait_ge(w2_in[s], 16 * (cb // 2 + i + 1))
                    if not free:
                        act.wait_ge(o_mm, 2 * (cb + c) - 2)
                    act.activation(w_hi_t[:, s, 2 * D:FW], w_raw[:, s, 2 * D:FW], ACT.Copy).then_inc(w2_hi, 1)

                def silu(c, u):
                    act.wait_ge(ab, 2 * (cb + c) + u + 1)
                    act.activation(sil_t[:, u, :], PS[:, 4 + 2 * u, :], ACT.Silu).then_inc(sil, 1)

                def g_split(c, u, free):
                    m = 2 * (cb + c) + u
                    if mx:
                        act.wait_ge(g_q, 2 * c + u + 1)
                    elif routed:
                        act.wait_ge(g_cw, m + 1 - 2 * cb + 2 * ROUTED_BASE[fi])
                    else:
                        act.wait_ge(gm, m + 1)
                    if not free:
                        act.wait_ge(o_mm, m - 1)
                    act.activation(g_hi_t[:, u, :], g_t[:, u, :], ACT.Copy).then_inc(g_hi, 1)

                act.wait_ge(x_out, 2 * p)
                w13_split(0, 0, 0, True)
                layernorm(p, mx)
                if routed:
                    if fi == 0:
                        act.wait_ge(r_sub, 1)
                        act.activation(r_ex, r_lg, ACT.Exp).then_inc(r_act, 1)
                    else:
                        act.wait_ge(r_mm, 2)
                        act.activation(r_ex, PS[:, 0, 0:2 * NT * E].rearrange("p (n e) -> p n e", e=E),
                                       ACT.Sigmoid).then_inc(r_act, 1)
                w13_split(1, 1, 0, True)
                silu(0, 0)
                w2_split(0, 0, 0, True)
                silu(0, 1)
                if routed:
                    act.wait_ge(cw_tr, 1 if fi == 0 else 2)
                    act.activation(cw_T[0:E, :], PS[0:E, 2:4, :].rearrange("p a b -> p (a b)"),
                                   ACT.Copy).then_inc(cw_ev, 1)
                g_split(0, 0, True)

                def chunk(c, s, i, first, last):
                    if not last:
                        w13_split(c + 1, 1 - s, i + s, False)
                    silu(c, 0)
                    g_split(c - 1, 1, first)
                    w2_split(c, s, i, first)
                    silu(c, 1)
                    g_split(c, 0, False)

                chunk(1, 1, 0, True, False)
                loop_end, tail = pairs(n)
                with act.Fori(1, loop_end) as i:
                    chunk(2 * i, 0, i, False, False)
                    chunk(2 * i + 1, 1, i, False, False)
                for c in tail:
                    chunk(c, c % 2, c // 2, False, c == n - 1)
                g_split(n - 1, 1, False)

            def gqa(p):
                act.wait_ge(x_out, 2 * p)

                def w_split(g, s, i, free):
                    act.wait_ge(lw_in[s], 16 * (i + 1))
                    if not free:
                        act.wait_ge(l_out, 2 * g - 2)
                    act.activation(l_hi_t[:, s, :], l_raw[:, s, :], ACT.Copy).then_inc(lw_hi, 1)

                def head(g):
                    for h in range(2):
                        for u in range(2):
                            act.wait_ge(lq_mm, 4 * g + 2 * h + u + 1)
                            act.activation(lq_hi_t[:, h, half(u)], PS[:, 4 + 2 * h + u, :],
                                           ACT.Copy).then_inc(lq_hi, 1)
                    for u in range(2):
                        act.wait_ge(lk_mm, 2 * g + u + 1)
                        act.activation(lk_hi_t[:, half(u)], PS[:, 4 + u, :], ACT.Copy).then_inc(lk_hi, 1)
                    for u in range(2):
                        act.wait_ge(l_sub, 2 * g + u + 1)
                        s = ls_t[:, u].rearrange("p b h k -> p (b h k)")
                        act.activation(s, s, ACT.Exp, scale=D2 ** -0.5).then_inc(l_exp, 1)
                    for u in range(2):
                        act.wait_ge(l_T, 2 * g + u + 1)
                        act.activation(lp_t[:, u].rearrange("p b h k -> p (b h k)"),
                                       PS[:, 4 + 2 * u:6 + 2 * u, :].rearrange("p a b -> p (a b)"),
                                       ACT.Copy).then_inc(l_pT, 1)
                    for u in range(2):
                        act.wait_ge(l_av, 2 * g + u + 1)
                        act.activation(
                            lo_hi_t[:, :, half(u)].rearrange("p h (b t) -> p b h t", b=4),
                            PS[:, 4 + 2 * u:6 + 2 * u, :].rearrange("p a (b h t) -> p (a b) h t", b=2, h=2),
                            ACT.Copy).then_inc(l_ohi, 1)

                w_split(0, 0, 0, True)
                layernorm(p, False)
                w_split(1, 1, 0, True)
                head(0)
                head(1)
                with act.Fori(1, 4) as i:
                    for s in range(2):
                        w_split(2 * i + s, s, i, False)
                        head(2 * i + s)

            for p, (kind, i) in enumerate(PHASES):
                if kind == "rope":
                    rope(i, p)
                elif kind == "ffn":
                    ffn(i, p)
                else:
                    gqa(p)

        @block.tensor
        def _(pe):
            pe.wait_ge(s_const, 7 * 16)
            pe.wait_ge(s_act0, 2)
            pe.wait_ge(s_dve0, 4)

            def ln_forward(p):
                for u in range(2):
                    wait_x(pe, p, u)
                    for t in range(NT):
                        for k in range(KC):
                            tr = pe.transpose(PS[:, 4 + 2 * u + t // 2, (t % 2) * D + k * P:(t % 2) * D + k * P + P],
                                              X[:, k, u * H + t * P:u * H + t * P + P], ident[:])
                    tr.then_inc(ln_xT, 1)

            def ln_back(p):
                for u in range(2):
                    pe.wait_ge(ln_h, 2 * p + u + 1)
                    for t in range(NT):
                        for k in range(KC):
                            tr = pe.transpose(PS[:, 4 + 2 * u + k, t * P:t * P + P],
                                              h_tok[:, NT * u + t, k * P:k * P + P], ident[:])
                    tr.then_inc(ln_hT, 1)

            def rope(a, p):
                ln_forward(p)
                pe.wait_ge(rw_hi, a + 1)
                pe.wait_ge(rw_lo, a + 1)

                def w(off, n):
                    return rw_hi_t[:, off:off + n], rw_lo_t[:, off:off + n]

                wv = w(1536, D)
                for b in range(B):
                    c = slice(b * S, b * S + S)
                    mm = product(pe, PS[:, b // 2, (b % 2) * D:(b % 2) * D + D],
                                 [(ctx_hi[:, c], ctx_lo[:, c], *wv)])
                mm.then_inc(v_mm, 1)
                ln_back(p)
                pe.wait_ge(v_ev, a + 1)
                for i in range(8):
                    j, u, gi = i // 2, i % 2, 8 * a + i
                    m, bank = j % 2, 2 * (i % 2)
                    if i >= 2:
                        pe.wait_ge(rp_mul, gi - 1)
                    if i >= 4:
                        pe.wait_ge(h_lo, 2 * p + u + 1)
                    for swapped in range(2):
                        if j < 2:
                            wk = w(1024 + swapped * D + m * P, P)
                            sides = [(*wk, ctx_hi[:, half(u)], ctx_lo[:, half(u)])]
                        else:
                            sides = [(*w(swapped * 2 * D + k * D + m * P, P), h_hi_t[:, k, half(u)],
                                      h_lo_t[:, k, half(u)]) for k in range(KC)]
                        mm = product(pe, PS[:, bank + swapped, :], sides)
                    mm.then_inc(rp_mm, 1)

                def score(b, c, v, free):
                    w_ = 32 * a + 4 * b + 2 * c + v
                    if v == 0:
                        pe.wait_ge(km, 16 * a + 2 * b + c + 1)
                        pe.wait_ge(qf, 16 * a + 2 * b + c + 1)
                    if not free:
                        pe.wait_ge(at_sub, w_ - 1)
                    for g in range(2):
                        mm = pe.matmul(PS[:, 4 + 2 * v + g, :], q_fix[0:96, c, 2 * v + g, :],
                                       k_msk[0:96, c, 2 * v + g].rearrange("p j t -> p (j t)"),
                                       start=True, stop=True)
                    mm.then_inc(lg_mm, 1)

                def turn(b, c, v, free):
                    w_ = 32 * a + 4 * b + 2 * c + v
                    pe.wait_ge(at_exp, w_ + 1)
                    if not free:
                        pe.wait_ge(at_ev, w_)
                    for h in range(8):
                        tr = pe.transpose(PS[:, h // 4, (h % 4) * P:(h % 4) * P + P],
                                          scores[:, 2 * c + v, h, :], ident[:])
                    tr.then_inc(at_T, 1)

                def weigh(b, c, v):
                    w_ = 32 * a + 4 * b + 2 * c + v
                    pe.wait_ge(at_ev, w_ + 1)
                    for h in range(8):
                        o = c * 256 + (8 * v + h) * 9
                        mm = pe.matmul(PS[:, 2, o:o + 9], pT[:, v, h, :],
                                       v_aug[:, bass.ds(b, 1), 16 * c + 8 * v + h, :] if not isinstance(b, int)
                                       else v_aug[:, b, 16 * c + 8 * v + h, :], start=True, stop=True)
                    mm.then_inc(at_av, 1)

                def out_turn(b, c):
                    pe.wait_ge(a_ok, 16 * a + 2 * b + c + 1)
                    pe.transpose(PS[:, 3, c * P:c * P + P], a_tok[:, c, :], ident[:]).then_inc(at_z, 1)

                def batch(b, first):
                    for c in range(2):
                        for v in range(2):
                            score(b, c, v, first and c == 0)
                            if v == 1 and not first:
                                out_turn(b - 1, c)
                            if c == 1:
                                turn(b, 0, v, first and v == 0)
                            elif not first:
                                turn(b - 1, 1, v, False)
                            if (c, v) == (1, 1):
                                weigh(b, 0, 0)
                            elif not first:
                                weigh(b - 1, *((0, 1), (1, 0), (1, 1))[2 * c + v])

                pe.wait_ge(rp_lo, 8 * (a + 1))
                batch(0, True)
                with pe.Fori(1, B) as b:
                    batch(b, False)
                turn(B - 1, 1, 0, False)
                weigh(B - 1, 0, 1)
                out_turn(B - 1, 0)
                turn(B - 1, 1, 1, False)
                weigh(B - 1, 1, 0)
                weigh(B - 1, 1, 1)
                out_turn(B - 1, 1)
                pe.wait_ge(a_hi, 16 * (a + 1))
                pe.wait_ge(a_lo, 16 * (a + 1))
                for u in range(2):
                    for m in range(KC):
                        mm = product(pe, PS[:, 2 * m + u, :],
                                     [(*w(1792 + k * D + m * P, P), a_hi_t[:, k, half(u)], a_lo_t[:, k, half(u)])
                                      for k in range(KC)])
                    mm.then_inc(op_mm, 1)

            def ffn(fi, p):
                n, cb = FFN_CHUNKS[fi], CHUNK_BASE[fi]
                ln_forward(p)
                ln_back(p)
                if FFN_ROUTED[fi]:
                    ri = 0 if fi == 0 else 1
                    for u in range(2):
                        pe.wait_ge(h_lo, 2 * p + u + 1)
                        for t in range(NT):
                            c = slice(u * H + t * P, u * H + t * P + P)
                            j = NT * u + t
                            mm = product(pe, PS[:, 0, j * E:(j + 1) * E],
                                         [(h_hi_t[:, k, c], h_lo_t[:, k, c], wr_hi[:, ri, k, :], wr_lo[:, ri, k, :])
                                          for k in range(KC)])
                    mm.then_inc(r_mm, 1)

                def ab_mm(c, s, u, free):
                    if u == 0:
                        pe.wait_ge(w13_lo, cb + c + 1)
                    if free:
                        pe.wait_ge(h_lo, 2 * p + u + 1)
                    else:
                        pe.wait_ge(gm, 2 * (cb + c) + u - 1)
                    for x in range(2):
                        mm = product(pe, PS[:, 4 + 2 * u + x, :],
                                     [(w_hi_t[:, s, o:o + P], w_lo_t[:, s, o:o + P], h_hi_t[:, k, half(u)],
                                       h_lo_t[:, k, half(u)]) for k in range(KC) for o in [x * D + k * P]])
                    mm.then_inc(ab, 1)

                def down(c, s, u, first, last):
                    if u == 0:
                        pe.wait_ge(w2_lo, cb + c + 1)
                    pe.wait_ge(g_lo, 2 * (cb + c) + u + 1)
                    for m in range(KC):
                        o = 2 * D + m * P
                        mm = product(pe, PS[:, 2 * m + u, :],
                                     [(w_hi_t[:, s, o:o + P], w_lo_t[:, s, o:o + P], g_hi_t[:, u, :], g_lo_t[:, u, :])],
                                     start=first, stop=last)
                    mm.then_inc(o_mm, 1)

                ab_mm(0, 0, 0, True)
                ab_mm(0, 0, 1, True)
                if FFN_ROUTED[fi]:
                    pe.wait_ge(cw_ok, 1 if fi == 0 else 2)
                    for j in range(2 * NT):
                        tr = pe.transpose(PS[0:E, 2 + j // 4, (j % 4) * P:(j % 4) * P + P], r_m[:, j, :], ident[:])
                    tr.then_inc(cw_tr, 1)
                    pe.wait_ge(cw_ev, 1 if fi == 0 else 2)
                def chunk(c, s, first):
                    for u in range(2):
                        ab_mm(c, s, u, False)
                        down(c - 1, 1 - s, u, first, False)

                chunk(1, 1, True)
                loop_end, tail = pairs(n)
                with pe.Fori(1, loop_end) as i:
                    chunk(2 * i, 0, False)
                    chunk(2 * i + 1, 1, False)
                for c in tail:
                    chunk(c, c % 2, False)
                for u in range(2):
                    down(n - 1, (n - 1) % 2, u, False, True)

            def gqa(p):
                ln_forward(p)
                ln_back(p)

                def head(g, s, first, last):
                    def w(off, n):
                        return l_hi_t[:, s, off:off + n], l_lo_t[:, s, off:off + n]

                    pe.wait_ge(lw_lo, g + 1)
                    if not first:
                        pe.wait_ge(l_olo, 2 * g)
                    for h in range(2):
                        for u in range(2):
                            if first:
                                pe.wait_ge(h_lo, 2 * p + 2)
                            product(pe, PS[:, 4 + 2 * h + u, :],
                                    [(*w(k * D + h * P, P), h_hi_t[:, k, half(u)], h_lo_t[:, k, half(u)])
                                     for k in range(KC)]).then_inc(lq_mm, 1)
                    for u in range(2):
                        pe.wait_ge(lq_lo, 4 * g + u + 1)
                        product(pe, PS[:, 4 + u, :],
                                [(*w(2 * D, P), ctx_hi[:, half(u)], ctx_lo[:, half(u)])]).then_inc(lk_mm, 1)
                    pe.wait_ge(lq_lo, 4 * g + 4)
                    for b in range(B):
                        c = slice(b * S, b * S + S)
                        mm = product(pe, PS[:, 6 + b // 4, (b % 4) * P:(b % 4) * P + P],
                                     [(ctx_hi[:, c], ctx_lo[:, c], *w(2 * D + P, P))])
                    mm.then_inc(lv_mm, 1)
                    pe.wait_ge(lk_lo, 2 * g + 2)
                    for u in range(2):
                        if u == 1:
                            pe.wait_ge(lv_ev, g + 1)
                        for b in range(4):
                            c = slice((4 * u + b) * S, (4 * u + b) * S + S)
                            for h in range(2):
                                o = (b % 2) * 256 + h * P
                                mm = product(pe, PS[:, 4 + 2 * u + b // 2, o:o + P],
                                             [(lq_hi_t[:, h, c], lq_lo_t[:, h, c], lk_hi_t[:, c], lk_lo_t[:, c])])
                        mm.then_inc(l_lg, 1)
                    for u in range(2):
                        pe.wait_ge(l_nrm, 2 * g + u + 1)
                        for b in range(4):
                            for h in range(2):
                                o = (b % 2) * 256 + h * P
                                tr = pe.transpose(PS[:, 4 + 2 * u + b // 2, o:o + P], ls_t[:, u, b, h, :], ident[:])
                        tr.then_inc(l_T, 1)
                    for u in range(2):
                        pe.wait_ge(l_pT, 2 * g + u + 1)
                        for b in range(4):
                            o = (b % 2) * 256
                            mm = pe.matmul(PS[:, 4 + 2 * u + b // 2, o:o + 256], lv_t[:, 4 * u + b, :],
                                           lp_t[:, u, b].rearrange("p h k -> p (h k)"), start=True, stop=True)
                        mm.then_inc(l_av, 1)
                    for u in range(2):
                        pe.wait_ge(l_olo, 2 * g + u + 1)
                        for m in range(KC):
                            mm = product(pe, PS[:, 2 * m + u, :],
                                         [(*w(2 * D + 2 * P + h * D + m * P, P), lo_hi_t[:, h, half(u)],
                                           lo_lo_t[:, h, half(u)]) for h in range(2)],
                                         start=first, stop=last)
                        mm.then_inc(l_out, 1)

                head(0, 0, True, False)
                head(1, 1, False, False)
                with pe.Fori(1, G2 // 2 - 1) as i:
                    head(2 * i, 0, False, False)
                    head(2 * i + 1, 1, False, False)
                head(G2 - 2, 0, False, False)
                head(G2 - 1, 1, False, True)

            for p, (kind, i) in enumerate(PHASES):
                if kind == "rope":
                    rope(i, p)
                elif kind == "ffn":
                    ffn(i, p)
                else:
                    gqa(p)

        @block.vector
        def _(dve):
            link_n = [0]

            def link(ins):
                link_n[0] += 1
                ins.then_inc(q_step, 1)
                dve.wait_ge(q_step, link_n[0])

            dve.memset(shared_c[:, 0, :], 1.0 / (TOPK + 1)).then_inc(s_dve0, 1)
            dve.memset(shared_c[:, 1, :], 1.0).then_inc(s_dve0, 1)
            dve.wait_ge(s_act0, 1)
            dve.tensor_tensor(ctx_lo[:], ctx_raw, f32(ctx_hi[:]),
                              ALU.subtract).then_inc(s_dve0, 1)
            dve.wait_ge(s_act0, 2)
            dve.tensor_tensor(wr_lo[:], wr_raw[:], f32(wr_hi[:]), ALU.subtract).then_inc(s_dve0, 1)
            dve.wait_ge(s_const, 7 * 16)
            link(dve.tensor_copy(mcol[:], mcol8[:]))
            ang_n = [0]

            def turn_step(ins):
                ang_n[0] += 1
                ins.then_inc(s_ang, 1)
                dve.wait_ge(s_ang, ang_n[0])

            ang, turns = h_tok[:, 4:8, :].rearrange("p a b -> p (a b)"), AF[:, 4096:4096 + T]
            turn_step(dve.tensor_scalar(ang, cos_t[:], col[:, 0:1], None, ALU.mult))
            for dst, shift in ((sin_t, 0.0), (cos_t, 1.5707963267948966)):
                turn_step(dve.tensor_scalar(dst[:], ang, shift, None, ALU.add))
                turn_step(dve.tensor_scalar(turns, dst[:], TWO_PI_INV, ROUND, ALU.mult, ALU.add))
                turn_step(dve.tensor_scalar(turns, turns, ROUND, None, ALU.subtract))
                turn_step(dve.scalar_tensor_tensor(dst[:], turns, -PI_HI, dst[:], ALU.mult, ALU.add))
                turn_step(dve.scalar_tensor_tensor(dst[:], turns, -PI_LO, dst[:], ALU.mult, ALU.add))
                turn_step(dve.tensor_scalar(dst[:], dst[:], 3.1415925, -3.1415925, ALU.min, ALU.max))
            dve.wait_ge(s_sin, 2)
            link(dve.tensor_scalar(sin_t[:], sin_t[:], col[:, 1:2], None, ALU.mult))

            quantised = []

            def quantise(v, n, done):
                ta, tb = tmp_a[:, 0:n], tmp_b[:, 0:n]
                nb = n // 32
                am, sc, rc = amax[:, 0:nb], scl[:, 0:nb], rscl[:, 0:nb]
                blocks = ta.rearrange("p (n c) -> p n c", c=32)
                if quantised:
                    dve.wait_ge(*quantised[-1])
                link(dve.transpose(ta, v))
                link(dve.tensor_reduce(am, blocks, AX_X, ALU.max, apply_absolute_value=True))
                link(dve.tensor_scalar(sc, am, 1.0 / 448.0, 1e-30, ALU.mult, ALU.max))
                link(dve.reciprocal(rc, sc))
                link(dve.tensor_tensor(blocks, blocks, rc.unsqueeze(2).to_broadcast([P, nb, 32]), ALU.mult))
                link(dve.tensor_scalar(tb.bitcast(I32), ta.bitcast(I32), 0x7F800000, None, ALU.bitwise_and))
                link(dve.tensor_scalar(tb, tb, 2.0 ** -6, FP8_ROUND, ALU.max, ALU.mult))
                link(dve.tensor_tensor(ta, ta, tb, ALU.add))
                link(dve.tensor_tensor(ta, ta, tb, ALU.subtract))
                link(dve.tensor_tensor(blocks, blocks, sc.unsqueeze(2).to_broadcast([P, nb, 32]), ALU.mult))
                dve.transpose(v, ta).then_inc(done, 1)
                quantised.append((done, 1 + sum(q[0] is done for q in quantised)))

            def layernorm(p, mx):
                for u in range(2):
                    n = 2 * p + u
                    dve.wait_ge(ln_xT, n + 1)
                    for t in range(NT):
                        s = dve.bn_stats(st6[:, t, :], PS[:, 4 + 2 * u + t // 2, (t % 2) * D:(t % 2) * D + D])
                    s.then_inc(ln_st, 1)
                    dve.wait_ge(ln_st, n + 1)
                    for t in range(NT):
                        s = dve.bn_aggr(mv[:, NT * u + t, :], st6[:, t, :])
                    s.then_inc(ln_mv, 1)
                    dve.wait_ge(ln_sd, n + 1)
                    dve.reciprocal(rstd[:, NT * u:NT * u + NT], sd[:, NT * u:NT * u + NT]).then_inc(ln_rs, 1)
                    dve.wait_ge(ln_rs, n + 1)
                    for t in range(NT):
                        j = NT * u + t
                        s = dve.tensor_scalar(h_tok[:, j, :],
                                              PS[:, 4 + 2 * u + t // 2, (t % 2) * D:(t % 2) * D + D],
                                              mv[:, j, 0:1], rstd[:, j:j + 1], ALU.subtract, ALU.mult)
                    s.then_inc(ln_h, 1)
                for u in range(2):
                    n = 2 * p + u
                    if mx:
                        dve.wait_ge(h_f32, u + 1)
                        quantise(cw_t[:, u, :], KC * H, h_q)
                        dve.wait_ge(h_hi, n + 1)
                        src = h_q_t[u]
                    else:
                        dve.wait_ge(h_hi, n + 1)
                        src = PS[:, 4 + 2 * u:6 + 2 * u, :]
                    dve.tensor_tensor(h_lo_t[:, :, half(u)], src, f32(h_hi_t[:, :, half(u)]),
                                      ALU.subtract).then_inc(h_lo, 1)

            def rope(a, p):
                if p > 0:
                    dve.wait_ge(x_out, 2 * p)
                dve.memset(v_aug[:, :, :, 8:9], 1.0).then_inc(v_one, 1)
                dve.wait_ge(rw_hi, a + 1)
                dve.tensor_tensor(rw_lo_t, rw_raw, f32(rw_hi_t), ALU.subtract).then_inc(rw_lo, 1)
                layernorm(p, False)
                for i in range(8):
                    j, u, gi = i // 2, i % 2, 8 * a + i
                    bank = 2 * (i % 2)
                    dve.wait_ge(rp_mm, gi + 1)
                    if i >= 2:
                        dve.wait_ge(rp_hi, gi - 1)
                    dve.tensor_tensor(rot_a[:, i % 2, :], PS[:, bank, :], cos_t[:, half(u)], ALU.mult)
                    dve.tensor_tensor(rot_b[:, i % 2, :], PS[:, bank + 1, :], sin_t[:, half(u)],
                                      ALU.mult).then_inc(rp_mul, 1)
                    dve.wait_ge(rp_mul, gi + 1)
                    dve.tensor_tensor(rot_a[:, i % 2, :], rot_a[:, i % 2, :], rot_b[:, i % 2, :],
                                      ALU.add).then_inc(rp_add, 1)
                    dve.wait_ge(rp_hi, gi + 1)
                    dve.tensor_tensor(rot_lo[:, j % 2, half(u)], rot_a[:, i % 2, :],
                                      f32(rot_hi[:, j % 2, half(u)]), ALU.subtract).then_inc(rp_lo, 1)

                def heads(ap, c):
                    return ap[:, c * 256:c * 256 + 144].rearrange("p (h d) -> p h d", d=9)

                def soft(b, c, v, free):
                    w = 32 * a + 4 * b + 2 * c + v
                    s = 2 * c + v
                    ps = PS[:, 4 + 2 * v:6 + 2 * v, :].rearrange("p a (h t) -> p (a h) t", t=S)
                    dve.wait_ge(lg_mm, w + 1)
                    dve.tensor_reduce(row_max[:, s, :], ps, AX_X, ALU.max).then_inc(at_mx, 1)
                    dve.wait_ge(at_mx, w + 1)
                    if not free:
                        dve.wait_ge(at_T, w - 3)
                    dve.tensor_tensor(scores[:, s], ps, row_max[:, s, :].unsqueeze(2).to_broadcast([P, 8, S]),
                                      ALU.subtract).then_inc(at_sub, 1)

                def o_norm(b, c):
                    un = 16 * a + 2 * b + c
                    o = heads(PS[:, 2, :], c)
                    dve.wait_ge(at_av, 2 * un + 2)
                    dve.reciprocal(o_rcp[:, c, :], o[:, :, 8]).then_inc(o_rc, 1)
                    dve.wait_ge(o_rc, un + 1)
                    dve.tensor_tensor(a_tok[:, c, :].rearrange("p (h d) -> p h d", d=8), o[:, :, 0:8],
                                      o_rcp[:, c, :].unsqueeze(2).to_broadcast([P, 16, 8]),
                                      ALU.mult).then_inc(a_ok, 1)

                def attn_lo(b, c):
                    dve.wait_ge(a_hi, 16 * a + 2 * b + c + 1)
                    dve.tensor_tensor(a_lo_t[:, c, bass.ds(b * S, S)], PS[:, 3, c * P:c * P + P],
                                      f32(a_hi_t[:, c, bass.ds(b * S, S)]), ALU.subtract).then_inc(a_lo, 1)

                def batch(b, first):
                    for c in range(2):
                        for v in range(2):
                            if v == 1 and not first:
                                o_norm(b - 1, c)
                            soft(b, c, v, first)
                            if v == 1 and not first:
                                attn_lo(b - 1, c)

                dve.wait_ge(v_ev, a + 1)
                batch(0, True)
                with dve.Fori(1, B) as b:
                    batch(b, False)
                for c in range(2):
                    o_norm(B - 1, c)
                    attn_lo(B - 1, c)
                for u in range(2):
                    dve.wait_ge(op_mm, 2 * a + u + 1)
                    for m in range(KC):
                        s = dve.scalar_tensor_tensor(X[:, m, half(u)], PS[:, 2 * m + u, :], bias_o[:, a, m:m + 1],
                                                     X[:, m, half(u)], ALU.add, ALU.add)
                    s.then_inc(x_out, 1)

            def select_top(vals, e, k, sel, gt, eq):
                shape = [P, 2 * NT, e, e]
                gt = gt[:, 0:2 * NT * e * e].rearrange("p (n i j) -> p n i j", i=e, j=e)
                eq = eq[:, 0:2 * NT * e * e].rearrange("p (n i j) -> p n i j", i=e, j=e)
                vj, vi = vals.unsqueeze(2).to_broadcast(shape), vals.unsqueeze(3).to_broadcast(shape)
                link(dve.tensor_tensor(gt, vj, vi, ALU.is_gt))
                link(dve.tensor_tensor(eq, vj, vi, ALU.is_equal))
                link(dve.tensor_tensor(eq, eq, tri[:, 0:e, 0:e].unsqueeze(1).to_broadcast(shape), ALU.mult))
                link(dve.tensor_tensor(gt, gt, eq, ALU.add))
                link(dve.tensor_reduce(sel, gt, AX_X, ALU.add))
                link(dve.tensor_scalar(sel, sel, float(k), None, ALU.is_lt))

            def route(fi):
                logits = PS[:, 0, 0:2 * NT * E].rearrange("p (n e) -> p n e", e=E)
                shape = [P, 2 * NT, E]
                dve.wait_ge(r_mm, 1 if fi == 0 else 2)
                if fi == 0:
                    link(dve.tensor_reduce(r_s, logits, AX_X, ALU.max))
                    dve.tensor_tensor(r_lg, logits, r_s.unsqueeze(2).to_broadcast(shape),
                                      ALU.subtract).then_inc(r_sub, 1)
                    dve.wait_ge(r_act, 1)
                    select_top(r_ex, E, TOPK, r_sel, cmp_a, cmp_b)
                    gain = TOPK / (TOPK + 1.0)
                else:
                    dve.wait_ge(r_act, 2)
                    link(dve.tensor_reduce(r_g, r_ex.rearrange("p n (g e) -> p n g e", g=4), AX_X, ALU.max))
                    select_top(r_g, 4, 2, r_gs, cmp_a, cmp_b)
                    link(dve.tensor_tensor(r_m.rearrange("p n (g e) -> p n g e", g=4),
                                           r_ex.rearrange("p n (g e) -> p n g e", g=4),
                                           r_gs.unsqueeze(3).to_broadcast([P, 2 * NT, 4, 4]), ALU.mult))
                    select_top(r_m, E, TOPK, r_sel, cmp_a, cmp_b)
                    gain = 1.0
                link(dve.tensor_tensor(r_m, r_ex, r_sel, ALU.mult))
                link(dve.tensor_reduce(r_s, r_m, AX_X, ALU.add))
                link(dve.reciprocal(r_r, r_s))
                link(dve.tensor_scalar(r_r, r_r, gain, None, ALU.mult))
                dve.tensor_tensor(r_m, r_m, r_r.unsqueeze(2).to_broadcast(shape), ALU.mult).then_inc(cw_ok, 1)

            def ffn(fi, p):
                n, cb = FFN_CHUNKS[fi], CHUNK_BASE[fi]
                routed, mx = FFN_ROUTED[fi], FFN_MX[fi]
                if mx:
                    dve.wait_ge(x_out, 2 * p)

                def w_quant(c, s, i):
                    dve.wait_ge(w13_in[s], 16 * (cb // 2 + i + 1))
                    dve.wait_ge(w2_in[s], 16 * (cb // 2 + i + 1))
                    quantise(w_raw[:, s, :], FW, w_q)

                def gate(c, u, free):
                    m = 2 * (cb + c) + u
                    dve.wait_ge(sil, m + 1)
                    if not free:
                        dve.wait_ge(g_lo, m - 1)
                    dve.tensor_tensor(g_t[:, u, :], sil_t[:, u, :], PS[:, 5 + 2 * u, :], ALU.mult).then_inc(gm, 1)
                    if mx:
                        dve.wait_ge(gm, m + 1)
                        quantise(g_t[:, u, :], H, g_q)

                def g_rest(c, u):
                    dve.wait_ge(g_hi, 2 * (cb + c) + u + 1)
                    dve.tensor_tensor(g_lo_t[:, u, :], g_t[:, u, :], f32(g_hi_t[:, u, :]),
                                      ALU.subtract).then_inc(g_lo, 1)

                if mx:
                    w_quant(0, 0, 0)
                layernorm(p, mx)
                if routed:
                    route(fi)
                if mx:
                    for c in range(n):
                        if c + 1 < n:
                            w_quant(c + 1, (c + 1) % 2, (c + 1) // 2)
                        gate(c, 0, c == 0)
                        if c:
                            g_rest(c - 1, 1)
                        gate(c, 1, c == 0)
                        g_rest(c, 0)
                    g_rest(n - 1, 1)
                else:
                    gate(0, 0, True)
                    gate(0, 1, True)
                    g_rest(0, 0)

                    def chunk(c):
                        gate(c, 0, False)
                        g_rest(c - 1, 1)
                        gate(c, 1, False)
                        g_rest(c, 0)

                    chunk(1)
                    loop_end, tail = pairs(n)
                    with dve.Fori(1, loop_end) as i:
                        chunk(2 * i)
                        chunk(2 * i + 1)
                    for c in tail:
                        chunk(c)
                    g_rest(n - 1, 1)
                for u in range(2):
                    dve.wait_ge(o_mm, 2 * (cb + n) - 1 + u)
                    for m in range(KC):
                        s = dve.tensor_tensor(X[:, m, half(u)], PS[:, 2 * m + u, :], X[:, m, half(u)], ALU.add)
                    s.then_inc(x_out, 1)

            def gqa(p):
                dve.wait_ge(l_mk, 16)
                link(dve.tensor_scalar(mbias.rearrange("p b k -> p (b k)"), mask8, MASKED, -MASKED,
                                       ALU.mult, ALU.add))
                layernorm(p, False)

                def head(g):
                    for h in range(2):
                        for u in range(2):
                            dve.wait_ge(lq_hi, 4 * g + 2 * h + u + 1)
                            dve.tensor_tensor(lq_lo_t[:, h, half(u)], PS[:, 4 + 2 * h + u, :],
                                              f32(lq_hi_t[:, h, half(u)]), ALU.subtract).then_inc(lq_lo, 1)
                    for u in range(2):
                        dve.wait_ge(lk_hi, 2 * g + u + 1)
                        dve.tensor_tensor(lk_lo_t[:, half(u)], PS[:, 4 + u, :], f32(lk_hi_t[:, half(u)]),
                                          ALU.subtract).then_inc(lk_lo, 1)
                    dve.wait_ge(lv_mm, g + 1)
                    dve.tensor_tensor(lv_t, PS[:, 6:8, :].rearrange("p a (b d) -> p (a b) d", d=D2),
                                      mcol[:].unsqueeze(2).to_broadcast([P, B, D2]), ALU.mult).then_inc(lv_ev, 1)
                    for u in range(2):
                        n = 2 * g + u
                        dve.wait_ge(l_lg, n + 1)
                        s = ls_t[:, u].rearrange("p b h k -> p (b h) k")
                        dve.tensor_tensor(
                            ls_t[:, u], PS[:, 4 + 2 * u:6 + 2 * u, :].rearrange("p a (b h k) -> p (a b) h k", b=2, h=2),
                            mbias[:, 4 * u:4 * u + 4, :].unsqueeze(2).to_broadcast([P, 4, 2, S]),
                            ALU.add).then_inc(l_add, 1)
                        dve.wait_ge(l_add, n + 1)
                        dve.tensor_reduce(l_mx[:, u, :], s, AX_X, ALU.max).then_inc(l_max, 1)
                        dve.wait_ge(l_max, n + 1)
                        dve.tensor_tensor(s, s, l_mx[:, u, :].unsqueeze(2).to_broadcast([P, 8, S]),
                                          ALU.subtract).then_inc(l_sub, 1)
                    for u in range(2):
                        n = 2 * g + u
                        dve.wait_ge(l_exp, n + 1)
                        dve.tensor_reduce(l_sm[:, u, :], ls_t[:, u].rearrange("p b h k -> p (b h) k"), AX_X,
                                          ALU.add).then_inc(l_sum, 1)
                        dve.wait_ge(l_sum, n + 1)
                        dve.reciprocal(l_rc[:, u, :], l_sm[:, u, :]).then_inc(l_rcp, 1)
                    for u in range(2):
                        dve.wait_ge(l_ohi, 2 * g + u + 1)
                        dve.tensor_tensor(
                            lo_lo_t[:, :, half(u)].rearrange("p h (b t) -> p b h t", b=4),
                            PS[:, 4 + 2 * u:6 + 2 * u, :].rearrange("p a (b h t) -> p (a b) h t", b=2, h=2),
                            f32(lo_hi_t[:, :, half(u)]).rearrange("p h (b t) -> p b h t", b=4),
                            ALU.subtract).then_inc(l_olo, 1)

                head(0)
                head(1)
                with dve.Fori(1, 4) as i:
                    head(2 * i)
                    head(2 * i + 1)
                for u in range(2):
                    dve.wait_ge(l_out, 15 + u)
                    for m in range(KC):
                        s = dve.tensor_tensor(X[:, m, half(u)], PS[:, 2 * m + u, :], X[:, m, half(u)], ALU.add)
                    s.then_inc(x_out, 1)

            for p, (kind, i) in enumerate(PHASES):
                if kind == "rope":
                    rope(i, p)
                elif kind == "ffn":
                    ffn(i, p)
                else:
                    gqa(p)


def laid_out(i):
    import numpy as np

    f4 = np.float32
    n = {k: np.asarray(v) for k, v in i.items()}

    def chunks(w):
        return w.reshape(-1, P, w.shape[1]).transpose(1, 0, 2)

    def packed(w1, w3, w2):
        c = w1.shape[1] // P
        a, b = (chunks(w).reshape(P, KC, c, P).transpose(2, 0, 1, 3).reshape(c, P, D) for w in (w1, w3))
        return np.ascontiguousarray(np.concatenate([a, b, w2.reshape(c, P, D)], 2))

    def padded(w, axis):
        pad = [(0, 0), (0, 0)]
        pad[axis] = (0, -w.shape[axis] % P)
        return np.pad(w, pad)

    swap = np.arange(D) ^ 1
    rope = []
    for l in (0, 2, 3):
        q, kv, o = n[f"L{l}_xattn_Wq"], n[f"L{l}_xattn_Wkv"], n[f"L{l}_xattn_Wout"]
        rope.append(np.concatenate([chunks(q).reshape(P, -1), chunks(q[:, swap]).reshape(P, -1), kv[:, :D],
                                    kv[:, :D][:, swap], kv[:, D:], chunks(o).reshape(P, -1)], 1))
    w0 = packed(np.concatenate([n["L0_ffn_we1"].transpose(1, 0, 2).reshape(D, -1), n["L0_ffn_ws1"]], 1),
                np.concatenate([n["L0_ffn_we3"].transpose(1, 0, 2).reshape(D, -1), n["L0_ffn_ws3"]], 1),
                np.concatenate([n["L0_ffn_we2"].reshape(-1, D), n["L0_ffn_ws2"]], 0))
    w1 = packed(n["L1_ffn_gate_w"].T, n["L1_ffn_up_w"].T, n["L1_ffn_down_w"].T)
    w2 = packed(n["L2_ffn_w_gate"].T, n["L2_ffn_w_up"].T, n["L2_ffn_w_down"].T)
    w3 = packed(padded(np.concatenate([n["L3_ffn_W1"].reshape(-1, D), n["L3_ffn_Ws1"]], 0).T, 1),
                padded(np.concatenate([n["L3_ffn_W3"].reshape(-1, D), n["L3_ffn_Ws3"]], 0).T, 1),
                padded(np.concatenate([n["L3_ffn_W2"].transpose(0, 2, 1).reshape(-1, D), n["L3_ffn_Ws2"].T], 0), 0))
    gqa = []
    for g in range(G2):
        q = n["L1_xattn_Wq"][:, g * D:(g + 1) * D]
        k, v = (n[f"L1_xattn_{x}"][:, g * D2:(g + 1) * D2] for x in ("Wk", "Wv"))
        gqa.append(np.concatenate([chunks(q).reshape(P, -1), k, v,
                                   chunks(n["L1_xattn_Wo"][g * D:(g + 1) * D]).reshape(P, -1)], 1))
    p = np.arange(P)
    cols = np.zeros((P, 8), f4)
    cols[:, 0] = np.where((p % 4) // 2 == 0, 1.0, 10000.0 ** -0.5)
    cols[:, 1] = np.where(p % 2 == 0, -1.0, 1.0)
    for j in range(4):
        cols[:, 2 + j] = (p % 32) // HD == j
    cols[:, 6] = LN_EPS
    tri = np.tile(np.tril(np.ones((E, E), f4), -1).reshape(1, -1), (P, 1))
    pos = n["fside_BxSx2_0"].reshape(T, 2).T
    mask = n["mask_BxS2_bf1"].view(np.uint8)
    return dict(
        x_t=n["x"].reshape(T, D).T, ctx_t=n["ctx_1024"].reshape(T, P).T,
        pos_rows=pos[(p % HD) // 4], mask_row=mask.reshape(1, T), mask_col=mask.T,
        rope_w=np.stack(rope), rope_b=np.stack([n[f"L{l}_xattn_bout"].reshape(KC, P).T for l in (0, 2, 3)]),
        router_w=np.stack([chunks(n["L0_ffn_w_router"]), chunks(n["L3_ffn_gate_w"].T)]),
        ffn_w0=w0, ffn_w1=w1, ffn_w2=w2, ffn_w3=w3, gqa_w=np.stack(gqa),
        cols=cols, ident_in=np.eye(P, dtype=f4), tri_in=tri)


def kernel(**inputs):
    import numpy as np
    import concourse.bacc as bacc
    from concourse.bass_utils import run_bass_kernel_spmd

    nc = bacc.Bacc("TRN2", target_bir_lowering=False, num_devices=1)
    arrays = {f"in_{k}": np.ascontiguousarray(v) for k, v in laid_out(inputs).items()}
    args = [nc.dram_tensor(k, v.shape, mybir.dt.from_np(v.dtype), kind="ExternalInput").ap()
            for k, v in arrays.items()]
    args.append(nc.dram_tensor("out_t", (D, T), F32, kind="ExternalOutput").ap())
    build(nc, *args)
    r = run_bass_kernel_spmd(nc, [arrays], core_ids=[0])
    return np.ascontiguousarray(r.results[0]["out_t"].T).reshape(B, S, D)
```

```python
from contextlib import ExitStack

import concourse.bass as bass
from concourse import mybir

F32 = mybir.dt.float32
F32R = mybir.dt.float32r
I32 = mybir.dt.int32
U8 = mybir.dt.uint8
ALU = mybir.AluOpType
ACT = mybir.ActivationFunctionType
AX_X = mybir.AxisListType.X

P = 128
B, S, D = 8, 128, 256
T = B * S
H = T // 2
KC = D // P
NT = H // P
Q_ACT = 2
HEADS, HD = 32, 8
GL = 4
E = 16
TOPK = 4
G2, D2 = 8, 128
LN_EPS = 1e-5
RW = 2304
FW = 3 * D
LW = 2 * D + 2 * P + 2 * D
MASKED = 1e30
TWO_PI_INV = 0.15915494309189535
PI_HI, PI_LO = 6.28125, 0.0019353071795864769
ROUND = 12582912.0
FP8_ROUND = 1.5 * 2.0 ** 20

FFN_CHUNKS = [20, 8, 8, 25]
FFN_ROUTED = [True, False, False, True]
FFN_MX = [False, True, False, False]
CHUNK_BASE = [0, 20, 28, 36]
ROUTED_BASE = {0: 0, 3: 20}
ROW_BLOCK = 16
ROWS_PER_EXPERT = {0: 8, 3: 11}


def build(nc, x_t, ctx_t, pos_rows, mask_row, mask_col, rope_w, rope_b, router_w, ffn_w0, ffn_w1,
          ffn_w2, ffn_w3, gqa_w, cols, ident_in, tri_in, out, n_phases=8):
    ffn_w = [ffn_w0, ffn_w1, ffn_w2, ffn_w3]
    PHASES = [("rope", 0), ("ffn", 0), ("gqa", 0), ("ffn", 1), ("rope", 1), ("ffn", 2), ("rope", 2),
              ("ffn", 3)][:n_phases]

    with ExitStack() as ctx:
        def sb(name, shape, dt=F32):
            return ctx.enter_context(nc.sbuf_tensor(name, shape, dt))

        def sem(name):
            return ctx.enter_context(nc.semaphore(name))

        PS = ctx.enter_context(nc.psum_tensor("PS", [P, 8, 512], F32))
        cw_rows = {f: nc.dram_tensor(f"cw_rows{f}", [FFN_CHUNKS[f] * 8, T], F32, kind="Internal").ap()
                   for f in (0, 3)}
        turned = nc.dram_tensor("turned", [8, P, 2, H], F32, kind="Internal").ap()

        X = sb("X", [P, KC, T])
        h_hi_t = sb("h_hi_t", [P, KC, T], F32R)
        h_lo_t = sb("h_lo_t", [P, KC, T], F32R)
        h_tok = sb("h_tok", [P, 2 * NT, D])
        ctx_hi = sb("ctx_hi", [P, T], F32R)
        ctx_lo = sb("ctx_lo", [P, T], F32R)
        cos_t = sb("cos_t", [P, T])
        sin_t = sb("sin_t", [P, T])
        ident = sb("ident", [P, P])
        tri = sb("tri", [P, E, E])
        col = sb("col", [P, 8])
        bias_o = sb("bias_o", [P, 3, KC])
        wr_raw = sb("wr_raw", [P, 2, KC, E])
        wr_hi = sb("wr_hi", [P, 2, KC, E], F32R)
        wr_lo = sb("wr_lo", [P, 2, KC, E], F32R)
        st6 = sb("st6", [P, NT, 6])
        mv = sb("mv", [P, 2 * NT, 2])
        sd = sb("sd", [P, 2 * NT])
        rstd = sb("rstd", [P, 2 * NT])
        mcol8 = sb("mcol8", [P, B], U8)
        mcol = sb("mcol", [P, B])
        ctx_raw = h_tok[:, 0:4, :].rearrange("p a b -> p (a b)")
        shared_c = sb("shared_c", [32, 2, 64])

        RSZ = 2 * RW + 4 * T + 2 * 512 + 4 * 2048
        FSZ = 21888
        AR = sb("AR", [P, RSZ], F32R)
        AF = sb("AF", [P, FSZ])

        def carve(arena):
            at = [0]

            def take(n):
                a = arena[:, at[0]:at[0] + n]
                at[0] += n
                return a
            return take

        r = carve(AR)
        rw_hi_t, rw_lo_t = r(RW), r(RW)
        rot = r(4 * T).rearrange("p (n s t) -> p n s t", n=4, s=2)
        q_fix = r(2 * 512).rearrange("p (c g t) -> p c g t", c=2, g=GL)
        k_msk, q_msk = ([r(2048).rearrange("p (g j t) -> p g j t", g=GL, j=4) for _ in range(2)] for _ in range(2))
        k_fix = rw_hi_t[:, 0:1024].rearrange("p (c g t) -> p c g t", c=2, g=GL)
        minus_one = rw_hi_t[:, 1024:1024 + P]
        diag = rw_lo_t[:, 0:1024].rearrange("p (h t) -> p h t", h=8)
        f = carve(AF)
        pT_or_rot = f(RW)
        rw_raw = pT_or_rot
        pT = pT_or_rot[:, 0:2048].rearrange("p (v h t) -> p v h t", v=2, h=8)
        rot_a = pT_or_rot[:, 0:1024].rearrange("p (s t) -> p s t", s=2)
        rot_b = pT_or_rot[:, 1024:2048].rearrange("p (s t) -> p s t", s=2)
        K_all = f(8 * T).rearrange("p (g t) -> p g t", g=8)
        Q_all = f(8 * T).rearrange("p (g t) -> p g t", g=8)
        turns = AF[:, RW:RW + T]
        v_all = h_tok[:].rearrange("p a n -> p (a n)").rearrange("p (b h d) -> p b h d", b=B, h=HEADS)
        v_fix = f(HEADS * 32).rearrange("p (h d) -> p h d", h=HEADS)
        o_feat = f(2 * 512).rearrange("p (c n) -> p c n", c=2)
        a_tok = f(2 * P).rearrange("p (c d) -> p c d", c=2)
        row_max = f(2 * 8).rearrange("p (s h) -> p s h", s=2)
        o_rcp = f(2 * 16).rearrange("p (c h) -> p c h", c=2)
        r = carve(AR)
        w_hi_t = r(2 * FW).rearrange("p (s n) -> p s n", s=2)
        w_lo_t = r(2 * FW).rearrange("p (s n) -> p s n", s=2)
        g_hi_t = r(2 * H).rearrange("p (u t) -> p u t", u=2)
        g_lo_t = r(2 * H).rearrange("p (u t) -> p u t", u=2)
        f = carve(AF)
        w_raw = f(2 * FW).rearrange("p (s n) -> p s n", s=2)
        cw_t = f(2 * T).rearrange("p (s t) -> p s t", s=2)
        sil_t = f(2 * H).rearrange("p (u t) -> p u t", u=2)
        g_t = f(2 * H).rearrange("p (u t) -> p u t", u=2)
        tmp_ab = f(2048)
        tmp_a, tmp_b = tmp_ab[:, 0:1024], tmp_ab[:, 1024:2048]
        amax, scl, rscl = f(32), f(32), f(32)
        cw_T = f(T)
        r_lg = f(2 * NT * E).rearrange("p (n e) -> p n e", e=E)
        r_ex = f(2 * NT * E).rearrange("p (n e) -> p n e", e=E)
        r_sel = f(2 * NT * E).rearrange("p (n e) -> p n e", e=E)
        r_m = f(2 * NT * E).rearrange("p (n e) -> p n e", e=E)
        r_g = f(2 * NT * 4).rearrange("p (n e) -> p n e", e=4)
        r_gs = f(2 * NT * 4).rearrange("p (n e) -> p n e", e=4)
        r_s = f(2 * NT)
        r_r = f(2 * NT)
        cmp_a = cw_t.rearrange("p s t -> p (s t)")
        cmp_b = tmp_ab
        h_q_t = [cw_t[:, u, :].rearrange("p (k t) -> p k t", k=KC) for u in range(2)]
        r = carve(AR)
        l_hi_t = r(2 * LW).rearrange("p (s n) -> p s n", s=2)
        l_lo_t = r(2 * LW).rearrange("p (s n) -> p s n", s=2)
        lq_hi_t = r(2 * T).rearrange("p (h t) -> p h t", h=2)
        lq_lo_t = r(2 * T).rearrange("p (h t) -> p h t", h=2)
        lk_hi_t, lk_lo_t = r(T), r(T)
        lo_hi_t = r(2 * T).rearrange("p (h t) -> p h t", h=2)
        lo_lo_t = r(2 * T).rearrange("p (h t) -> p h t", h=2)
        f = carve(AF)
        l_raw = f(2 * LW).rearrange("p (s n) -> p s n", s=2)
        lv_t = f(T).rearrange("p (b d) -> p b d", b=B)
        ls_t = f(2 * T).rearrange("p (u b h k) -> p u b h k", u=2, b=4, h=2)
        lp_t = f(2 * T).rearrange("p (u b h k) -> p u b h k", u=2, b=4, h=2)
        l_mx = f(16).rearrange("p (u b) -> p u b", u=2)
        l_sm = f(16).rearrange("p (u b) -> p u b", u=2)
        l_rc = f(16).rearrange("p (u b) -> p u b", u=2)
        mask8 = f(T // 4).bitcast(U8)
        mbias = f(T).rearrange("p (b k) -> p b k", b=B)

        s_const, s_x, s_ctx = sem("s_const"), sem("s_x"), sem("s_ctx")
        s_pool0, s_act0, s_dve0 = sem("s_pool0"), sem("s_act0"), sem("s_dve0")
        s_sin, s_ang = sem("s_sin"), sem("s_ang")
        x_out = sem("x_out")
        ln_xT, ln_st, ln_mv, ln_sd, ln_rs, ln_h, ln_hT = (
            sem(n) for n in ("ln_xT", "ln_st", "ln_mv", "ln_sd", "ln_rs", "ln_h", "ln_hT"))
        h_f32, h_q, h_hi, h_lo = sem("h_f32"), sem("h_q"), sem("h_hi"), sem("h_lo")
        rw_in, rw_hi, rw_lo = sem("rw_in"), sem("rw_hi"), sem("rw_lo")
        v_one, v_mm, v_ev = sem("v_one"), sem("v_mm"), sem("v_ev")
        rp_mm, rp_mul, rp_add, rp_hi, rp_lo = (
            sem(n) for n in ("rp_mm", "rp_mul", "rp_add", "rp_hi", "rp_lo"))
        rp_wr, k_in, q_in = ([sem(f"{n}{i}") for i in range(2)] for n in ("rp_wr", "k_in", "q_in"))
        km, qm, fix, v_fx, lg_mm, lt_mm, at_mx, at_dg, at_exp, at_av = (
            sem(n) for n in ("km", "qm", "fix", "v_fx", "lg_mm", "lt_mm", "at_mx", "at_dg", "at_exp", "at_av"))
        o_ev, o_bk, o_rc, a_ok, at_z, a_hi, a_lo, op_mm = (
            sem(n) for n in ("o_ev", "o_bk", "o_rc", "a_ok", "at_z", "a_hi", "a_lo", "op_mm"))
        w13_in, w2_in = [sem("w13_in0"), sem("w13_in1")], [sem("w2_in0"), sem("w2_in1")]
        cw_in = [sem("cw_in0"), sem("cw_in1")]
        w_q, w13_hi, w13_lo, w2_hi, w2_lo = (sem(n) for n in ("w_q", "w13_hi", "w13_lo", "w2_hi", "w2_lo"))
        ab, sil, gm, g_cw, g_q, g_hi, g_lo, o_mm = (
            sem(n) for n in ("ab", "sil", "gm", "g_cw", "g_q", "g_hi", "g_lo", "o_mm"))
        r_mm, r_sub, r_act, cw_ok, cw_tr, cw_ev, cw_wr, cw_sh = (
            sem(n) for n in ("r_mm", "r_sub", "r_act", "cw_ok", "cw_tr", "cw_ev", "cw_wr", "cw_sh"))
        q_step = sem("q_step")
        lw_in = [sem("lw_in0"), sem("lw_in1")]
        lw_hi, lw_lo = sem("lw_hi"), sem("lw_lo")
        lq_mm, lq_hi, lq_lo, lk_mm, lk_hi, lk_lo, lv_mm, lv_ev = (
            sem(n) for n in ("lq_mm", "lq_hi", "lq_lo", "lk_mm", "lk_hi", "lk_lo", "lv_mm", "lv_ev"))
        l_lg, l_add, l_max, l_sub, l_exp, l_sum, l_rcp, l_nrm, l_T, l_pT, l_av, l_ohi, l_olo, l_out = (
            sem(n) for n in ("l_lg", "l_add", "l_max", "l_sub", "l_exp", "l_sum", "l_rcp", "l_nrm", "l_T",
                             "l_pT", "l_av", "l_ohi", "l_olo", "l_out"))
        l_mk = sem("l_mk")
        s_out = sem("s_out")

        block = ctx.enter_context(nc.Block())

        def f32(ap):
            return ap.bitcast(F32)

        def half(u):
            return slice(u * H, (u + 1) * H)

        def wait_x(eng, p, u):
            if p == 0:
                eng.wait_ge(s_x, 16)
            else:
                eng.wait_ge(x_out, 2 * (p - 1) + u + 1)

        def pairs(n):
            return n // 2 - (1 if n % 2 == 0 else 0), range(n - (2 - n % 2), n)

        def behind(b, c, v, lag):
            i = 2 * c + v - lag
            return (b if i >= 0 else b - 1), i % 4 // 2, i % 2

        def product(pe, dst, sides, start=True, stop=True):
            for i, (wh, wl, mh, ml) in enumerate(sides):
                pe.matmul(dst, wh, mh, start=start and i == 0, stop=False)
                pe.matmul(dst, wh, ml, start=False, stop=False)
                last = pe.matmul(dst, wl, mh, start=False, stop=stop and i == len(sides) - 1)
            return last

        @block.sync
        def _(sp):
            sp.dma_start(X[:], x_t.rearrange("(k p) t -> p k t", p=P)).then_inc(s_x, 16)
            sp.dma_start(col[:], cols).then_inc(s_const, 16)
            sp.dma_start(cos_t[:], pos_rows).then_inc(s_const, 16)
            sp.dma_start(ident[:], ident_in).then_inc(s_const, 16)
            sp.dma_start(ctx_raw, ctx_t).then_inc(s_ctx, 16)
            sp.dma_start(tri[:], tri_in.rearrange("p (i j) -> p i j", i=E)).then_inc(s_const, 16)
            sp.dma_start(bias_o[:], rope_b.rearrange("l p k -> p l k")).then_inc(s_const, 16)
            sp.dma_start(wr_raw[:], router_w.rearrange("l p k e -> p l k e")).then_inc(s_const, 16)
            sp.dma_start(mcol8[:], mask_col).then_inc(s_const, 16)
            sp.wait_ge(s_dve0, 2)
            for i, (fi, n) in enumerate(((0, 32), (3, 24))):
                sp.dma_start(cw_rows[fi][FFN_CHUNKS[fi] * 8 - n:, :].rearrange("n (a c) -> n a c", c=64),
                             shared_c[0:n, i:i + 1, :].to_broadcast([n, T // 64, 64])).then_inc(cw_sh, 16)

            def rope_moves(a, p):
                if p > 0:
                    sp.wait_ge(x_out, 2 * p)
                sp.dma_start(rw_raw, rope_w[a]).then_inc(rw_in, 16)
                def write(t):
                    sp.wait_ge(rp_lo, 8 * a + t + 1)
                    sp.dma_start(turned[t], f32(rot[:, t % 4])).then_inc(rp_wr[t % 2], 16)

                def read(t):
                    u, j = t // 4, t % 4
                    dst, arrived, m = (K_all, Q_all)[j // 2], (k_in, q_in)[j // 2], j % 2
                    sp.wait_ge(rp_wr[t % 2], 16 * (4 * a + t // 2 + 1))
                    for s, part in enumerate((0, 0, 1) if j < 2 else (0, 1, 0)):
                        sp.dma_start(dst[32 * s:32 * s + 32, GL * m:GL * m + GL, half(u)],
                                     turned[t, :, part, :].rearrange("(g r) t -> r g t", g=GL)
                                     ).then_inc(arrived[u], 16)

                write(0)
                for t in range(1, 8):
                    write(t)
                    read(t - 1)
                read(7)

            def ffn_loads(fi, p):
                n, cb = FFN_CHUNKS[fi], CHUNK_BASE[fi]
                routed, rb = FFN_ROUTED[fi], ROUTED_BASE.get(fi)
                sp.wait_ge(x_out, 2 * p)

                def w_load(c, s, first):
                    src = ffn_w[fi][c] if isinstance(c, int) else \
                        ffn_w[fi][bass.ds(c, 1)].rearrange("a p n -> (a p) n")
                    if not first:
                        sp.wait_ge(w13_lo, cb + c - 1)
                    sp.dma_start(w_raw[:, s, 0:2 * D], src[:, 0:2 * D]).then_inc(w13_in[s], 16)
                    if not first:
                        sp.wait_ge(w2_lo, cb + c - 1)
                    sp.dma_start(w_raw[:, s, 2 * D:FW], src[:, 2 * D:FW]).then_inc(w2_in[s], 16)

                def cw_load(c, s, src, first):
                    if not first:
                        sp.wait_ge(g_cw, 2 * (rb + c) - 2)
                    sp.dma_start(cw_t[:, s, :], src).then_inc(cw_in[s], 16)

                def cw_src(c):
                    v = cw_rows[fi].rearrange("(c r) t -> c r t", r=8)
                    v = v[c] if isinstance(c, int) else v[bass.ds(c, 1)].rearrange("a r t -> (a r) t")
                    return v.unsqueeze(1).to_broadcast([8, ROW_BLOCK, T])

                for c in range(2):
                    w_load(c, c, True)
                if routed:
                    e_rows = ROWS_PER_EXPERT[fi]
                    sp.wait_ge(cw_ev, 1 if fi == 0 else 2)
                    sp.dma_start(cw_rows[fi][0:E * e_rows, :].rearrange("(e r) t -> e r t", r=e_rows),
                                 cw_T[0:E, :].unsqueeze(1).to_broadcast([E, e_rows, T])).then_inc(cw_wr, 16)
                    sp.wait_ge(cw_wr, 16 if fi == 0 else 32)
                    sp.wait_ge(cw_sh, 32)
                    for c in range(2):
                        cw_load(c, c, cw_src(c), True)
                loop_end, tail = pairs(n)
                with sp.Fori(1, loop_end) as i:
                    for s in range(2):
                        w_load(2 * i + s, s, False)
                        if routed:
                            cw_load(2 * i + s, s, cw_src(2 * i + s), False)
                for c in tail:
                    w_load(c, c % 2, False)
                    if routed:
                        cw_load(c, c % 2, cw_src(c), False)

            def gqa_loads(p):
                sp.wait_ge(x_out, 2 * p)
                sp.dma_start(mask8, mask_row.to_broadcast([P, T])).then_inc(l_mk, 16)
                for g in range(2):
                    sp.dma_start(l_raw[:, g, :], gqa_w[g]).then_inc(lw_in[g], 16)
                with sp.Fori(1, 4) as i:
                    for s in range(2):
                        sp.wait_ge(lw_lo, 2 * i + s - 1)
                        sp.dma_start(l_raw[:, s, :], gqa_w[bass.ds(2 * i + s, 1)]
                                     .rearrange("a p n -> (a p) n")).then_inc(lw_in[s], 16)

            for p, (kind, i) in enumerate(PHASES):
                if kind == "rope":
                    rope_moves(i, p)
                elif kind == "ffn":
                    ffn_loads(i, p)
                else:
                    gqa_loads(p)
            for u in range(2):
                sp.wait_ge(x_out, 2 * (len(PHASES) - 1) + u + 1)
                sp.dma_start(out.rearrange("(k p) t -> p k t", p=P)[:, :, half(u)],
                             X[:, :, half(u)]).then_inc(s_out, 16)
            sp.wait_ge(s_out, 32)
            sp.wait_ge(cw_sh, 32)

        @block.gpsimd
        def _(pool):
            def rope(a, p):
                if a > 0:
                    pool.wait_ge(x_out, 2 * p)
                pool.memset(v_fix[:, :, 9:32], 0.0)
                pool.memset(v_fix[:, :, 8:9], 1.0).then_inc(v_one, 1)
                for t in range(8):
                    pool.wait_ge(rp_mul, 8 * a + t + 1)
                    pool.tensor_tensor(rot_a[:, t % 2, :], rot_a[:, t % 2, :], rot_b[:, t % 2, :],
                                       ALU.add).then_inc(rp_add, 1)
                pool.tensor_scalar(minus_one, ident[:], 0.0, -1.0, ALU.mult, ALU.add).then_inc(v_one, 1)

                def unit(b, c, free):
                    for dst, src, mm, done, j in ((k_msk, K_all, lg_mm, km, 0), (q_msk, Q_all, lt_mm, qm, Q_ACT)):
                        if not free:
                            pool.wait_ge(mm, 2 * (16 * a + 2 * b + c - 1))
                        part = src[0:96, GL * c:GL * c + GL, bass.ds(b * S, S)]
                        shape = [96, GL, 4 - j, S]
                        pool.tensor_tensor(dst[c][0:96, :, j:4], part.unsqueeze(2).to_broadcast(shape),
                                           col[0:96, 2 + j:6].unsqueeze(1).unsqueeze(3).to_broadcast(shape),
                                           ALU.mult).then_inc(done, 1)

                for u in range(2):
                    pool.wait_ge(k_in[u], 96 * (a + 1))
                    pool.wait_ge(q_in[u], 96 * (a + 1))
                    if u == 0:
                        for c in range(2):
                            unit(0, c, True)
                with pool.Fori(1, B) as b:
                    for c in range(2):
                        unit(b, c, False)

            def ffn(fi):
                n, cb = FFN_CHUNKS[fi], CHUNK_BASE[fi]
                routed, rb = FFN_ROUTED[fi], ROUTED_BASE.get(fi)

                def split(c, s, part, hi, lo):
                    pool.wait_ge(hi, cb + c + 1)
                    pool.tensor_tensor(w_lo_t[:, s, part], w_raw[:, s, part], f32(w_hi_t[:, s, part]),
                                       ALU.subtract).then_inc(lo, 1)

                def route(c, s, i, u):
                    if u == 0:
                        pool.wait_ge(cw_in[s], 16 * (rb // 2 + i + 1))
                    pool.wait_ge(gm, 2 * (cb + c) + u + 1)
                    pool.tensor_tensor(g_t[:, u, :], g_t[:, u, :], cw_t[:, s, half(u)],
                                       ALU.mult).then_inc(g_cw, 1)

                def chunk(c, s, i, last):
                    if routed:
                        route(c, s, i, 0)
                    if not last:
                        split(c + 1, 1 - s, slice(0, 2 * D), w13_hi, w13_lo)
                    if routed:
                        route(c, s, i, 1)
                    split(c, s, slice(2 * D, FW), w2_hi, w2_lo)

                split(0, 0, slice(0, 2 * D), w13_hi, w13_lo)
                chunk(0, 0, 0, False)
                chunk(1, 1, 0, False)
                loop_end, tail = pairs(n)
                with pool.Fori(1, loop_end) as i:
                    chunk(2 * i, 0, i, False)
                    chunk(2 * i + 1, 1, i, False)
                for c in tail:
                    chunk(c, c % 2, c // 2, c == n - 1)

            def gqa():
                def split(g, s):
                    pool.wait_ge(lw_hi, g + 1)
                    pool.tensor_tensor(l_lo_t[:, s, :], l_raw[:, s, :], f32(l_hi_t[:, s, :]),
                                       ALU.subtract).then_inc(lw_lo, 1)

                def norm(g):
                    for u in range(2):
                        pool.wait_ge(l_rcp, 2 * g + u + 1)
                        v = ls_t[:, u].rearrange("p b h k -> p (b h) k")
                        pool.tensor_tensor(v, v, l_rc[:, u, :].unsqueeze(2).to_broadcast([P, 8, S]),
                                           ALU.mult).then_inc(l_nrm, 1)

                split(0, 0)
                split(1, 1)
                norm(0)
                norm(1)
                with pool.Fori(1, 4) as i:
                    for s in range(2):
                        split(2 * i + s, s)
                        norm(2 * i + s)

            for p, (kind, i) in enumerate(PHASES):
                if kind == "rope":
                    rope(i, p)
                elif kind == "ffn":
                    ffn(i)
                else:
                    gqa()

        @block.scalar
        def _(act):
            act.wait_ge(s_ctx, 16)
            act.activation(ctx_hi[:], ctx_raw, ACT.Copy).then_inc(s_act0, 1)
            act.wait_ge(s_const, 7 * 16)
            act.activation(wr_hi[:], wr_raw[:], ACT.Copy).then_inc(s_act0, 1)
            act.wait_ge(s_ang, 13)
            act.activation(cos_t[:], cos_t[:], ACT.Sin).then_inc(s_sin, 1)
            act.activation(sin_t[:], sin_t[:], ACT.Sin).then_inc(s_sin, 1)

            def layernorm(p, mx):
                for u in range(2):
                    n = 2 * p + u
                    act.wait_ge(ln_mv, n + 1)
                    act.activation(sd[:, NT * u:NT * u + NT], mv[:, NT * u:NT * u + NT, 1], ACT.Sqrt,
                                   bias=col[:, 6:7]).then_inc(ln_sd, 1)
                for u in range(2):
                    n = 2 * p + u
                    act.wait_ge(ln_hT, n + 1)
                    src = PS[:, 4 + 2 * u:6 + 2 * u, :]
                    if mx:
                        dst = h_q_t[u]
                        act.activation(dst, src, ACT.Copy).then_inc(h_f32, 1)
                        act.wait_ge(h_q, u + 1)
                        src = dst
                    act.activation(h_hi_t[:, :, half(u)], src, ACT.Copy).then_inc(h_hi, 1)

            def rope(a, p):
                act.wait_ge(rw_in, 16 * (a + 1))
                act.activation(rw_hi_t, rw_raw, ACT.Copy).then_inc(rw_hi, 1)
                layernorm(p, False)
                act.wait_ge(v_mm, a + 1)
                for n in range(4):
                    act.activation(v_all[:, 2 * n:2 * n + 2].rearrange("p b h d -> p (b h d)"), PS[:, n, :],
                                   ACT.Copy).then_inc(v_ev, 1)
                for t in range(8):
                    act.wait_ge(rp_add, 8 * a + t + 1)
                    if t >= 4:
                        act.wait_ge(rp_wr[t % 2], 16 * (4 * a + t // 2 - 1))
                    act.activation(rot[:, t % 4, 0, :], rot_a[:, t % 2, :], ACT.Copy).then_inc(rp_hi, 1)

                def fixed(b, c):
                    for dst, src in ((q_fix, Q_all), (k_fix, K_all)):
                        act.activation(dst[0:96, c], src[0:96, GL * c:GL * c + GL, bass.ds(b * S, S)],
                                       ACT.Copy)
                    for j in range(Q_ACT):
                        s = act.activation(q_msk[c][0:96, :, j, :],
                                           Q_all[0:96, GL * c:GL * c + GL, bass.ds(b * S, S)], ACT.Copy,
                                           scale=col[0:96, 2 + j:3 + j])
                    s.then_inc(fix, 1)

                def v_fixed(b, c, free):
                    if not free:
                        act.wait_ge(at_av, 32 * a + 4 * b + 2 * c - 2)
                    vb = v_all[:, bass.ds(b, 1), 16 * c:16 * c + 16, :].rearrange("p a h d -> p (a h) d")
                    act.activation(v_fix[:, 16 * c:16 * c + 16, 0:8], vb, ACT.Copy).then_inc(v_fx, 1)

                def probs(b, c, v, free):
                    w = 32 * a + 4 * b + 2 * c + v
                    act.wait_ge(lt_mm, w + 1)
                    if not free:
                        act.wait_ge(at_av, w - 1)
                    act.activation(pT[:, v].rearrange("p h t -> p (h t)"),
                                   PS[:, 2:4, :].rearrange("p a b -> p (a b)"), ACT.Exp,
                                   scale=HD ** -0.5).then_inc(at_exp, 1)

                def o_copy(b, c):
                    act.wait_ge(at_av, 32 * a + 4 * b + 2 * c + 2)
                    act.activation(o_feat[:, c, :], PS[:, 4 + c, :], ACT.Copy).then_inc(o_ev, 1)

                def attn_hi(b, c):
                    act.wait_ge(at_z, 16 * a + 2 * b + c + 1)
                    act.activation(h_hi_t[:, c, bass.ds(b * S, S)], PS[:, 7, c * P:c * P + P],
                                   ACT.Copy).then_inc(a_hi, 1)

                def batch(b, first, last):
                    for c in range(2):
                        for v in range(2):
                            i = 2 * c + v
                            if v == 0 and not first:
                                o_copy(b - 1, c)
                            if not first or i >= 1:
                                probs(*behind(b, c, v, 1), first and i <= 2)
                            if v == 0 and c == 0 and not first:
                                fixed(b, 1)
                            if v == 0 and c == 1 and not last:
                                fixed(b + 1, 0)
                            if v == 1:
                                v_fixed(b, c, first)
                                if not first:
                                    attn_hi(b - 1, c)

                act.wait_ge(k_in[0], 96 * (a + 1))
                act.wait_ge(q_in[0], 96 * (a + 1))
                fixed(0, 0)
                fixed(0, 1)
                batch(0, True, False)
                act.wait_ge(k_in[1], 96 * (a + 1))
                act.wait_ge(q_in[1], 96 * (a + 1))
                with act.Fori(1, B - 1) as b:
                    batch(b, False, False)
                batch(B - 1, False, True)
                o_copy(B - 1, 0)
                probs(B - 1, 1, 1, False)
                o_copy(B - 1, 1)
                for c in range(2):
                    attn_hi(B - 1, c)

            def ffn(fi, p):
                n, cb = FFN_CHUNKS[fi], CHUNK_BASE[fi]
                routed, mx = FFN_ROUTED[fi], FFN_MX[fi]

                def w13_split(c, s, i, free):
                    act.wait_ge(w13_in[s], 16 * (cb // 2 + i + 1))
                    if mx:
                        act.wait_ge(w_q, c + 1)
                    if not free:
                        act.wait_ge(ab, 2 * (cb + c) - 2)
                    act.activation(w_hi_t[:, s, 0:2 * D], w_raw[:, s, 0:2 * D], ACT.Copy).then_inc(w13_hi, 1)

                def w2_split(c, s, i, free):
                    act.wait_ge(w2_in[s], 16 * (cb // 2 + i + 1))
                    if not free:
                        act.wait_ge(o_mm, 2 * (cb + c) - 2)
                    act.activation(w_hi_t[:, s, 2 * D:FW], w_raw[:, s, 2 * D:FW], ACT.Copy).then_inc(w2_hi, 1)

                def silu(c, u):
                    act.wait_ge(ab, 2 * (cb + c) + u + 1)
                    act.activation(sil_t[:, u, :], PS[:, 4 + 2 * u, :], ACT.Silu).then_inc(sil, 1)

                def g_split(c, u, free):
                    m = 2 * (cb + c) + u
                    if mx:
                        act.wait_ge(g_q, 2 * c + u + 1)
                    elif routed:
                        act.wait_ge(g_cw, m + 1 - 2 * cb + 2 * ROUTED_BASE[fi])
                    else:
                        act.wait_ge(gm, m + 1)
                    if not free:
                        act.wait_ge(o_mm, m - 1)
                    act.activation(g_hi_t[:, u, :], g_t[:, u, :], ACT.Copy).then_inc(g_hi, 1)

                act.wait_ge(x_out, 2 * p)
                w13_split(0, 0, 0, True)
                layernorm(p, mx)
                if routed:
                    if fi == 0:
                        act.wait_ge(r_sub, 1)
                        act.activation(r_ex, r_lg, ACT.Exp).then_inc(r_act, 1)
                    else:
                        act.wait_ge(r_mm, 2)
                        act.activation(r_ex, PS[:, 0, 0:2 * NT * E].rearrange("p (n e) -> p n e", e=E),
                                       ACT.Sigmoid).then_inc(r_act, 1)
                w13_split(1, 1, 0, True)
                silu(0, 0)
                w2_split(0, 0, 0, True)
                silu(0, 1)
                if routed:
                    act.wait_ge(cw_tr, 1 if fi == 0 else 2)
                    act.activation(cw_T[0:E, :], PS[0:E, 2:4, :].rearrange("p a b -> p (a b)"),
                                   ACT.Copy).then_inc(cw_ev, 1)
                g_split(0, 0, True)

                def chunk(c, s, i, first, last):
                    if not last:
                        w13_split(c + 1, 1 - s, i + s, False)
                    silu(c, 0)
                    g_split(c - 1, 1, first)
                    w2_split(c, s, i, first)
                    silu(c, 1)
                    g_split(c, 0, False)

                chunk(1, 1, 0, True, False)
                loop_end, tail = pairs(n)
                with act.Fori(1, loop_end) as i:
                    chunk(2 * i, 0, i, False, False)
                    chunk(2 * i + 1, 1, i, False, False)
                for c in tail:
                    chunk(c, c % 2, c // 2, False, c == n - 1)
                g_split(n - 1, 1, False)

            def gqa(p):
                act.wait_ge(x_out, 2 * p)

                def w_split(g, s, i, free):
                    act.wait_ge(lw_in[s], 16 * (i + 1))
                    if not free:
                        act.wait_ge(l_out, 2 * g - 2)
                    act.activation(l_hi_t[:, s, :], l_raw[:, s, :], ACT.Copy).then_inc(lw_hi, 1)

                def head(g):
                    for h in range(2):
                        for u in range(2):
                            act.wait_ge(lq_mm, 4 * g + 2 * h + u + 1)
                            act.activation(lq_hi_t[:, h, half(u)], PS[:, 4 + 2 * h + u, :],
                                           ACT.Copy).then_inc(lq_hi, 1)
                    for u in range(2):
                        act.wait_ge(lk_mm, 2 * g + u + 1)
                        act.activation(lk_hi_t[:, half(u)], PS[:, 4 + u, :], ACT.Copy).then_inc(lk_hi, 1)
                    for u in range(2):
                        act.wait_ge(l_sub, 2 * g + u + 1)
                        s = ls_t[:, u].rearrange("p b h k -> p (b h k)")
                        act.activation(s, s, ACT.Exp, scale=D2 ** -0.5).then_inc(l_exp, 1)
                    for u in range(2):
                        act.wait_ge(l_T, 2 * g + u + 1)
                        act.activation(lp_t[:, u].rearrange("p b h k -> p (b h k)"),
                                       PS[:, 4 + 2 * u:6 + 2 * u, :].rearrange("p a b -> p (a b)"),
                                       ACT.Copy).then_inc(l_pT, 1)
                    for u in range(2):
                        act.wait_ge(l_av, 2 * g + u + 1)
                        act.activation(
                            lo_hi_t[:, :, half(u)].rearrange("p h (b t) -> p b h t", b=4),
                            PS[:, 4 + 2 * u:6 + 2 * u, :].rearrange("p a (b h t) -> p (a b) h t", b=2, h=2),
                            ACT.Copy).then_inc(l_ohi, 1)

                w_split(0, 0, 0, True)
                layernorm(p, False)
                w_split(1, 1, 0, True)
                head(0)
                head(1)
                with act.Fori(1, 4) as i:
                    for s in range(2):
                        w_split(2 * i + s, s, i, False)
                        head(2 * i + s)

            for p, (kind, i) in enumerate(PHASES):
                if kind == "rope":
                    rope(i, p)
                elif kind == "ffn":
                    ffn(i, p)
                else:
                    gqa(p)

        @block.tensor
        def _(pe):
            pe.wait_ge(s_const, 7 * 16)
            pe.wait_ge(s_act0, 2)
            pe.wait_ge(s_dve0, 4)

            def ln_forward(p):
                for u in range(2):
                    wait_x(pe, p, u)
                    for t in range(NT):
                        for k in range(KC):
                            tr = pe.transpose(PS[:, 4 + 2 * u + t // 2, (t % 2) * D + k * P:(t % 2) * D + k * P + P],
                                              X[:, k, u * H + t * P:u * H + t * P + P], ident[:])
                    tr.then_inc(ln_xT, 1)

            def ln_back(p):
                for u in range(2):
                    pe.wait_ge(ln_h, 2 * p + u + 1)
                    for t in range(NT):
                        for k in range(KC):
                            tr = pe.transpose(PS[:, 4 + 2 * u + k, t * P:t * P + P],
                                              h_tok[:, NT * u + t, k * P:k * P + P], ident[:])
                    tr.then_inc(ln_hT, 1)

            def rope(a, p):
                ln_forward(p)
                ln_back(p)
                pe.wait_ge(rw_hi, a + 1)
                pe.wait_ge(rw_lo, a + 1)

                def w(off, n):
                    return rw_hi_t[:, off:off + n], rw_lo_t[:, off:off + n]

                wv = w(1536, D)
                for b in range(B):
                    c = slice(b * S, b * S + S)
                    mm = product(pe, PS[:, b // 2, (b % 2) * D:(b % 2) * D + D],
                                 [(ctx_hi[:, c], ctx_lo[:, c], *wv)])
                mm.then_inc(v_mm, 1)
                for t in range(8):
                    u, j, bank = t // 4, t % 4, 2 * (t % 2)
                    m = j % 2
                    if t < 2:
                        pe.wait_ge(v_ev, 4 * a + 2 * t + 2)
                    else:
                        pe.wait_ge(rp_mul, 8 * a + t - 1)
                    if j == 2:
                        pe.wait_ge(h_lo, 2 * p + u + 1)
                    for swapped in range(2):
                        if j < 2:
                            wk = w(1024 + swapped * D + m * P, P)
                            sides = [(*wk, ctx_hi[:, half(u)], ctx_lo[:, half(u)])]
                        else:
                            sides = [(*w(swapped * 2 * D + k * D + m * P, P), h_hi_t[:, k, half(u)],
                                      h_lo_t[:, k, half(u)]) for k in range(KC)]
                        mm = product(pe, PS[:, bank + swapped, :], sides)
                    mm.then_inc(rp_mm, 1)

                def score(b, c, v, free):
                    w_ = 32 * a + 4 * b + 2 * c + v
                    if v == 0:
                        pe.wait_ge(km, 16 * a + 2 * b + c + 1)
                        pe.wait_ge(fix, 16 * a + 2 * b + c + 1)
                    if not free:
                        pe.wait_ge(at_mx, w_)
                    for g in range(2):
                        mm = pe.matmul(PS[:, g, :], q_fix[0:96, c, 2 * v + g, :],
                                       k_msk[c][0:96, 2 * v + g].rearrange("p j t -> p (j t)"),
                                       start=True, stop=True)
                    mm.then_inc(lg_mm, 1)

                def score_t(b, c, v, free):
                    w_ = 32 * a + 4 * b + 2 * c + v
                    if v == 0:
                        pe.wait_ge(qm, 16 * a + 2 * b + c + 1)
                    if not free:
                        pe.wait_ge(at_exp, w_)
                    for g in range(2):
                        pe.matmul(PS[:, 2 + g, :], k_fix[0:96, c, 2 * v + g, :],
                                  q_msk[c][0:96, 2 * v + g].rearrange("p j t -> p (j t)"),
                                  start=True, stop=False)
                        if g == 0:
                            pe.wait_ge(at_dg, w_ + 1)
                        mm = pe.matmul(PS[:, 2 + g, :], minus_one,
                                       diag[:, 4 * g:4 * g + 4, :].rearrange("p h t -> p (h t)"),
                                       start=False, stop=True)
                    mm.then_inc(lt_mm, 1)

                def weigh(b, c, v, g, free):
                    w_ = 32 * a + 4 * b + 2 * c + v
                    if g == 0:
                        pe.wait_ge(at_exp, w_ + 1)
                        if v == 0:
                            pe.wait_ge(v_fx, 16 * a + 2 * b + c + 1)
                            if not free:
                                pe.wait_ge(o_ev, 16 * a + 2 * b + c - 1)
                    for j in range(4):
                        n = 2 * v + g
                        mm = pe.matmul(PS[32 * j:32 * j + 32, 4 + c, n * S:n * S + S],
                                       v_fix[:, 16 * c + 4 * n + j, :], pT[:, v, 4 * g + j, :],
                                       start=True, stop=True)
                    if g == 1:
                        mm.then_inc(at_av, 1)

                def o_back(b, c, free):
                    pe.wait_ge(o_ev, 16 * a + 2 * b + c + 1)
                    if not free:
                        pe.wait_ge(a_ok, 16 * a + 2 * b + c)
                    for n in range(GL):
                        tr = pe.transpose(PS[:, 6, n * P:n * P + P], o_feat[:, c, n * P:n * P + P], ident[:])
                    tr.then_inc(o_bk, 1)

                def out_turn(b, c, last=False):
                    pe.wait_ge(a_ok, 16 * a + 2 * b + c + 1)
                    if last:
                        pe.wait_ge(a_lo, 16 * a + 2 * b + c)
                    pe.transpose(PS[:, 7, c * P:c * P + P], a_tok[:, c, :], ident[:]).then_inc(at_z, 1)

                def batch(b, first):
                    for c in range(2):
                        for v in range(2):
                            i = 2 * c + v
                            score(b, c, v, first and i == 0)
                            if not first or i >= 1:
                                score_t(*behind(b, c, v, 1), first and i == 1)
                            if not first or i >= 2:
                                weigh(*behind(b, c, v, 2), 0, first)
                            if v == 1 and not first:
                                out_turn(b - 1, c)
                            if not first or i >= 2:
                                weigh(*behind(b, c, v, 2), 1, first)
                            if v == 0 and not first:
                                o_back(b - 1, c, False)

                def out(b, c):
                    o_back(b, c, False)
                    out_turn(b, c, True)

                pe.wait_ge(v_one, 2 * (a + 1))
                pe.wait_ge(rp_lo, 8 * (a + 1))
                batch(0, True)
                with pe.Fori(1, B) as b:
                    batch(b, False)
                score_t(B - 1, 1, 1, False)
                for g in range(2):
                    weigh(B - 1, 1, 0, g, False)
                out(B - 1, 0)
                for g in range(2):
                    weigh(B - 1, 1, 1, g, False)
                out(B - 1, 1)
                pe.wait_ge(a_hi, 16 * (a + 1))
                pe.wait_ge(a_lo, 16 * (a + 1))
                for u in range(2):
                    for m in range(KC):
                        mm = product(pe, PS[:, 2 * m + u, :],
                                     [(*w(1792 + k * D + m * P, P), h_hi_t[:, k, half(u)], h_lo_t[:, k, half(u)])
                                      for k in range(KC)])
                    mm.then_inc(op_mm, 1)

            def ffn(fi, p):
                n, cb = FFN_CHUNKS[fi], CHUNK_BASE[fi]
                ln_forward(p)
                ln_back(p)
                if FFN_ROUTED[fi]:
                    ri = 0 if fi == 0 else 1
                    for u in range(2):
                        pe.wait_ge(h_lo, 2 * p + u + 1)
                        for t in range(NT):
                            c = slice(u * H + t * P, u * H + t * P + P)
                            j = NT * u + t
                            mm = product(pe, PS[:, 0, j * E:(j + 1) * E],
                                         [(h_hi_t[:, k, c], h_lo_t[:, k, c], wr_hi[:, ri, k, :], wr_lo[:, ri, k, :])
                                          for k in range(KC)])
                    mm.then_inc(r_mm, 1)

                def ab_mm(c, s, u, free):
                    if u == 0:
                        pe.wait_ge(w13_lo, cb + c + 1)
                    if free:
                        pe.wait_ge(h_lo, 2 * p + u + 1)
                    else:
                        pe.wait_ge(gm, 2 * (cb + c) + u - 1)
                    for x in range(2):
                        mm = product(pe, PS[:, 4 + 2 * u + x, :],
                                     [(w_hi_t[:, s, o:o + P], w_lo_t[:, s, o:o + P], h_hi_t[:, k, half(u)],
                                       h_lo_t[:, k, half(u)]) for k in range(KC) for o in [x * D + k * P]])
                    mm.then_inc(ab, 1)

                def down(c, s, u, first, last):
                    if u == 0:
                        pe.wait_ge(w2_lo, cb + c + 1)
                    pe.wait_ge(g_lo, 2 * (cb + c) + u + 1)
                    for m in range(KC):
                        o = 2 * D + m * P
                        mm = product(pe, PS[:, 2 * m + u, :],
                                     [(w_hi_t[:, s, o:o + P], w_lo_t[:, s, o:o + P], g_hi_t[:, u, :], g_lo_t[:, u, :])],
                                     start=first, stop=last)
                    mm.then_inc(o_mm, 1)

                ab_mm(0, 0, 0, True)
                ab_mm(0, 0, 1, True)
                if FFN_ROUTED[fi]:
                    pe.wait_ge(cw_ok, 1 if fi == 0 else 2)
                    for j in range(2 * NT):
                        tr = pe.transpose(PS[0:E, 2 + j // 4, (j % 4) * P:(j % 4) * P + P], r_m[:, j, :], ident[:])
                    tr.then_inc(cw_tr, 1)
                    pe.wait_ge(cw_ev, 1 if fi == 0 else 2)
                def chunk(c, s, first):
                    for u in range(2):
                        ab_mm(c, s, u, False)
                        down(c - 1, 1 - s, u, first, False)

                chunk(1, 1, True)
                loop_end, tail = pairs(n)
                with pe.Fori(1, loop_end) as i:
                    chunk(2 * i, 0, False)
                    chunk(2 * i + 1, 1, False)
                for c in tail:
                    chunk(c, c % 2, False)
                for u in range(2):
                    down(n - 1, (n - 1) % 2, u, False, True)

            def gqa(p):
                ln_forward(p)
                ln_back(p)

                def head(g, s, first, last):
                    def w(off, n):
                        return l_hi_t[:, s, off:off + n], l_lo_t[:, s, off:off + n]

                    pe.wait_ge(lw_lo, g + 1)
                    if not first:
                        pe.wait_ge(l_olo, 2 * g)
                    for h in range(2):
                        for u in range(2):
                            if first:
                                pe.wait_ge(h_lo, 2 * p + 2)
                            product(pe, PS[:, 4 + 2 * h + u, :],
                                    [(*w(k * D + h * P, P), h_hi_t[:, k, half(u)], h_lo_t[:, k, half(u)])
                                     for k in range(KC)]).then_inc(lq_mm, 1)
                    for u in range(2):
                        pe.wait_ge(lq_lo, 4 * g + u + 1)
                        product(pe, PS[:, 4 + u, :],
                                [(*w(2 * D, P), ctx_hi[:, half(u)], ctx_lo[:, half(u)])]).then_inc(lk_mm, 1)
                    pe.wait_ge(lq_lo, 4 * g + 4)
                    for b in range(B):
                        c = slice(b * S, b * S + S)
                        mm = product(pe, PS[:, 6 + b // 4, (b % 4) * P:(b % 4) * P + P],
                                     [(ctx_hi[:, c], ctx_lo[:, c], *w(2 * D + P, P))])
                    mm.then_inc(lv_mm, 1)
                    pe.wait_ge(lk_lo, 2 * g + 2)
                    for u in range(2):
                        if u == 1:
                            pe.wait_ge(lv_ev, g + 1)
                        for b in range(4):
                            c = slice((4 * u + b) * S, (4 * u + b) * S + S)
                            for h in range(2):
                                o = (b % 2) * 256 + h * P
                                mm = product(pe, PS[:, 4 + 2 * u + b // 2, o:o + P],
                                             [(lq_hi_t[:, h, c], lq_lo_t[:, h, c], lk_hi_t[:, c], lk_lo_t[:, c])])
                        mm.then_inc(l_lg, 1)
                    for u in range(2):
                        pe.wait_ge(l_nrm, 2 * g + u + 1)
                        for b in range(4):
                            for h in range(2):
                                o = (b % 2) * 256 + h * P
                                tr = pe.transpose(PS[:, 4 + 2 * u + b // 2, o:o + P], ls_t[:, u, b, h, :], ident[:])
                        tr.then_inc(l_T, 1)
                    for u in range(2):
                        pe.wait_ge(l_pT, 2 * g + u + 1)
                        for b in range(4):
                            o = (b % 2) * 256
                            mm = pe.matmul(PS[:, 4 + 2 * u + b // 2, o:o + 256], lv_t[:, 4 * u + b, :],
                                           lp_t[:, u, b].rearrange("p h k -> p (h k)"), start=True, stop=True)
                        mm.then_inc(l_av, 1)
                    for u in range(2):
                        pe.wait_ge(l_olo, 2 * g + u + 1)
                        for m in range(KC):
                            mm = product(pe, PS[:, 2 * m + u, :],
                                         [(*w(2 * D + 2 * P + h * D + m * P, P), lo_hi_t[:, h, half(u)],
                                           lo_lo_t[:, h, half(u)]) for h in range(2)],
                                         start=first, stop=last)
                        mm.then_inc(l_out, 1)

                head(0, 0, True, False)
                head(1, 1, False, False)
                with pe.Fori(1, G2 // 2 - 1) as i:
                    head(2 * i, 0, False, False)
                    head(2 * i + 1, 1, False, False)
                head(G2 - 2, 0, False, False)
                head(G2 - 1, 1, False, True)

            for p, (kind, i) in enumerate(PHASES):
                if kind == "rope":
                    rope(i, p)
                elif kind == "ffn":
                    ffn(i, p)
                else:
                    gqa(p)

        @block.vector
        def _(dve):
            link_n = [0]

            def link(ins):
                link_n[0] += 1
                ins.then_inc(q_step, 1)
                dve.wait_ge(q_step, link_n[0])

            dve.memset(shared_c[:, 0, :], 1.0 / (TOPK + 1)).then_inc(s_dve0, 1)
            dve.memset(shared_c[:, 1, :], 1.0).then_inc(s_dve0, 1)
            dve.wait_ge(s_act0, 1)
            dve.tensor_tensor(ctx_lo[:], ctx_raw, f32(ctx_hi[:]),
                              ALU.subtract).then_inc(s_dve0, 1)
            dve.wait_ge(s_act0, 2)
            dve.tensor_tensor(wr_lo[:], wr_raw[:], f32(wr_hi[:]), ALU.subtract).then_inc(s_dve0, 1)
            dve.wait_ge(s_const, 7 * 16)
            link(dve.tensor_copy(mcol[:], mcol8[:]))
            ang_n = [0]

            def turn_step(ins):
                ang_n[0] += 1
                ins.then_inc(s_ang, 1)
                dve.wait_ge(s_ang, ang_n[0])

            ang = h_tok[:, 4:8, :].rearrange("p a b -> p (a b)")
            turn_step(dve.tensor_scalar(ang, cos_t[:], col[:, 0:1], None, ALU.mult))
            for dst, shift in ((sin_t, 0.0), (cos_t, 1.5707963267948966)):
                turn_step(dve.tensor_scalar(dst[:], ang, shift, None, ALU.add))
                turn_step(dve.tensor_scalar(turns, dst[:], TWO_PI_INV, ROUND, ALU.mult, ALU.add))
                turn_step(dve.tensor_scalar(turns, turns, ROUND, None, ALU.subtract))
                turn_step(dve.scalar_tensor_tensor(dst[:], turns, -PI_HI, dst[:], ALU.mult, ALU.add))
                turn_step(dve.scalar_tensor_tensor(dst[:], turns, -PI_LO, dst[:], ALU.mult, ALU.add))
                turn_step(dve.tensor_scalar(dst[:], dst[:], 3.1415925, -3.1415925, ALU.min, ALU.max))
            dve.wait_ge(s_sin, 2)
            link(dve.tensor_scalar(sin_t[:], sin_t[:], col[:, 1:2], None, ALU.mult))

            quantised = []

            def quantise(v, n, done):
                ta, tb = tmp_a[:, 0:n], tmp_b[:, 0:n]
                nb = n // 32
                am, sc, rc = amax[:, 0:nb], scl[:, 0:nb], rscl[:, 0:nb]
                blocks = ta.rearrange("p (n c) -> p n c", c=32)
                if quantised:
                    dve.wait_ge(*quantised[-1])
                link(dve.transpose(ta, v))
                link(dve.tensor_reduce(am, blocks, AX_X, ALU.max, apply_absolute_value=True))
                link(dve.tensor_scalar(sc, am, 1.0 / 448.0, 1e-30, ALU.mult, ALU.max))
                link(dve.reciprocal(rc, sc))
                link(dve.tensor_tensor(blocks, blocks, rc.unsqueeze(2).to_broadcast([P, nb, 32]), ALU.mult))
                link(dve.tensor_scalar(tb.bitcast(I32), ta.bitcast(I32), 0x7F800000, None, ALU.bitwise_and))
                link(dve.tensor_scalar(tb, tb, 2.0 ** -6, FP8_ROUND, ALU.max, ALU.mult))
                link(dve.tensor_tensor(ta, ta, tb, ALU.add))
                link(dve.tensor_tensor(ta, ta, tb, ALU.subtract))
                link(dve.tensor_tensor(blocks, blocks, sc.unsqueeze(2).to_broadcast([P, nb, 32]), ALU.mult))
                dve.transpose(v, ta).then_inc(done, 1)
                quantised.append((done, 1 + sum(q[0] is done for q in quantised)))

            def layernorm(p, mx, between=None):
                for u in range(2):
                    n = 2 * p + u
                    dve.wait_ge(ln_xT, n + 1)
                    for t in range(NT):
                        s = dve.bn_stats(st6[:, t, :], PS[:, 4 + 2 * u + t // 2, (t % 2) * D:(t % 2) * D + D])
                    s.then_inc(ln_st, 1)
                    dve.wait_ge(ln_st, n + 1)
                    for t in range(NT):
                        s = dve.bn_aggr(mv[:, NT * u + t, :], st6[:, t, :])
                    s.then_inc(ln_mv, 1)
                    dve.wait_ge(ln_sd, n + 1)
                    dve.reciprocal(rstd[:, NT * u:NT * u + NT], sd[:, NT * u:NT * u + NT]).then_inc(ln_rs, 1)
                    dve.wait_ge(ln_rs, n + 1)
                    for t in range(NT):
                        j = NT * u + t
                        s = dve.tensor_scalar(h_tok[:, j, :],
                                              PS[:, 4 + 2 * u + t // 2, (t % 2) * D:(t % 2) * D + D],
                                              mv[:, j, 0:1], rstd[:, j:j + 1], ALU.subtract, ALU.mult)
                    s.then_inc(ln_h, 1)
                if between:
                    between()
                for u in range(2):
                    n = 2 * p + u
                    if mx:
                        dve.wait_ge(h_f32, u + 1)
                        quantise(cw_t[:, u, :], KC * H, h_q)
                        dve.wait_ge(h_hi, n + 1)
                        src = h_q_t[u]
                    else:
                        dve.wait_ge(h_hi, n + 1)
                        src = PS[:, 4 + 2 * u:6 + 2 * u, :]
                    dve.tensor_tensor(h_lo_t[:, :, half(u)], src, f32(h_hi_t[:, :, half(u)]),
                                      ALU.subtract).then_inc(h_lo, 1)

            def rope(a, p):
                def w_rest():
                    dve.wait_ge(rw_hi, a + 1)
                    dve.tensor_tensor(rw_lo_t, rw_raw, f32(rw_hi_t), ALU.subtract).then_inc(rw_lo, 1)

                layernorm(p, False, w_rest)

                def rot_rest(t):
                    dve.wait_ge(rp_hi, 8 * a + t + 1)
                    dve.tensor_tensor(rot[:, t % 4, 1, :], rot_a[:, t % 2, :], f32(rot[:, t % 4, 0, :]),
                                      ALU.subtract).then_inc(rp_lo, 1)

                for t in range(8):
                    u, bank = t // 4, 2 * (t % 2)
                    dve.wait_ge(rp_mm, 8 * a + t + 1)
                    if t >= 2:
                        dve.wait_ge(rp_lo, 8 * a + t - 1)
                    dve.tensor_tensor(rot_a[:, t % 2, :], PS[:, bank, :], cos_t[:, half(u)], ALU.mult)
                    dve.tensor_tensor(rot_b[:, t % 2, :], PS[:, bank + 1, :], sin_t[:, half(u)],
                                      ALU.mult).then_inc(rp_mul, 1)
                    if t:
                        rot_rest(t - 1)
                rot_rest(7)

                def o_norm(b, c):
                    un = 16 * a + 2 * b + c
                    o = PS[:, 6, :].rearrange("p (h d) -> p h d", h=16)
                    dve.wait_ge(o_bk, un + 1)
                    dve.reciprocal(o_rcp[:, c, :], o[:, :, 8]).then_inc(o_rc, 1)
                    dve.wait_ge(o_rc, un + 1)
                    dve.tensor_tensor(a_tok[:, c, :].rearrange("p (h d) -> p h d", d=8), o[:, :, 0:8],
                                      o_rcp[:, c, :].unsqueeze(2).to_broadcast([P, 16, 8]),
                                      ALU.mult).then_inc(a_ok, 1)

                def attn_lo(b, c):
                    dve.wait_ge(a_hi, 16 * a + 2 * b + c + 1)
                    dve.tensor_tensor(h_lo_t[:, c, bass.ds(b * S, S)], PS[:, 7, c * P:c * P + P],
                                      f32(h_hi_t[:, c, bass.ds(b * S, S)]), ALU.subtract).then_inc(a_lo, 1)

                def batch(b, first):
                    for c in range(2):
                        for v in range(2):
                            i = 2 * c + v
                            w = 32 * a + 4 * b + i
                            dve.wait_ge(lg_mm, w + 1)
                            dve.tensor_reduce(row_max[:, v, :],
                                              PS[:, 0:2, :].rearrange("p a (h t) -> p (a h) t", t=S),
                                              AX_X, ALU.max).then_inc(at_mx, 1)
                            if v == 1 and not first:
                                o_norm(b - 1, c)
                            dve.wait_ge(at_mx, w + 1)
                            if not first or i >= 1:
                                dve.wait_ge(lt_mm, w)
                            dve.tensor_tensor(diag, ident[:].unsqueeze(1).to_broadcast([P, 8, P]),
                                              row_max[:, v, :].unsqueeze(2).to_broadcast([P, 8, P]),
                                              ALU.mult).then_inc(at_dg, 1)
                            if v == 1 and not first:
                                attn_lo(b - 1, c)

                batch(0, True)
                with dve.Fori(1, B) as b:
                    batch(b, False)
                for c in range(2):
                    o_norm(B - 1, c)
                    attn_lo(B - 1, c)
                for u in range(2):
                    dve.wait_ge(op_mm, 2 * a + u + 1)
                    for m in range(KC):
                        s = dve.scalar_tensor_tensor(X[:, m, half(u)], PS[:, 2 * m + u, :], bias_o[:, a, m:m + 1],
                                                     X[:, m, half(u)], ALU.add, ALU.add)
                    s.then_inc(x_out, 1)

            def select_top(vals, e, k, sel, gt, eq):
                shape = [P, 2 * NT, e, e]
                gt = gt[:, 0:2 * NT * e * e].rearrange("p (n i j) -> p n i j", i=e, j=e)
                eq = eq[:, 0:2 * NT * e * e].rearrange("p (n i j) -> p n i j", i=e, j=e)
                vj, vi = vals.unsqueeze(2).to_broadcast(shape), vals.unsqueeze(3).to_broadcast(shape)
                link(dve.tensor_tensor(gt, vj, vi, ALU.is_gt))
                link(dve.tensor_tensor(eq, vj, vi, ALU.is_equal))
                link(dve.tensor_tensor(eq, eq, tri[:, 0:e, 0:e].unsqueeze(1).to_broadcast(shape), ALU.mult))
                link(dve.tensor_tensor(gt, gt, eq, ALU.add))
                link(dve.tensor_reduce(sel, gt, AX_X, ALU.add))
                link(dve.tensor_scalar(sel, sel, float(k), None, ALU.is_lt))

            def route(fi):
                logits = PS[:, 0, 0:2 * NT * E].rearrange("p (n e) -> p n e", e=E)
                shape = [P, 2 * NT, E]
                dve.wait_ge(r_mm, 1 if fi == 0 else 2)
                if fi == 0:
                    link(dve.tensor_reduce(r_s, logits, AX_X, ALU.max))
                    dve.tensor_tensor(r_lg, logits, r_s.unsqueeze(2).to_broadcast(shape),
                                      ALU.subtract).then_inc(r_sub, 1)
                    dve.wait_ge(r_act, 1)
                    select_top(r_ex, E, TOPK, r_sel, cmp_a, cmp_b)
                    gain = TOPK / (TOPK + 1.0)
                else:
                    dve.wait_ge(r_act, 2)
                    link(dve.tensor_reduce(r_g, r_ex.rearrange("p n (g e) -> p n g e", g=4), AX_X, ALU.max))
                    select_top(r_g, 4, 2, r_gs, cmp_a, cmp_b)
                    link(dve.tensor_tensor(r_m.rearrange("p n (g e) -> p n g e", g=4),
                                           r_ex.rearrange("p n (g e) -> p n g e", g=4),
                                           r_gs.unsqueeze(3).to_broadcast([P, 2 * NT, 4, 4]), ALU.mult))
                    select_top(r_m, E, TOPK, r_sel, cmp_a, cmp_b)
                    gain = 1.0
                link(dve.tensor_tensor(r_m, r_ex, r_sel, ALU.mult))
                link(dve.tensor_reduce(r_s, r_m, AX_X, ALU.add))
                link(dve.reciprocal(r_r, r_s))
                link(dve.tensor_scalar(r_r, r_r, gain, None, ALU.mult))
                dve.tensor_tensor(r_m, r_m, r_r.unsqueeze(2).to_broadcast(shape), ALU.mult).then_inc(cw_ok, 1)

            def ffn(fi, p):
                n, cb = FFN_CHUNKS[fi], CHUNK_BASE[fi]
                routed, mx = FFN_ROUTED[fi], FFN_MX[fi]
                if mx:
                    dve.wait_ge(x_out, 2 * p)

                def w_quant(c, s, i):
                    dve.wait_ge(w13_in[s], 16 * (cb // 2 + i + 1))
                    dve.wait_ge(w2_in[s], 16 * (cb // 2 + i + 1))
                    quantise(w_raw[:, s, :], FW, w_q)

                def gate(c, u, free):
                    m = 2 * (cb + c) + u
                    dve.wait_ge(sil, m + 1)
                    if not free:
                        dve.wait_ge(g_lo, m - 1)
                    dve.tensor_tensor(g_t[:, u, :], sil_t[:, u, :], PS[:, 5 + 2 * u, :], ALU.mult).then_inc(gm, 1)
                    if mx:
                        dve.wait_ge(gm, m + 1)
                        quantise(g_t[:, u, :], H, g_q)

                def g_rest(c, u):
                    dve.wait_ge(g_hi, 2 * (cb + c) + u + 1)
                    dve.tensor_tensor(g_lo_t[:, u, :], g_t[:, u, :], f32(g_hi_t[:, u, :]),
                                      ALU.subtract).then_inc(g_lo, 1)

                if mx:
                    w_quant(0, 0, 0)
                layernorm(p, mx)
                if routed:
                    route(fi)
                if mx:
                    for c in range(n):
                        if c + 1 < n:
                            w_quant(c + 1, (c + 1) % 2, (c + 1) // 2)
                        gate(c, 0, c == 0)
                        if c:
                            g_rest(c - 1, 1)
                        gate(c, 1, c == 0)
                        g_rest(c, 0)
                    g_rest(n - 1, 1)
                else:
                    gate(0, 0, True)
                    gate(0, 1, True)
                    g_rest(0, 0)

                    def chunk(c):
                        gate(c, 0, False)
                        g_rest(c - 1, 1)
                        gate(c, 1, False)
                        g_rest(c, 0)

                    chunk(1)
                    loop_end, tail = pairs(n)
                    with dve.Fori(1, loop_end) as i:
                        chunk(2 * i)
                        chunk(2 * i + 1)
                    for c in tail:
                        chunk(c)
                    g_rest(n - 1, 1)
                for u in range(2):
                    dve.wait_ge(o_mm, 2 * (cb + n) - 1 + u)
                    for m in range(KC):
                        s = dve.tensor_tensor(X[:, m, half(u)], PS[:, 2 * m + u, :], X[:, m, half(u)], ALU.add)
                    s.then_inc(x_out, 1)

            def gqa(p):
                dve.wait_ge(l_mk, 16)
                link(dve.tensor_scalar(mbias.rearrange("p b k -> p (b k)"), mask8, MASKED, -MASKED,
                                       ALU.mult, ALU.add))
                layernorm(p, False)

                def head(g):
                    for h in range(2):
                        for u in range(2):
                            dve.wait_ge(lq_hi, 4 * g + 2 * h + u + 1)
                            dve.tensor_tensor(lq_lo_t[:, h, half(u)], PS[:, 4 + 2 * h + u, :],
                                              f32(lq_hi_t[:, h, half(u)]), ALU.subtract).then_inc(lq_lo, 1)
                    for u in range(2):
                        dve.wait_ge(lk_hi, 2 * g + u + 1)
                        dve.tensor_tensor(lk_lo_t[:, half(u)], PS[:, 4 + u, :], f32(lk_hi_t[:, half(u)]),
                                          ALU.subtract).then_inc(lk_lo, 1)
                    dve.wait_ge(lv_mm, g + 1)
                    dve.tensor_tensor(lv_t, PS[:, 6:8, :].rearrange("p a (b d) -> p (a b) d", d=D2),
                                      mcol[:].unsqueeze(2).to_broadcast([P, B, D2]), ALU.mult).then_inc(lv_ev, 1)
                    for u in range(2):
                        n = 2 * g + u
                        dve.wait_ge(l_lg, n + 1)
                        s = ls_t[:, u].rearrange("p b h k -> p (b h) k")
                        dve.tensor_tensor(
                            ls_t[:, u], PS[:, 4 + 2 * u:6 + 2 * u, :].rearrange("p a (b h k) -> p (a b) h k", b=2, h=2),
                            mbias[:, 4 * u:4 * u + 4, :].unsqueeze(2).to_broadcast([P, 4, 2, S]),
                            ALU.add).then_inc(l_add, 1)
                        dve.wait_ge(l_add, n + 1)
                        dve.tensor_reduce(l_mx[:, u, :], s, AX_X, ALU.max).then_inc(l_max, 1)
                        dve.wait_ge(l_max, n + 1)
                        dve.tensor_tensor(s, s, l_mx[:, u, :].unsqueeze(2).to_broadcast([P, 8, S]),
                                          ALU.subtract).then_inc(l_sub, 1)
                    for u in range(2):
                        n = 2 * g + u
                        dve.wait_ge(l_exp, n + 1)
                        dve.tensor_reduce(l_sm[:, u, :], ls_t[:, u].rearrange("p b h k -> p (b h) k"), AX_X,
                                          ALU.add).then_inc(l_sum, 1)
                        dve.wait_ge(l_sum, n + 1)
                        dve.reciprocal(l_rc[:, u, :], l_sm[:, u, :]).then_inc(l_rcp, 1)
                    for u in range(2):
                        dve.wait_ge(l_ohi, 2 * g + u + 1)
                        dve.tensor_tensor(
                            lo_lo_t[:, :, half(u)].rearrange("p h (b t) -> p b h t", b=4),
                            PS[:, 4 + 2 * u:6 + 2 * u, :].rearrange("p a (b h t) -> p (a b) h t", b=2, h=2),
                            f32(lo_hi_t[:, :, half(u)]).rearrange("p h (b t) -> p b h t", b=4),
                            ALU.subtract).then_inc(l_olo, 1)

                head(0)
                head(1)
                with dve.Fori(1, 4) as i:
                    head(2 * i)
                    head(2 * i + 1)
                for u in range(2):
                    dve.wait_ge(l_out, 15 + u)
                    for m in range(KC):
                        s = dve.tensor_tensor(X[:, m, half(u)], PS[:, 2 * m + u, :], X[:, m, half(u)], ALU.add)
                    s.then_inc(x_out, 1)

            for p, (kind, i) in enumerate(PHASES):
                if kind == "rope":
                    rope(i, p)
                elif kind == "ffn":
                    ffn(i, p)
                else:
                    gqa(p)


def laid_out(i):
    import numpy as np

    f4 = np.float32
    n = {k: np.asarray(v) for k, v in i.items()}

    def chunks(w):
        return w.reshape(-1, P, w.shape[1]).transpose(1, 0, 2)

    def packed(w1, w3, w2):
        c = w1.shape[1] // P
        a, b = (chunks(w).reshape(P, KC, c, P).transpose(2, 0, 1, 3).reshape(c, P, D) for w in (w1, w3))
        return np.ascontiguousarray(np.concatenate([a, b, w2.reshape(c, P, D)], 2))

    def padded(w, axis):
        pad = [(0, 0), (0, 0)]
        pad[axis] = (0, -w.shape[axis] % P)
        return np.pad(w, pad)

    swap = np.arange(D) ^ 1
    rope = []
    for l in (0, 2, 3):
        q, kv, o = n[f"L{l}_xattn_Wq"], n[f"L{l}_xattn_Wkv"], n[f"L{l}_xattn_Wout"]
        rope.append(np.concatenate([chunks(q).reshape(P, -1), chunks(q[:, swap]).reshape(P, -1), kv[:, :D],
                                    kv[:, :D][:, swap], kv[:, D:], chunks(o).reshape(P, -1)], 1))
    w0 = packed(np.concatenate([n["L0_ffn_we1"].transpose(1, 0, 2).reshape(D, -1), n["L0_ffn_ws1"]], 1),
                np.concatenate([n["L0_ffn_we3"].transpose(1, 0, 2).reshape(D, -1), n["L0_ffn_ws3"]], 1),
                np.concatenate([n["L0_ffn_we2"].reshape(-1, D), n["L0_ffn_ws2"]], 0))
    w1 = packed(n["L1_ffn_gate_w"].T, n["L1_ffn_up_w"].T, n["L1_ffn_down_w"].T)
    w2 = packed(n["L2_ffn_w_gate"].T, n["L2_ffn_w_up"].T, n["L2_ffn_w_down"].T)
    w3 = packed(padded(np.concatenate([n["L3_ffn_W1"].reshape(-1, D), n["L3_ffn_Ws1"]], 0).T, 1),
                padded(np.concatenate([n["L3_ffn_W3"].reshape(-1, D), n["L3_ffn_Ws3"]], 0).T, 1),
                padded(np.concatenate([n["L3_ffn_W2"].transpose(0, 2, 1).reshape(-1, D), n["L3_ffn_Ws2"].T], 0), 0))
    gqa = []
    for g in range(G2):
        q = n["L1_xattn_Wq"][:, g * D:(g + 1) * D]
        k, v = (n[f"L1_xattn_{x}"][:, g * D2:(g + 1) * D2] for x in ("Wk", "Wv"))
        gqa.append(np.concatenate([chunks(q).reshape(P, -1), k, v,
                                   chunks(n["L1_xattn_Wo"][g * D:(g + 1) * D]).reshape(P, -1)], 1))
    p = np.arange(P)
    cols = np.zeros((P, 8), f4)
    cols[:, 0] = np.where((p % 4) // 2 == 0, 1.0, 10000.0 ** -0.5)
    cols[:, 1] = np.where(p % 2 == 0, -1.0, 1.0)
    for j in range(4):
        cols[:, 2 + j] = (p % 32) // HD == j
    cols[:, 6] = LN_EPS
    tri = np.tile(np.tril(np.ones((E, E), f4), -1).reshape(1, -1), (P, 1))
    pos = n["fside_BxSx2_0"].reshape(T, 2).T
    mask = n["mask_BxS2_bf1"].view(np.uint8)
    return dict(
        x_t=n["x"].reshape(T, D).T, ctx_t=n["ctx_1024"].reshape(T, P).T,
        pos_rows=pos[(p % HD) // 4], mask_row=mask.reshape(1, T), mask_col=mask.T,
        rope_w=np.stack(rope), rope_b=np.stack([n[f"L{l}_xattn_bout"].reshape(KC, P).T for l in (0, 2, 3)]),
        router_w=np.stack([chunks(n["L0_ffn_w_router"]), chunks(n["L3_ffn_gate_w"].T)]),
        ffn_w0=w0, ffn_w1=w1, ffn_w2=w2, ffn_w3=w3, gqa_w=np.stack(gqa),
        cols=cols, ident_in=np.eye(P, dtype=f4), tri_in=tri)


def kernel(**inputs):
    import numpy as np
    import concourse.bacc as bacc
    from concourse.bass_utils import run_bass_kernel_spmd

    nc = bacc.Bacc("TRN2", target_bir_lowering=False, num_devices=1)
    arrays = {f"in_{k}": np.ascontiguousarray(v) for k, v in laid_out(inputs).items()}
    args = [nc.dram_tensor(k, v.shape, mybir.dt.from_np(v.dtype), kind="ExternalInput").ap()
            for k, v in arrays.items()]
    args.append(nc.dram_tensor("out_t", (D, T), F32, kind="ExternalOutput").ap())
    build(nc, *args)
    r = run_bass_kernel_spmd(nc, [arrays], core_ids=[0])
    return np.ascontiguousarray(r.results[0]["out_t"].T).reshape(B, S, D)
```

```python
from contextlib import ExitStack

import concourse.bass as bass
from concourse import mybir

F32 = mybir.dt.float32
F32R = mybir.dt.float32r
I32 = mybir.dt.int32
U8 = mybir.dt.uint8
ALU = mybir.AluOpType
ACT = mybir.ActivationFunctionType
AX_X = mybir.AxisListType.X

P = 128
B, S, D = 8, 128, 256
T = B * S
H = T // 2
KC = D // P
NT = H // P
Q_ACT = 2
HEADS, HD = 32, 8
GL = 4
E = 16
TOPK = 4
G2, D2 = 8, 128
LN_EPS = 1e-5
RW = 2304
FW = 3 * D
LK = 2 * D + P
LQ = LK + P
LW = LQ + 2 * D
MASKED = 1e30
TWO_PI_INV = 0.15915494309189535
PI_HI, PI_LO = 6.28125, 0.0019353071795864769
ROUND = 12582912.0
FP8_ROUND = 1.5 * 2.0 ** 20

FFN_CHUNKS = [20, 8, 8, 25]
FFN_ROUTED = [True, False, False, True]
FFN_MX = [False, True, False, False]
CHUNK_BASE = [0, 20, 28, 36]
ROUTED_BASE = {0: 0, 3: 20}
ROW_BLOCK = 16
ROWS_PER_EXPERT = {0: 8, 3: 11}
SHARED_ROWS = {0: 32, 3: 22}


def build(nc, x_t, ctx_t, pos_rows, mask_row, mask_col, rope_w, rope_b, router_w, ffn_w0, ffn_w1,
          ffn_w2, ffn_w3, gqa_w, cols, ident_in, tri_in, out, n_phases=8):
    ffn_w = [ffn_w0, ffn_w1, ffn_w2, ffn_w3]
    PHASES = [("rope", 0), ("ffn", 0), ("gqa", 0), ("ffn", 1), ("rope", 1), ("ffn", 2), ("rope", 2),
              ("ffn", 3)][:n_phases]

    with ExitStack() as ctx:
        def sb(name, shape, dt=F32):
            return ctx.enter_context(nc.sbuf_tensor(name, shape, dt))

        def sem(name):
            return ctx.enter_context(nc.semaphore(name))

        def f32(ap):
            return ap.bitcast(F32)

        PS = ctx.enter_context(nc.psum_tensor("PS", [P, 8, 512], F32))
        cw_rows = {f: nc.dram_tensor(f"cw_rows{f}", [FFN_CHUNKS[f] * 8, T], F32, kind="Internal").ap()
                   for f in (0, 3)}
        cw_tab = {f: nc.dram_tensor(f"cw_tab{f}", [E, T], F32, kind="Internal").ap() for f in (0, 3)}
        turned = nc.dram_tensor("turned", [8, P, 2, H], F32, kind="Internal").ap()

        X = sb("X", [P, KC, T])
        h_hi_t = sb("h_hi_t", [P, KC, T], F32R)
        h_lo_t = sb("h_lo_t", [P, KC, T], F32R)
        h_tok = sb("h_tok", [P, 2 * NT, D])
        ctx_hi = sb("ctx_hi", [P, T], F32R)
        ctx_lo = sb("ctx_lo", [P, T], F32R)
        cos_t = sb("cos_t", [P, T])
        sin_t = sb("sin_t", [P, T])
        ident = sb("ident", [P, P])
        tri = sb("tri", [P, E, E])
        col = sb("col", [P, 8])
        bias_o = sb("bias_o", [P, 3, KC])
        wr_raw = sb("wr_raw", [P, 2, KC, E])
        wr_hi = sb("wr_hi", [P, 2, KC, E], F32R)
        wr_lo = sb("wr_lo", [P, 2, KC, E], F32R)
        st6 = sb("st6", [P, NT, 6])
        mv = sb("mv", [P, 2 * NT, 2])
        sd = sb("sd", [P, 2 * NT])
        rstd = sb("rstd", [P, 2 * NT])
        mcol8 = sb("mcol8", [P, B], U8)
        mcol = sb("mcol", [P, B])
        ctx_raw = h_tok[:, 0:4, :].rearrange("p a b -> p (a b)")
        shared_c = sb("shared_c", [32, 2, 64])

        RSZ = 2 * RW + 2 * 512 + 4 * 2048
        FSZ = 25984
        AR = sb("AR", [P, RSZ], F32R)
        AF = sb("AF", [P, FSZ])

        def carve(arena):
            at = [0]

            def take(n):
                a = arena[:, at[0]:at[0] + n]
                at[0] += n
                return a
            return take

        r = carve(AR)
        k_msk, q_msk = ([r(2048).rearrange("p (g j t) -> p g j t", g=GL, j=4) for _ in range(2)] for _ in range(2))
        q_fix = r(2 * 512).rearrange("p (c g t) -> p c g t", c=2, g=GL)
        rw_hi_t, rw_lo_t = r(RW), r(RW)
        k_fix = rw_hi_t[:, 0:1024].rearrange("p (c g t) -> p c g t", c=2, g=GL)
        minus_one = rw_hi_t[:, 1024:1024 + P]
        diag = rw_lo_t[:, 0:1024].rearrange("p (h t) -> p h t", h=8)
        f = carve(AF)
        pT_or_rot = f(2048)
        pT = pT_or_rot[:, 0:2048].rearrange("p (v h t) -> p v h t", v=2, h=8)
        rot_a = pT_or_rot[:, 0:1024].rearrange("p (s t) -> p s t", s=2)
        rot_b = pT_or_rot[:, 1024:2048].rearrange("p (s t) -> p s t", s=2)
        K_all = f(8 * T).rearrange("p (g t) -> p g t", g=8)
        Q_all = f(8 * T).rearrange("p (g t) -> p g t", g=8)
        rw_raw = Q_all[:, 4:7, :].rearrange("p g t -> p (g t)")[:, 0:RW]
        turns = K_all[:, 0, :]
        rot = f(4 * T).bitcast(F32R).rearrange("p (n s t) -> p n s t", n=4, s=2)
        v_all = h_tok[:].rearrange("p a n -> p (a n)").rearrange("p (b h d) -> p b h d", b=B, h=HEADS)
        v_fix = f(HEADS * 32).rearrange("p (h d) -> p h d", h=HEADS)
        o_feat = f(2 * 512).rearrange("p (c n) -> p c n", c=2)
        a_tok = f(2 * P).rearrange("p (c d) -> p c d", c=2)
        row_max = f(2 * 8).rearrange("p (s h) -> p s h", s=2)
        o_rcp = f(2 * 16).rearrange("p (c h) -> p c h", c=2)
        r = carve(AR)
        w_hi_t = r(2 * FW).rearrange("p (s n) -> p s n", s=2)
        w_lo_t = r(2 * FW).rearrange("p (s n) -> p s n", s=2)
        g_hi_t = r(2 * H).rearrange("p (u t) -> p u t", u=2)
        g_lo_t = r(2 * H).rearrange("p (u t) -> p u t", u=2)
        f = carve(AF)
        w_raw = f(2 * FW).rearrange("p (s n) -> p s n", s=2)
        cw_t = f(2 * T).rearrange("p (s t) -> p s t", s=2)
        sil_t = f(2 * H).rearrange("p (u t) -> p u t", u=2)
        g_t = f(2 * H).rearrange("p (u t) -> p u t", u=2)
        tmp_ab = f(2048)
        tmp_a, tmp_b = tmp_ab[:, 0:1024], tmp_ab[:, 1024:2048]
        qs = f(2 * 3 * 32).rearrange("p (s i n) -> p s i n", s=2, i=3)
        r_T = f(P)
        r_lgT = f(T)
        r_lg = f(2 * NT * E).rearrange("p (n e) -> p n e", e=E)
        r_ex = f(2 * NT * E).rearrange("p (n e) -> p n e", e=E)
        r_sel = f(2 * NT * E).rearrange("p (n e) -> p n e", e=E)
        r_m = f(2 * NT * E).rearrange("p (n e) -> p n e", e=E)
        r_g = f(2 * NT * 4).rearrange("p (n e) -> p n e", e=4)
        r_gs = f(2 * NT * 4).rearrange("p (n e) -> p n e", e=4)
        r_s = f(2 * NT)
        r_r = f(2 * NT)
        qg_a = f(2 * H).rearrange("p (u t) -> p u t", u=2)
        qg_b = f(2 * H).rearrange("p (u t) -> p u t", u=2)
        cmp_a = f(2048)
        cmp_b = tmp_ab
        hq_tmp = [(tmp_a, tmp_b), tuple(q.rearrange("p u t -> p (u t)") for q in (qg_a, qg_b))]
        h_q_t = [cw_t[:, u, :].rearrange("p (k t) -> p k t", k=KC) for u in range(2)]
        r = carve(AR)
        l_hi_t = r(2 * LW).rearrange("p (s n) -> p s n", s=2)
        l_lo_t = r(2 * LW).rearrange("p (s n) -> p s n", s=2)
        lo_hi_t = r(2 * T).rearrange("p (h t) -> p h t", h=2)
        lo_lo_t = r(2 * T).rearrange("p (h t) -> p h t", h=2)
        f = carve(AF)
        l_raw = f(2 * LW).rearrange("p (s n) -> p s n", s=2)
        lq_t = f(2 * T).rearrange("p (h t) -> p h t", h=2)
        lk_t = f(T)
        lv_w = f(2 * P).rearrange("p (s n) -> p s n", s=2)
        ctx_t32 = f(T)
        lv_t = f(2 * T).rearrange("p (s b d) -> p s b d", s=2, b=B)
        ls_t = f(2 * T).rearrange("p (u b h k) -> p u b h k", u=2, b=4, h=2)
        lp_t = f(2 * T).rearrange("p (u b h k) -> p u b h k", u=2, b=4, h=2)
        l_mx = f(16).rearrange("p (u b) -> p u b", u=2)
        l_sm = f(16).rearrange("p (u b) -> p u b", u=2)
        l_rc = f(16).rearrange("p (u b) -> p u b", u=2)
        mask8 = f(T // 4).bitcast(U8)
        mbias = f(T).rearrange("p (b k) -> p b k", b=B)
        qw_in = f(2 * FW).rearrange("p (s n) -> p s n", s=2)
        qw_a = f(2 * FW).rearrange("p (s n) -> p s n", s=2)
        qw_b = f(2 * FW).rearrange("p (s n) -> p s n", s=2)
        qw_s = f(2 * 3 * 32).rearrange("p (s i n) -> p s i n", s=2, i=3)
        qw = AF[:, FSZ - 8 * FW:FSZ].rearrange("p (c n) -> p c n", c=8)

        s_const, s_x, s_ctx = sem("s_const"), sem("s_x"), sem("s_ctx")
        s_act0, s_dve0 = sem("s_act0"), sem("s_dve0")
        s_sin, s_ang = sem("s_sin"), sem("s_ang")
        x_out = sem("x_out")
        ln_xT, ln_st, ln_mv, ln_sd, ln_rs, ln_h, ln_hT = (
            sem(n) for n in ("ln_xT", "ln_st", "ln_mv", "ln_sd", "ln_rs", "ln_h", "ln_hT"))
        h_fr, h_2, h_rd = sem("h_fr"), sem("h_2"), sem("h_rd")
        h_f32, h_q, h_hi, h_lo = sem("h_f32"), sem("h_q"), sem("h_hi"), sem("h_lo")
        rw_in, rw_hi, rw_lo = sem("rw_in"), sem("rw_hi"), sem("rw_lo")
        v_one, v_mm, v_ev = sem("v_one"), sem("v_mm"), sem("v_ev")
        rp_mm, rp_mul, rp_add, rp_hi, rp_lo = (
            sem(n) for n in ("rp_mm", "rp_mul", "rp_add", "rp_hi", "rp_lo"))
        rp_wr, k_in, q_in = ([sem(f"{n}{i}") for i in range(2)] for n in ("rp_wr", "k_in", "q_in"))
        km, qm, fix, v_fx, lg_mm, lt_mm, at_mx, at_dg, at_exp, at_av = (
            sem(n) for n in ("km", "qm", "fix", "v_fx", "lg_mm", "lt_mm", "at_mx", "at_dg", "at_exp", "at_av"))
        o_ev, o_bk, o_rc, a_ok, at_z, a_hi, a_lo, op_mm = (
            sem(n) for n in ("o_ev", "o_bk", "o_rc", "a_ok", "at_z", "a_hi", "a_lo", "op_mm"))
        w13_in, w2_in = [sem("w13_in0"), sem("w13_in1")], [sem("w2_in0"), sem("w2_in1")]
        cw_in = [sem("cw_in0"), sem("cw_in1")]
        w13_hi, w13_lo, w2_hi, w2_lo = (sem(n) for n in ("w13_hi", "w13_lo", "w2_hi", "w2_lo"))
        ab, sil, gm, g_cw, g_q, g_hi, g_lo, o_mm = (
            sem(n) for n in ("ab", "sil", "gm", "g_cw", "g_q", "g_hi", "g_lo", "o_mm"))
        r_pr, r_ev = sem("r_pr"), sem("r_ev")
        r_mm, r_sub, r_act, cw_ok, cw_tb, cw_wr, cw_sh = (
            sem(n) for n in ("r_mm", "r_sub", "r_act", "cw_ok", "cw_tb", "cw_wr", "cw_sh"))
        q_step = sem("q_step")
        qw_ld, qw_1, qw_f, qw_2, qw_r, qw_ok = (
            [sem("qw_ld0"), sem("qw_ld1")], *(sem(n) for n in ("qw_1", "qw_f", "qw_2", "qw_r", "qw_ok")))
        qw_t = sem("qw_t")
        qg_f, qg_2, qg_r = sem("qg_f"), sem("qg_2"), sem("qg_r")
        lw_in = [sem("lw_in0"), sem("lw_in1")]
        lw_hi, lw_lo, lo_hi, lo_lo = (sem(n) for n in ("lw_hi", "lw_lo", "lo_hi", "lo_lo"))
        l_ctx, lq_mm, lq_ev, lk_mm, lk_ev, lv_mm, lv_ev = (
            sem(n) for n in ("l_ctx", "lq_mm", "lq_ev", "lk_mm", "lk_ev", "lv_mm", "lv_ev"))
        l_lg, l_add, l_max, l_sub, l_exp, l_sum, l_rcp, l_nrm, l_T, l_pT, l_av, l_ohi, l_olo, l_out = (
            sem(n) for n in ("l_lg", "l_add", "l_max", "l_sub", "l_exp", "l_sum", "l_rcp", "l_nrm", "l_T",
                             "l_pT", "l_av", "l_ohi", "l_olo", "l_out"))
        l_mk = sem("l_mk")
        s_out = sem("s_out")

        block = ctx.enter_context(nc.Block())

        def half(u):
            return slice(u * H, (u + 1) * H)

        def wait_x(eng, p, u):
            if p == 0:
                eng.wait_ge(s_x, 16)
            else:
                eng.wait_ge(x_out, 2 * (p - 1) + u + 1)

        def pairs(n):
            return n // 2 - (1 if n % 2 == 0 else 0), range(n - (2 - n % 2), n)

        def behind(b, c, v, lag):
            i = 2 * c + v - lag
            return (b if i >= 0 else b - 1), i % 4 // 2, i % 2

        def chain(eng, sem_, done=0):
            n = [0]

            def step(ins):
                n[0] += 1
                ins.then_inc(sem_, 1)
                eng.wait_ge(sem_, done + n[0])
            return step

        def scaled(v, sc):
            n = v.shape[-1] // 32
            return v.rearrange("p (n c) -> p n c", c=32), sc[:, 0:n].unsqueeze(2).to_broadcast([P, n, 32])

        def quant_front(dve, step, src, ta, tb, s):
            n = src.shape[-1] // 32
            am, sc, rc = s[:, 0, 0:n], s[:, 1, 0:n], s[:, 2, 0:n]
            step(dve.transpose(ta, src))
            step(dve.tensor_reduce(am, ta.rearrange("p (n c) -> p n c", c=32), AX_X, ALU.max,
                                   apply_absolute_value=True))
            step(dve.tensor_scalar(sc, am, 1.0 / 448.0, 1e-30, ALU.mult, ALU.max))
            step(dve.reciprocal(rc, sc))
            blocks, over = scaled(ta, s[:, 2])
            step(dve.tensor_tensor(blocks, blocks, over, ALU.mult))
            step(dve.tensor_scalar(tb.bitcast(I32), ta.bitcast(I32), 0x7F800000, None, ALU.bitwise_and))
            return dve.tensor_scalar(tb, tb, 2.0 ** -6, FP8_ROUND, ALU.max, ALU.mult)

        def quant_round(eng, step, ta, tb, s):
            step(eng.tensor_tensor(ta, ta, tb, ALU.add))
            step(eng.tensor_tensor(ta, ta, tb, ALU.subtract))
            blocks, over = scaled(ta, s[:, 1])
            return eng.tensor_tensor(blocks, blocks, over, ALU.mult)

        def product(pe, dst, sides, start=True, stop=True):
            for i, (wh, wl, mh, ml) in enumerate(sides):
                pe.matmul(dst, wh, mh, start=start and i == 0, stop=False)
                pe.matmul(dst, wh, ml, start=False, stop=False)
                last = pe.matmul(dst, wl, mh, start=False, stop=stop and i == len(sides) - 1)
            return last

        @block.sync
        def _(sp):
            sp.dma_start(X[:], x_t.rearrange("(k p) t -> p k t", p=P)).then_inc(s_x, 16)
            sp.dma_start(col[:], cols).then_inc(s_const, 16)
            sp.dma_start(cos_t[:], pos_rows).then_inc(s_const, 16)
            sp.dma_start(ident[:], ident_in).then_inc(s_const, 16)
            sp.dma_start(ctx_raw, ctx_t).then_inc(s_ctx, 16)
            sp.dma_start(tri[:], tri_in.rearrange("p (i j) -> p i j", i=E)).then_inc(s_const, 16)
            sp.dma_start(bias_o[:], rope_b.rearrange("l p k -> p l k")).then_inc(s_const, 16)
            sp.dma_start(wr_raw[:], router_w.rearrange("l p k e -> p l k e")).then_inc(s_const, 16)
            sp.dma_start(mcol8[:], mask_col).then_inc(s_const, 16)
            sp.wait_ge(s_dve0, 2)
            for i, fi, rows in ((0, 0, slice(0, 32)), (1, 3, slice(0, 22)), (1, 3, slice(198, 200))):
                n = rows.stop - rows.start
                sp.dma_start(cw_rows[fi][rows, :].rearrange("n (a c) -> n a c", c=64),
                             shared_c[0:n, i:i + 1, :].to_broadcast([n, T // 64, 64])).then_inc(cw_sh, 16)

            def rope_moves(a, p):
                if p > 0:
                    sp.wait_ge(x_out, 2 * (p - 1))
                sp.dma_start(rw_raw, rope_w[a]).then_inc(rw_in, 16)
                def write(t):
                    sp.wait_ge(rp_lo, 8 * a + t + 1)
                    sp.dma_start(turned[t], f32(rot[:, t % 4])).then_inc(rp_wr[t % 2], 16)

                def read(t):
                    u, j = t // 4, t % 4
                    dst, arrived, m = (K_all, Q_all)[j // 2], (k_in, q_in)[j // 2], j % 2
                    sp.wait_ge(rp_wr[t % 2], 16 * (4 * a + t // 2 + 1))
                    for s, part in enumerate((0, 0, 1) if j < 2 else (0, 1, 0)):
                        sp.dma_start(dst[32 * s:32 * s + 32, GL * m:GL * m + GL, half(u)],
                                     turned[t, :, part, :].rearrange("(g r) t -> r g t", g=GL)
                                     ).then_inc(arrived[u], 16)

                write(0)
                for t in range(1, 8):
                    write(t)
                    read(t - 1)
                read(7)

            def ffn_loads(fi, p):
                n, cb = FFN_CHUNKS[fi], CHUNK_BASE[fi] - (8 if fi > 1 else 0)
                routed, rb = FFN_ROUTED[fi], ROUTED_BASE.get(fi)
                sp.wait_ge(x_out, 2 * p)

                def w_load(c, s, first):
                    src = ffn_w[fi][c] if isinstance(c, int) else \
                        ffn_w[fi][bass.ds(c, 1)].rearrange("a p n -> (a p) n")
                    if not first:
                        sp.wait_ge(w13_lo, CHUNK_BASE[fi] + c - 1)
                    sp.dma_start(w_raw[:, s, 0:2 * D], src[:, 0:2 * D]).then_inc(w13_in[s], 16)
                    if not first:
                        sp.wait_ge(w2_lo, CHUNK_BASE[fi] + c - 1)
                    sp.dma_start(w_raw[:, s, 2 * D:FW], src[:, 2 * D:FW]).then_inc(w2_in[s], 16)

                def cw_load(c, s, src, first):
                    if not first:
                        sp.wait_ge(g_cw, 2 * (rb + c) - 2)
                    sp.dma_start(cw_t[:, s, :], src).then_inc(cw_in[s], 16)

                def cw_src(c):
                    v = cw_rows[fi].rearrange("(c r) t -> c r t", r=8)
                    v = v[c] if isinstance(c, int) else v[bass.ds(c, 1)].rearrange("a r t -> (a r) t")
                    return v.unsqueeze(1).to_broadcast([8, ROW_BLOCK, T])

                for c in range(2):
                    w_load(c, c, True)
                done = 2
                if routed:
                    sp.wait_ge(cw_sh, 48)
                    for c in range(2):
                        cw_load(c, c, cw_src(c), True)
                    done = 4
                    for c in range(2, 4):
                        w_load(c, c % 2, False)
                        if fi == 0:
                            cw_load(c, c % 2, cw_src(c), False)
                    k, e_rows, first = (0 if fi == 0 else 1), ROWS_PER_EXPERT[fi], SHARED_ROWS[fi]
                    sp.wait_ge(cw_ok, k + 1)
                    for a in range(4):
                        for n2 in range(2):
                            o = 32 * a + E * n2
                            sp.dma_start(cw_tab[fi].rearrange("e (y n a j) -> a n e y j", n=2, a=4, j=32)[a, n2],
                                         r_T[o:o + E, :].rearrange("p (y j) -> p y j", j=32)).then_inc(cw_tb, 16)
                    if fi == 0:
                        w_load(4, 0, False)
                    sp.wait_ge(cw_tb, 128 * (k + 1))
                    sp.dma_start(cw_rows[fi][first:first + E * e_rows, :].rearrange("(e r) t -> e r t", r=e_rows),
                                 cw_tab[fi].unsqueeze(1).to_broadcast([E, e_rows, T])).then_inc(cw_wr, 16)
                    sp.wait_ge(cw_wr, 16 * (k + 1))
                    if fi == 0:
                        done = 6
                        cw_load(4, 0, cw_src(4), False)
                        w_load(5, 1, False)
                        cw_load(5, 1, cw_src(5), False)
                    else:
                        for c in range(2, 4):
                            cw_load(c, c % 2, cw_src(c), False)
                loop_end, tail = pairs(n)
                with sp.Fori(done // 2, loop_end) as i:
                    for s in range(2):
                        w_load(2 * i + s, s, False)
                        if routed:
                            cw_load(2 * i + s, s, cw_src(2 * i + s), False)
                for c in tail:
                    w_load(c, c % 2, False)
                    if routed:
                        cw_load(c, c % 2, cw_src(c), False)

            def gqa_loads(p):
                sp.wait_ge(x_out, 2 * p)
                sp.dma_start(mask8, mask_row.to_broadcast([P, T])).then_inc(l_mk, 16)
                for g in range(2):
                    sp.dma_start(l_raw[:, g, :], gqa_w[g]).then_inc(lw_in[g], 16)
                    sp.dma_start(qw_in[:, g, :], ffn_w1[g]).then_inc(qw_ld[g], 16)
                with sp.Fori(1, 4) as i:
                    for s in range(2):
                        sp.wait_ge(lw_lo, 2 * i + s - 1)
                        sp.wait_ge(lo_lo, 2 * i + s - 1)
                        sp.dma_start(l_raw[:, s, :], gqa_w[bass.ds(2 * i + s, 1)]
                                     .rearrange("a p n -> (a p) n")).then_inc(lw_in[s], 16)
                        sp.wait_ge(qw_f, 2 * i + s - 1)
                        sp.dma_start(qw_in[:, s, :], ffn_w1[bass.ds(2 * i + s, 1)]
                                     .rearrange("a p n -> (a p) n")).then_inc(qw_ld[s], 16)

            for p, (kind, i) in enumerate(PHASES):
                if kind == "rope":
                    rope_moves(i, p)
                elif kind == "ffn" and not FFN_MX[i]:
                    ffn_loads(i, p)
                elif kind == "gqa":
                    gqa_loads(p)
            for u in range(2):
                sp.wait_ge(x_out, 2 * (len(PHASES) - 1) + u + 1)
                sp.dma_start(out.rearrange("(k p) t -> p k t", p=P)[:, :, half(u)],
                             X[:, :, half(u)]).then_inc(s_out, 16)
            sp.wait_ge(s_out, 32)
            sp.wait_ge(cw_sh, 48)

        @block.gpsimd
        def _(pool):
            def rope(a, p):
                if a > 0:
                    pool.wait_ge(x_out, 2 * p)
                pool.memset(v_fix[:, :, 9:32], 0.0)
                pool.memset(v_fix[:, :, 8:9], 1.0).then_inc(v_one, 1)
                for t in range(8):
                    pool.wait_ge(rp_mul, 8 * a + t + 1)
                    pool.tensor_tensor(rot_a[:, t % 2, :], rot_a[:, t % 2, :], rot_b[:, t % 2, :],
                                       ALU.add).then_inc(rp_add, 1)
                pool.tensor_scalar(minus_one, ident[:], 0.0, -1.0, ALU.mult, ALU.add).then_inc(v_one, 1)

                def masked(b, c, free, dst, src, mm, done, j):
                    if not free:
                        pool.wait_ge(mm, 2 * (16 * a + 2 * b + c - 1))
                    shape = [96, GL, 4 - j, S]
                    pool.tensor_tensor(dst[c][0:96, :, j:4],
                                       src[0:96, GL * c:GL * c + GL, bass.ds(b * S, S)]
                                       .unsqueeze(2).to_broadcast(shape),
                                       col[0:96, 2 + j:6].unsqueeze(1).unsqueeze(3).to_broadcast(shape),
                                       ALU.mult).then_inc(done, 1)

                k_side, q_side = (k_msk, K_all, lg_mm, km, 0), (q_msk, Q_all, lt_mm, qm, Q_ACT)
                for side, arrived in ((k_side, k_in), (q_side, q_in)):
                    pool.wait_ge(arrived[0], 96 * (a + 1))
                    for c in range(2):
                        masked(0, c, True, *side)
                for u in range(2):
                    if u == 1:
                        for arrived in (k_in, q_in):
                            pool.wait_ge(arrived[1], 96 * (a + 1))
                    with pool.Fori(*((1, B // 2), (B // 2, B))[u]) as b:
                        for c in range(2):
                            for side in (k_side, q_side):
                                masked(b, c, False, *side)

            def ffn(fi):
                n, cb = FFN_CHUNKS[fi], CHUNK_BASE[fi]
                routed, rb = FFN_ROUTED[fi], ROUTED_BASE.get(fi)

                def split(c, s, part, hi, lo):
                    pool.wait_ge(hi, cb + c + 1)
                    src = qw[:, c, part] if FFN_MX[fi] else w_raw[:, s, part]
                    pool.tensor_tensor(w_lo_t[:, s, part], src, f32(w_hi_t[:, s, part]),
                                       ALU.subtract).then_inc(lo, 1)

                def route(c, s, i, u):
                    if u == 0:
                        pool.wait_ge(cw_in[s], 16 * (rb // 2 + i + 1))
                    pool.wait_ge(gm, 2 * (cb + c) + u + 1)
                    pool.tensor_tensor(g_t[:, u, :], g_t[:, u, :], cw_t[:, s, half(u)],
                                       ALU.mult).then_inc(g_cw, 1)

                def chunk(c, s, i, last):
                    if routed:
                        route(c, s, i, 0)
                    if not last:
                        split(c + 1, 1 - s, slice(0, 2 * D), w13_hi, w13_lo)
                    if routed:
                        route(c, s, i, 1)
                    split(c, s, slice(2 * D, FW), w2_hi, w2_lo)

                def rounded(c, u):
                    m = 2 * c + u
                    pool.wait_ge(qg_f, m + 1)
                    quant_round(pool, chain(pool, qg_2, 2 * m), qg_a[:, u, :], qg_b[:, u, :],
                                qs[:, u]).then_inc(qg_r, 1)

                split(0, 0, slice(0, 2 * D), w13_hi, w13_lo)
                if FFN_MX[fi]:
                    pool.wait_ge(h_fr, 1)
                    quant_round(pool, chain(pool, h_2), *hq_tmp[0], qs[:, 0]).then_inc(h_rd, 1)
                    for c in range(n):
                        if c + 1 < n:
                            split(c + 1, (c + 1) % 2, slice(0, 2 * D), w13_hi, w13_lo)
                        rounded(c, 0)
                        rounded(c, 1)
                        split(c, c % 2, slice(2 * D, FW), w2_hi, w2_lo)
                    return
                chunk(0, 0, 0, False)
                chunk(1, 1, 0, False)
                loop_end, tail = pairs(n)
                with pool.Fori(1, loop_end) as i:
                    chunk(2 * i, 0, i, False)
                    chunk(2 * i + 1, 1, i, False)
                for c in tail:
                    chunk(c, c % 2, c // 2, c == n - 1)

            def gqa():
                def split(g, s, part, hi, lo):
                    pool.wait_ge(hi, g + 1)
                    pool.tensor_tensor(l_lo_t[:, s, part], l_raw[:, s, part], f32(l_hi_t[:, s, part]),
                                       ALU.subtract).then_inc(lo, 1)

                def split_qk(g, s):
                    split(g, s, slice(0, LK), lw_hi, lw_lo)

                def split_o(g, s):
                    split(g, s, slice(LQ, LW), lo_hi, lo_lo)

                def norm(g):
                    for u in range(2):
                        pool.wait_ge(l_rcp, 2 * g + u + 1)
                        v = ls_t[:, u].rearrange("p b h k -> p (b h) k")
                        pool.tensor_tensor(v, v, l_rc[:, u, :].unsqueeze(2).to_broadcast([P, 8, S]),
                                           ALU.mult).then_inc(l_nrm, 1)

                def mx_round(g, s):
                    pool.wait_ge(qw_f, g + 1)
                    quant_round(pool, chain(pool, qw_2, 2 * g), qw_a[:, s, :], qw_b[:, s, :],
                                qw_s[:, s]).then_inc(qw_r, 1)

                def head(g, s, first=False, qkv=True, o=True):
                    if o and not first:
                        split_o(g + 1, 1 - s)
                    norm(g)
                    if qkv:
                        split_qk(g + 2, s)
                    mx_round(g, s)

                split_qk(0, 0)
                pool.tensor_tensor(ctx_t32, f32(ctx_hi[:]), f32(ctx_lo[:]), ALU.add).then_inc(l_ctx, 1)
                split_qk(1, 1)
                for g in range(2):
                    split_o(g, g)
                head(0, 0, first=True)
                head(1, 1)
                with pool.Fori(1, 3) as i:
                    head(2 * i, 0)
                    head(2 * i + 1, 1)
                head(6, 0, qkv=False)
                head(7, 1, qkv=False, o=False)

            for p, (kind, i) in enumerate(PHASES):
                if kind == "rope":
                    rope(i, p)
                elif kind == "ffn":
                    ffn(i)
                else:
                    gqa()

        @block.scalar
        def _(act):
            act.wait_ge(s_ctx, 16)
            act.activation(ctx_hi[:], ctx_raw, ACT.Copy).then_inc(s_act0, 1)
            act.wait_ge(s_const, 7 * 16)
            act.activation(wr_hi[:], wr_raw[:], ACT.Copy).then_inc(s_act0, 1)
            act.wait_ge(rw_in, 16)
            act.activation(rw_hi_t, rw_raw, ACT.Copy).then_inc(rw_hi, 1)
            act.wait_ge(s_ang, 13)
            act.activation(cos_t[:], cos_t[:], ACT.Sin).then_inc(s_sin, 1)
            act.activation(sin_t[:], sin_t[:], ACT.Sin).then_inc(s_sin, 1)

            def layernorm(p, mx, meanwhile=None, then=None):
                for u in range(2):
                    n = 2 * p + u
                    act.wait_ge(ln_mv, n + 1)
                    act.activation(sd[:, NT * u:NT * u + NT], mv[:, NT * u:NT * u + NT, 1], ACT.Sqrt,
                                   bias=col[:, 6:7]).then_inc(ln_sd, 1)
                    if u == 0 and meanwhile:
                        meanwhile()
                if mx:
                    for u in range(2):
                        act.wait_ge(ln_hT, 2 * p + u + 1)
                        act.activation(h_q_t[u], PS[:, 4 + 2 * u:6 + 2 * u, :], ACT.Copy).then_inc(h_f32, 1)
                for u in range(2):
                    n = 2 * p + u
                    if mx:
                        act.wait_ge(h_q, u + 1)
                        src = h_q_t[u]
                    else:
                        act.wait_ge(ln_hT, n + 1)
                        src = PS[:, 4 + 2 * u:6 + 2 * u, :]
                    act.activation(h_hi_t[:, :, half(u)], src, ACT.Copy).then_inc(h_hi, 1)
                    if then:
                        then(u)

            def rope(a, p):
                if p > 0:
                    act.wait_ge(rw_in, 16 * (a + 1))
                    act.activation(rw_hi_t, rw_raw, ACT.Copy).then_inc(rw_hi, 1)

                def rot_hi(t):
                    act.wait_ge(rp_add, 8 * a + t + 1)
                    if t >= 4:
                        act.wait_ge(rp_wr[t % 2], 16 * (4 * a + t // 2 - 1))
                    act.activation(rot[:, t % 4, 0, :], rot_a[:, t % 2, :], ACT.Copy).then_inc(rp_hi, 1)

                layernorm(p, False, then=rot_hi)
                for t in range(2, 8):
                    rot_hi(t)
                act.wait_ge(v_mm, a + 1)
                for n in range(4):
                    act.activation(v_all[:, 2 * n:2 * n + 2].rearrange("p b h d -> p (b h d)"), PS[:, 4 + n, :],
                                   ACT.Copy).then_inc(v_ev, 1)
                act.wait_ge(v_ev, 4 * (a + 1))

                def fixed(b, c):
                    for dst, src in ((q_fix, Q_all), (k_fix, K_all)):
                        act.activation(dst[0:96, c], src[0:96, GL * c:GL * c + GL, bass.ds(b * S, S)],
                                       ACT.Copy)
                    for j in range(Q_ACT):
                        s = act.activation(q_msk[c][0:96, :, j, :],
                                           Q_all[0:96, GL * c:GL * c + GL, bass.ds(b * S, S)], ACT.Copy,
                                           scale=col[0:96, 2 + j:3 + j])
                    s.then_inc(fix, 1)

                def v_fixed(b, c, free):
                    if not free:
                        act.wait_ge(at_av, 32 * a + 4 * b + 2 * c - 2)
                    vb = v_all[:, bass.ds(b, 1), 16 * c:16 * c + 16, :].rearrange("p a h d -> p (a h) d")
                    act.activation(v_fix[:, 16 * c:16 * c + 16, 0:8], vb, ACT.Copy).then_inc(v_fx, 1)

                def probs(b, c, v, free):
                    w = 32 * a + 4 * b + 2 * c + v
                    act.wait_ge(lt_mm, w + 1)
                    if not free:
                        act.wait_ge(at_av, w - 1)
                    act.activation(pT[:, v].rearrange("p h t -> p (h t)"),
                                   PS[:, 2:4, :].rearrange("p a b -> p (a b)"), ACT.Exp,
                                   scale=HD ** -0.5).then_inc(at_exp, 1)

                def o_copy(b, c):
                    act.wait_ge(at_av, 32 * a + 4 * b + 2 * c + 2)
                    act.activation(o_feat[:, c, :], PS[:, 4 + c, :], ACT.Copy).then_inc(o_ev, 1)

                def attn_hi(b, c):
                    act.wait_ge(at_z, 16 * a + 2 * b + c + 1)
                    act.activation(h_hi_t[:, c, bass.ds(b * S, S)], PS[:, 7, c * P:c * P + P],
                                   ACT.Copy).then_inc(a_hi, 1)

                def batch(b, first, last):
                    for c in range(2):
                        for v in range(2):
                            i = 2 * c + v
                            if v == 0 and not first:
                                o_copy(b - 1, c)
                            if not first or i >= 1:
                                probs(*behind(b, c, v, 1), first and i <= 2)
                            if v == 0 and c == 0 and not first:
                                fixed(b, 1)
                            if v == 0 and c == 1 and not last:
                                fixed(b + 1, 0)
                            if v == 1:
                                v_fixed(b, c, first)
                                if not first:
                                    attn_hi(b - 1, c)

                act.wait_ge(k_in[0], 96 * (a + 1))
                act.wait_ge(q_in[0], 96 * (a + 1))
                fixed(0, 0)
                fixed(0, 1)
                batch(0, True, False)
                for u in range(2):
                    if u == 1:
                        act.wait_ge(k_in[1], 96 * (a + 1))
                        act.wait_ge(q_in[1], 96 * (a + 1))
                    with act.Fori(*((1, B // 2 - 1), (B // 2 - 1, B - 1))[u]) as b:
                        batch(b, False, False)
                batch(B - 1, False, True)
                o_copy(B - 1, 0)
                probs(B - 1, 1, 1, False)
                o_copy(B - 1, 1)
                for c in range(2):
                    attn_hi(B - 1, c)

            def ffn(fi, p):
                n, cb = FFN_CHUNKS[fi], CHUNK_BASE[fi]
                lb = cb - (8 if fi > 1 else 0)
                routed, mx = FFN_ROUTED[fi], FFN_MX[fi]

                def w_src(c, s):
                    return qw[:, c, :] if mx else w_raw[:, s, :]

                def w13_split(c, s, i, free):
                    if mx:
                        act.wait_ge(qw_ok, c + 1)
                    else:
                        act.wait_ge(w13_in[s], 16 * (lb // 2 + i + 1))
                    if not free:
                        act.wait_ge(ab, 2 * (cb + c) - 2)
                    act.activation(w_hi_t[:, s, 0:2 * D], w_src(c, s)[:, 0:2 * D], ACT.Copy).then_inc(w13_hi, 1)

                def w2_split(c, s, i, free):
                    if not mx:
                        act.wait_ge(w2_in[s], 16 * (lb // 2 + i + 1))
                    if not free:
                        act.wait_ge(o_mm, 2 * (cb + c) - 2)
                    act.activation(w_hi_t[:, s, 2 * D:FW], w_src(c, s)[:, 2 * D:FW], ACT.Copy).then_inc(w2_hi, 1)

                def silu(c, u):
                    act.wait_ge(ab, 2 * (cb + c) + u + 1)
                    act.activation(sil_t[:, u, :], PS[:, 4 + 2 * u, :], ACT.Silu).then_inc(sil, 1)

                def g_split(c, u, free):
                    m = 2 * (cb + c) + u
                    if mx:
                        act.wait_ge(g_q, 2 * c + u + 1)
                    elif routed:
                        act.wait_ge(g_cw, m + 1 - 2 * cb + 2 * ROUTED_BASE[fi])
                    else:
                        act.wait_ge(gm, m + 1)
                    if not free:
                        act.wait_ge(o_mm, m - 1)
                    act.activation(g_hi_t[:, u, :], g_t[:, u, :], ACT.Copy).then_inc(g_hi, 1)

                act.wait_ge(x_out, 2 * p)
                layernorm(p, mx, meanwhile=lambda: w13_split(0, 0, 0, True))
                if routed:
                    act.wait_ge(r_pr, 1 if fi == 0 else 2)
                    act.activation(r_lgT[0:E, :], PS[0:E, 0:2, :].rearrange("p a b -> p (a b)"),
                                   ACT.Copy).then_inc(r_ev, 1)
                    if fi == 0:
                        act.wait_ge(r_sub, 1)
                        act.activation(r_ex, r_lg, ACT.Exp).then_inc(r_act, 1)
                    else:
                        act.wait_ge(r_mm, 2)
                        act.activation(r_ex, PS[:, 2, 0:2 * NT * E].rearrange("p (n e) -> p n e", e=E),
                                       ACT.Sigmoid).then_inc(r_act, 1)
                if mx:
                    for c in range(n):
                        silu(c, 0)
                        if c:
                            g_split(c - 1, 0, c == 1)
                        silu(c, 1)
                        if c + 1 < n:
                            w13_split(c + 1, (c + 1) % 2, 0, c == 0)
                        if c:
                            g_split(c - 1, 1, c == 1)
                        w2_split(c, c % 2, 0, c < 2)
                    g_split(n - 1, 0, False)
                    g_split(n - 1, 1, False)
                    return
                w13_split(1, 1, 0, True)
                silu(0, 0)
                w2_split(0, 0, 0, True)
                silu(0, 1)
                g_split(0, 0, True)

                def chunk(c, s, i, first, last):
                    if not last:
                        w13_split(c + 1, 1 - s, i + s, False)
                    silu(c, 0)
                    g_split(c - 1, 1, first)
                    w2_split(c, s, i, first)
                    silu(c, 1)
                    g_split(c, 0, False)

                chunk(1, 1, 0, True, False)
                loop_end, tail = pairs(n)
                with act.Fori(1, loop_end) as i:
                    chunk(2 * i, 0, i, False, False)
                    chunk(2 * i + 1, 1, i, False, False)
                for c in tail:
                    chunk(c, c % 2, c // 2, False, c == n - 1)
                g_split(n - 1, 1, False)

            def gqa(p):
                act.wait_ge(x_out, 2 * p)

                def split_qk(g, s, i):
                    act.wait_ge(lw_in[s], 16 * (i + 1))
                    if g is not None:
                        act.wait_ge(lk_mm, 2 * g - 2)
                        act.wait_ge(lv_mm, g - 1)
                    act.activation(lv_w[:, s, :], l_raw[:, s, LK:LQ], ACT.Copy)
                    act.activation(l_hi_t[:, s, 0:LK], l_raw[:, s, 0:LK], ACT.Copy).then_inc(lw_hi, 1)

                def split_o(g, s, i):
                    act.wait_ge(lw_in[s], 16 * (i + 1))
                    if g is not None:
                        act.wait_ge(l_out, 2 * g - 2)
                    act.activation(l_hi_t[:, s, LQ:LW], l_raw[:, s, LQ:LW], ACT.Copy).then_inc(lo_hi, 1)

                def q_copy(g, h):
                    for u in range(2):
                        act.wait_ge(lq_mm, 4 * g + 2 * h + u + 1)
                        act.activation(lq_t[:, h, half(u)], PS[:, 4 + 2 * h + u, :], ACT.Copy).then_inc(lq_ev, 1)

                def k_copy(g):
                    for u in range(2):
                        act.wait_ge(lk_mm, 2 * g + u + 1)
                        act.activation(lk_t[:, half(u)], PS[:, 4 + u, :], ACT.Copy).then_inc(lk_ev, 1)

                def head(g, s, i, first=False, qkv=True, o=True):
                    for u in range(2):
                        act.wait_ge(l_sub, 2 * g + u + 1)
                        v = ls_t[:, u].rearrange("p b h k -> p (b h k)")
                        act.activation(v, v, ACT.Exp, scale=D2 ** -0.5).then_inc(l_exp, 1)
                    if o:
                        q_copy(g + 1, 0)
                        if not first:
                            split_o(g + 1, 1 - s, i + s)
                        q_copy(g + 1, 1)
                        k_copy(g + 1)
                    if qkv:
                        split_qk(g + 2, s, i + 1)
                    for u in range(2):
                        act.wait_ge(l_T, 2 * g + u + 1)
                        act.activation(lp_t[:, u].rearrange("p b h k -> p (b h k)"),
                                       PS[:, 4 + 2 * u:6 + 2 * u, :].rearrange("p a b -> p (a b)"),
                                       ACT.Copy).then_inc(l_pT, 1)
                    for u in range(2):
                        act.wait_ge(l_av, 2 * g + u + 1)
                        act.activation(
                            lo_hi_t[:, :, half(u)].rearrange("p h (b t) -> p b h t", b=4),
                            PS[:, 4 + 2 * u:6 + 2 * u, :].rearrange("p a (b h t) -> p (a b) h t", b=2, h=2),
                            ACT.Copy).then_inc(l_ohi, 1)

                def first_qk():
                    for g in range(2):
                        split_qk(None, g, 0)

                layernorm(p, False, meanwhile=first_qk)
                for g in range(2):
                    split_o(None, g, 0)
                q_copy(0, 0)
                q_copy(0, 1)
                k_copy(0)
                head(0, 0, 0, first=True)
                head(1, 1, 0)
                with act.Fori(1, 3) as i:
                    head(2 * i, 0, i)
                    head(2 * i + 1, 1, i)
                head(6, 0, 3, qkv=False)
                head(7, 1, 3, qkv=False, o=False)

            for p, (kind, i) in enumerate(PHASES):
                if kind == "rope":
                    rope(i, p)
                elif kind == "ffn":
                    ffn(i, p)
                else:
                    gqa(p)

        @block.tensor
        def _(pe):
            pe.wait_ge(s_const, 7 * 16)
            pe.wait_ge(s_act0, 2)
            pe.wait_ge(s_dve0, 4)

            def ln_forward(p):
                for u in range(2):
                    wait_x(pe, p, u)
                    for t in range(NT):
                        for k in range(KC):
                            tr = pe.transpose(PS[:, 4 + 2 * u + t // 2, (t % 2) * D + k * P:(t % 2) * D + k * P + P],
                                              X[:, k, u * H + t * P:u * H + t * P + P], ident[:])
                    tr.then_inc(ln_xT, 1)

            def ln_back(p):
                for u in range(2):
                    pe.wait_ge(ln_h, 2 * p + u + 1)
                    for t in range(NT):
                        for k in range(KC):
                            tr = pe.transpose(PS[:, 4 + 2 * u + k, t * P:t * P + P],
                                              h_tok[:, NT * u + t, k * P:k * P + P], ident[:])
                    tr.then_inc(ln_hT, 1)

            def rope(a, p):
                def w(off, n):
                    return rw_hi_t[:, off:off + n], rw_lo_t[:, off:off + n]

                def rotate(t):
                    u, j, bank = t // 4, t % 4, 2 * (t % 2)
                    m = j % 2
                    if t >= 2:
                        pe.wait_ge(rp_mul, 8 * a + t - 1)
                    if j == 2:
                        pe.wait_ge(h_lo, 2 * p + u + 1)
                    for swapped in range(2):
                        if j < 2:
                            wk = w(1024 + swapped * D + m * P, P)
                            sides = [(*wk, ctx_hi[:, half(u)], ctx_lo[:, half(u)])]
                        else:
                            sides = [(*w(swapped * 2 * D + k * D + m * P, P), h_hi_t[:, k, half(u)],
                                      h_lo_t[:, k, half(u)]) for k in range(KC)]
                        mm = product(pe, PS[:, bank + swapped, :], sides)
                    mm.then_inc(rp_mm, 1)

                ln_forward(p)
                pe.wait_ge(rw_hi, a + 1)
                pe.wait_ge(rw_lo, a + 1)
                rotate(0)
                rotate(1)
                ln_back(p)
                for t in range(2, 8):
                    rotate(t)
                wv = w(1536, D)
                for b in range(B):
                    c = slice(b * S, b * S + S)
                    mm = product(pe, PS[:, 4 + b // 2, (b % 2) * D:(b % 2) * D + D],
                                 [(ctx_hi[:, c], ctx_lo[:, c], *wv)])
                mm.then_inc(v_mm, 1)

                def score(b, c, v, free):
                    w_ = 32 * a + 4 * b + 2 * c + v
                    if v == 0:
                        pe.wait_ge(km, 16 * a + 2 * b + c + 1)
                        pe.wait_ge(fix, 16 * a + 2 * b + c + 1)
                    if not free:
                        pe.wait_ge(at_mx, w_)
                    for g in range(2):
                        mm = pe.matmul(PS[:, g, :], q_fix[0:96, c, 2 * v + g, :],
                                       k_msk[c][0:96, 2 * v + g].rearrange("p j t -> p (j t)"),
                                       start=True, stop=True)
                    mm.then_inc(lg_mm, 1)

                def score_t(b, c, v, free):
                    w_ = 32 * a + 4 * b + 2 * c + v
                    if v == 0:
                        pe.wait_ge(qm, 16 * a + 2 * b + c + 1)
                    if not free:
                        pe.wait_ge(at_exp, w_)
                    for g in range(2):
                        pe.matmul(PS[:, 2 + g, :], k_fix[0:96, c, 2 * v + g, :],
                                  q_msk[c][0:96, 2 * v + g].rearrange("p j t -> p (j t)"),
                                  start=True, stop=False)
                        if g == 0:
                            pe.wait_ge(at_dg, w_ + 1)
                        mm = pe.matmul(PS[:, 2 + g, :], minus_one,
                                       diag[:, 4 * g:4 * g + 4, :].rearrange("p h t -> p (h t)"),
                                       start=False, stop=True)
                    mm.then_inc(lt_mm, 1)

                def weigh(b, c, v, g, free):
                    w_ = 32 * a + 4 * b + 2 * c + v
                    if g == 0:
                        pe.wait_ge(at_exp, w_ + 1)
                        if v == 0:
                            pe.wait_ge(v_fx, 16 * a + 2 * b + c + 1)
                            if not free:
                                pe.wait_ge(o_ev, 16 * a + 2 * b + c - 1)
                    for j in range(4):
                        n = 2 * v + g
                        mm = pe.matmul(PS[32 * j:32 * j + 32, 4 + c, n * S:n * S + S],
                                       v_fix[:, 16 * c + 4 * n + j, :], pT[:, v, 4 * g + j, :],
                                       start=True, stop=True)
                    if g == 1:
                        mm.then_inc(at_av, 1)

                def o_back(b, c, free):
                    pe.wait_ge(o_ev, 16 * a + 2 * b + c + 1)
                    if not free:
                        pe.wait_ge(a_ok, 16 * a + 2 * b + c)
                    for n in range(GL):
                        tr = pe.transpose(PS[:, 6, n * P:n * P + P], o_feat[:, c, n * P:n * P + P], ident[:])
                    tr.then_inc(o_bk, 1)

                def out_turn(b, c, last=False):
                    pe.wait_ge(a_ok, 16 * a + 2 * b + c + 1)
                    if last:
                        pe.wait_ge(a_lo, 16 * a + 2 * b + c)
                    pe.transpose(PS[:, 7, c * P:c * P + P], a_tok[:, c, :], ident[:]).then_inc(at_z, 1)

                def batch(b, first):
                    for c in range(2):
                        for v in range(2):
                            i = 2 * c + v
                            score(b, c, v, first and i == 0)
                            if not first or i >= 1:
                                score_t(*behind(b, c, v, 1), first and i == 1)
                            if not first or i >= 2:
                                weigh(*behind(b, c, v, 2), 0, first)
                            if v == 1 and not first:
                                out_turn(b - 1, c)
                            if not first or i >= 2:
                                weigh(*behind(b, c, v, 2), 1, first)
                            if v == 0 and not first:
                                o_back(b - 1, c, False)

                def out(b, c):
                    o_back(b, c, False)
                    out_turn(b, c, True)

                pe.wait_ge(v_one, 2 * (a + 1))
                pe.wait_ge(rp_lo, 8 * (a + 1))
                batch(0, True)
                with pe.Fori(1, B) as b:
                    batch(b, False)
                score_t(B - 1, 1, 1, False)
                for g in range(2):
                    weigh(B - 1, 1, 0, g, False)
                out(B - 1, 0)
                for g in range(2):
                    weigh(B - 1, 1, 1, g, False)

                def project(u):
                    for m in range(KC):
                        mm = product(pe, PS[:, 2 * m + u, :],
                                     [(*w(1792 + k * D + m * P, P), h_hi_t[:, k, half(u)], h_lo_t[:, k, half(u)])
                                      for k in range(KC)])
                    mm.then_inc(op_mm, 1)

                pe.wait_ge(at_mx, 32 * (a + 1))
                pe.wait_ge(at_exp, 32 * (a + 1))
                pe.wait_ge(a_lo, 16 * a + 8)
                project(0)
                out(B - 1, 1)
                pe.wait_ge(a_hi, 16 * (a + 1))
                pe.wait_ge(a_lo, 16 * (a + 1))
                project(1)

            def ffn(fi, p):
                n, cb = FFN_CHUNKS[fi], CHUNK_BASE[fi]
                ln_forward(p)
                ln_back(p)
                if FFN_ROUTED[fi]:
                    ri = 0 if fi == 0 else 1
                    for u in range(2):
                        pe.wait_ge(h_lo, 2 * p + u + 1)
                        mm = product(pe, PS[0:E, u, :], [(wr_hi[:, ri, k, :], wr_lo[:, ri, k, :], h_hi_t[:, k, half(u)],
                                                          h_lo_t[:, k, half(u)]) for k in range(KC)])
                    mm.then_inc(r_pr, 1)
                    pe.wait_ge(r_ev, ri + 1)
                    for j in range(2 * NT):
                        tr = pe.transpose(PS[:, 2, j * E:(j + 1) * E], r_lgT[0:E, j * P:(j + 1) * P], ident[0:E, 0:E])
                    tr.then_inc(r_mm, 1)

                def ab_mm(c, s, u, free):
                    if u == 0:
                        pe.wait_ge(w13_lo, cb + c + 1)
                    if free:
                        pe.wait_ge(h_lo, 2 * p + u + 1)
                    else:
                        pe.wait_ge(gm, 2 * (cb + c) + u - 1)
                    for x in range(2):
                        mm = product(pe, PS[:, 4 + 2 * u + x, :],
                                     [(w_hi_t[:, s, o:o + P], w_lo_t[:, s, o:o + P], h_hi_t[:, k, half(u)],
                                       h_lo_t[:, k, half(u)]) for k in range(KC) for o in [x * D + k * P]])
                    mm.then_inc(ab, 1)

                def down(c, s, u, first, last):
                    if u == 0:
                        pe.wait_ge(w2_lo, cb + c + 1)
                    pe.wait_ge(g_lo, 2 * (cb + c) + u + 1)
                    for m in range(KC):
                        o = 2 * D + m * P
                        mm = product(pe, PS[:, 2 * m + u, :],
                                     [(w_hi_t[:, s, o:o + P], w_lo_t[:, s, o:o + P], g_hi_t[:, u, :], g_lo_t[:, u, :])],
                                     start=first, stop=last)
                    mm.then_inc(o_mm, 1)

                ab_mm(0, 0, 0, True)
                ab_mm(0, 0, 1, True)
                if FFN_ROUTED[fi]:
                    if fi == 0:
                        pe.wait_ge(r_sub, 1)
                    else:
                        pe.wait_ge(r_act, 2)
                if FFN_MX[fi]:
                    for c in range(1, n + 2):
                        for u in range(2):
                            if c < n:
                                ab_mm(c, c % 2, u, False)
                            if c >= 2:
                                down(c - 2, c % 2, u, c == 2, c == n + 1)
                    return
                def chunk(c, s, first):
                    for u in range(2):
                        ab_mm(c, s, u, False)
                        down(c - 1, 1 - s, u, first, False)

                chunk(1, 1, True)
                loop_end, tail = pairs(n)
                with pe.Fori(1, loop_end) as i:
                    chunk(2 * i, 0, False)
                    chunk(2 * i + 1, 1, False)
                for c in tail:
                    chunk(c, c % 2, False)
                for u in range(2):
                    down(n - 1, (n - 1) % 2, u, False, True)

            def gqa(p):
                ln_forward(p)
                ln_back(p)

                def w(s, off, n):
                    return l_hi_t[:, s, off:off + n], l_lo_t[:, s, off:off + n]

                def qkv(g, s, first=False):
                    pe.wait_ge(lw_lo, g + 1)
                    for h in range(2):
                        if not first:
                            pe.wait_ge(l_add, 2 * g - 1 + h)
                        for u in range(2):
                            if first:
                                pe.wait_ge(h_lo, 2 * p + 2)
                            product(pe, PS[:, 4 + 2 * h + u, :],
                                    [(*w(s, k * D + h * P, P), h_hi_t[:, k, half(u)], h_lo_t[:, k, half(u)])
                                     for k in range(KC)]).then_inc(lq_mm, 1)
                    for u in range(2):
                        pe.wait_ge(lq_ev, 4 * g + u + 1)
                        product(pe, PS[:, 4 + u, :],
                                [(*w(s, 2 * D, P), ctx_hi[:, half(u)], ctx_lo[:, half(u)])]).then_inc(lk_mm, 1)
                    pe.wait_ge(lq_ev, 4 * g + 4)
                    if first:
                        pe.wait_ge(l_ctx, 1)
                    for b in range(B):
                        mm = pe.matmul(PS[:, 6 + b // 4, (b % 4) * P:(b % 4) * P + P], ctx_t32[:, b * S:b * S + S],
                                       lv_w[:, s, :], start=True, stop=True)
                    mm.then_inc(lv_mm, 1)

                def out(g, s, first, last):
                    pe.wait_ge(lo_lo, g + 1)
                    for u in range(2):
                        pe.wait_ge(l_olo, 2 * g + u + 1)
                        for m in range(KC):
                            mm = product(pe, PS[:, 2 * m + u, :],
                                         [(*w(s, LQ + h * D + m * P, P), lo_hi_t[:, h, half(u)],
                                           lo_lo_t[:, h, half(u)]) for h in range(2)],
                                         start=first, stop=last)
                        mm.then_inc(l_out, 1)

                def head(g, s, first=False, last=False):
                    pe.wait_ge(lk_ev, 2 * g + 2)
                    for u in range(2):
                        if u == 1:
                            pe.wait_ge(lv_ev, g + 1)
                        if not first:
                            pe.wait_ge(l_olo, 2 * g - 1 + u)
                        for b in range(4):
                            c = slice((4 * u + b) * S, (4 * u + b) * S + S)
                            for h in range(2):
                                o = (b % 2) * 256 + h * P
                                mm = pe.matmul(PS[:, 4 + 2 * u + b // 2, o:o + P], lq_t[:, h, c], lk_t[:, c],
                                               start=True, stop=True)
                        mm.then_inc(l_lg, 1)
                    if not first:
                        out(g - 1, 1 - s, isinstance(g, int) and g == 1, False)
                    if not last:
                        qkv(g + 1, 1 - s)
                    for u in range(2):
                        pe.wait_ge(l_nrm, 2 * g + u + 1)
                        if not last:
                            if u == 0:
                                pe.wait_ge(lk_ev, 2 * g + 4)
                            else:
                                pe.wait_ge(lv_ev, g + 2)
                        for b in range(4):
                            for h in range(2):
                                o = (b % 2) * 256 + h * P
                                tr = pe.transpose(PS[:, 4 + 2 * u + b // 2, o:o + P], ls_t[:, u, b, h, :], ident[:])
                        tr.then_inc(l_T, 1)
                    for u in range(2):
                        pe.wait_ge(l_pT, 2 * g + u + 1)
                        for b in range(4):
                            o = (b % 2) * 256
                            mm = pe.matmul(PS[:, 4 + 2 * u + b // 2, o:o + 256], lv_t[:, s, 4 * u + b, :],
                                           lp_t[:, u, b].rearrange("p h k -> p (h k)"), start=True, stop=True)
                        mm.then_inc(l_av, 1)

                qkv(0, 0, first=True)
                head(0, 0, first=True)
                head(1, 1)
                with pe.Fori(1, G2 // 2 - 1) as i:
                    head(2 * i, 0)
                    head(2 * i + 1, 1)
                head(G2 - 2, 0)
                head(G2 - 1, 1, last=True)
                out(G2 - 1, 1, False, True)

            for p, (kind, i) in enumerate(PHASES):
                if kind == "rope":
                    rope(i, p)
                elif kind == "ffn":
                    ffn(i, p)
                else:
                    gqa(p)

        @block.vector
        def _(dve):
            link_n = [0]

            def link(ins):
                link_n[0] += 1
                ins.then_inc(q_step, 1)
                dve.wait_ge(q_step, link_n[0])

            dve.memset(shared_c[:, 0, :], 1.0 / (TOPK + 1)).then_inc(s_dve0, 1)
            dve.memset(shared_c[:, 1, :], 1.0).then_inc(s_dve0, 1)
            dve.wait_ge(s_act0, 1)
            dve.tensor_tensor(ctx_lo[:], ctx_raw, f32(ctx_hi[:]),
                              ALU.subtract).then_inc(s_dve0, 1)
            dve.wait_ge(s_act0, 2)
            dve.tensor_tensor(wr_lo[:], wr_raw[:], f32(wr_hi[:]), ALU.subtract).then_inc(s_dve0, 1)
            dve.wait_ge(s_const, 7 * 16)
            link(dve.tensor_copy(mcol[:], mcol8[:]))
            ang_n = [0]

            def turn_step(ins):
                ang_n[0] += 1
                ins.then_inc(s_ang, 1)
                dve.wait_ge(s_ang, ang_n[0])

            ang = h_tok[:, 4:8, :].rearrange("p a b -> p (a b)")
            turn_step(dve.tensor_scalar(ang, cos_t[:], col[:, 0:1], None, ALU.mult))
            for dst, shift in ((sin_t, 0.0), (cos_t, 1.5707963267948966)):
                turn_step(dve.tensor_scalar(dst[:], ang, shift, None, ALU.add))
                turn_step(dve.tensor_scalar(turns, dst[:], TWO_PI_INV, ROUND, ALU.mult, ALU.add))
                turn_step(dve.tensor_scalar(turns, turns, ROUND, None, ALU.subtract))
                turn_step(dve.scalar_tensor_tensor(dst[:], turns, -PI_HI, dst[:], ALU.mult, ALU.add))
                turn_step(dve.scalar_tensor_tensor(dst[:], turns, -PI_LO, dst[:], ALU.mult, ALU.add))
                turn_step(dve.tensor_scalar(dst[:], dst[:], 3.1415925, -3.1415925, ALU.min, ALU.max))

            def layernorm(p, mx, between=None, then=None):
                for u in range(2):
                    n = 2 * p + u
                    dve.wait_ge(ln_xT, n + 1)
                    for t in range(NT):
                        s = dve.bn_stats(st6[:, t, :], PS[:, 4 + 2 * u + t // 2, (t % 2) * D:(t % 2) * D + D])
                    s.then_inc(ln_st, 1)
                    dve.wait_ge(ln_st, n + 1)
                    for t in range(NT):
                        s = dve.bn_aggr(mv[:, NT * u + t, :], st6[:, t, :])
                    s.then_inc(ln_mv, 1)
                    dve.wait_ge(ln_sd, n + 1)
                    dve.reciprocal(rstd[:, NT * u:NT * u + NT], sd[:, NT * u:NT * u + NT]).then_inc(ln_rs, 1)
                    dve.wait_ge(ln_rs, n + 1)
                    for t in range(NT):
                        j = NT * u + t
                        s = dve.tensor_scalar(h_tok[:, j, :],
                                              PS[:, 4 + 2 * u + t // 2, (t % 2) * D:(t % 2) * D + D],
                                              mv[:, j, 0:1], rstd[:, j:j + 1], ALU.subtract, ALU.mult)
                    s.then_inc(ln_h, 1)
                if between:
                    between()
                if mx:
                    for u in range(2):
                        dve.wait_ge(h_f32, u + 1)
                        quant_front(dve, link, cw_t[:, u, :], *hq_tmp[u], qs[:, u]).then_inc(h_fr, 1)
                    dve.wait_ge(h_rd, 1)
                    dve.transpose(cw_t[:, 0, :], hq_tmp[0][0]).then_inc(h_q, 1)
                    dve.wait_ge(h_fr, 2)
                    link(quant_round(dve, link, *hq_tmp[1], qs[:, 1]))
                for u in range(2):
                    n = 2 * p + u
                    if mx:
                        if u == 1:
                            dve.transpose(cw_t[:, 1, :], hq_tmp[1][0]).then_inc(h_q, 1)
                        dve.wait_ge(h_hi, n + 1)
                        src = h_q_t[u]
                    else:
                        dve.wait_ge(h_hi, n + 1)
                        src = PS[:, 4 + 2 * u:6 + 2 * u, :]
                    dve.tensor_tensor(h_lo_t[:, :, half(u)], src, f32(h_hi_t[:, :, half(u)]),
                                      ALU.subtract).then_inc(h_lo, 1)
                    if then:
                        then(u)

            def rope_weights_lo(a):
                dve.wait_ge(rw_hi, a + 1)
                dve.tensor_tensor(rw_lo_t, rw_raw, f32(rw_hi_t), ALU.subtract).then_inc(rw_lo, 1)

            def rope(a, p):
                def rot_mul(t):
                    u, bank = t // 4, 2 * (t % 2)
                    dve.wait_ge(rp_mm, 8 * a + t + 1)
                    if t >= 2:
                        dve.wait_ge(rp_lo, 8 * a + t - 1)
                    dve.tensor_tensor(rot_a[:, t % 2, :], PS[:, bank, :], cos_t[:, half(u)], ALU.mult)
                    dve.tensor_tensor(rot_b[:, t % 2, :], PS[:, bank + 1, :], sin_t[:, half(u)],
                                      ALU.mult).then_inc(rp_mul, 1)

                def rot_rest(t):
                    dve.wait_ge(rp_hi, 8 * a + t + 1)
                    dve.tensor_tensor(rot[:, t % 4, 1, :], rot_a[:, t % 2, :], f32(rot[:, t % 4, 0, :]),
                                      ALU.subtract).then_inc(rp_lo, 1)

                def k_first():
                    if p == 0:
                        dve.wait_ge(s_sin, 2)
                        link(dve.tensor_scalar(sin_t[:], sin_t[:], col[:, 1:2], None, ALU.mult))
                    for t in range(2):
                        rot_mul(t)

                if p == 0:
                    rope_weights_lo(a)
                layernorm(p, False, k_first, rot_rest)
                for t in range(2, 8):
                    rot_mul(t)
                    if t > 2:
                        rot_rest(t - 1)
                rot_rest(7)

                def o_norm(b, c):
                    un = 16 * a + 2 * b + c
                    o = PS[:, 6, :].rearrange("p (h d) -> p h d", h=16)
                    dve.wait_ge(o_bk, un + 1)
                    dve.reciprocal(o_rcp[:, c, :], o[:, :, 8]).then_inc(o_rc, 1)
                    dve.wait_ge(o_rc, un + 1)
                    dve.tensor_tensor(a_tok[:, c, :].rearrange("p (h d) -> p h d", d=8), o[:, :, 0:8],
                                      o_rcp[:, c, :].unsqueeze(2).to_broadcast([P, 16, 8]),
                                      ALU.mult).then_inc(a_ok, 1)

                def attn_lo(b, c):
                    dve.wait_ge(a_hi, 16 * a + 2 * b + c + 1)
                    dve.tensor_tensor(h_lo_t[:, c, bass.ds(b * S, S)], PS[:, 7, c * P:c * P + P],
                                      f32(h_hi_t[:, c, bass.ds(b * S, S)]), ALU.subtract).then_inc(a_lo, 1)

                def batch(b, first):
                    for c in range(2):
                        for v in range(2):
                            i = 2 * c + v
                            w = 32 * a + 4 * b + i
                            dve.wait_ge(lg_mm, w + 1)
                            dve.tensor_reduce(row_max[:, v, :],
                                              PS[:, 0:2, :].rearrange("p a (h t) -> p (a h) t", t=S),
                                              AX_X, ALU.max).then_inc(at_mx, 1)
                            if v == 1 and not first:
                                o_norm(b - 1, c)
                            dve.wait_ge(at_mx, w + 1)
                            if not first or i >= 1:
                                dve.wait_ge(lt_mm, w)
                            dve.tensor_tensor(diag, ident[:].unsqueeze(1).to_broadcast([P, 8, P]),
                                              row_max[:, v, :].unsqueeze(2).to_broadcast([P, 8, P]),
                                              ALU.mult).then_inc(at_dg, 1)
                            if v == 1 and not first:
                                attn_lo(b - 1, c)

                batch(0, True)
                with dve.Fori(1, B) as b:
                    batch(b, False)
                for c in range(2):
                    o_norm(B - 1, c)
                    attn_lo(B - 1, c)
                for u in range(2):
                    dve.wait_ge(op_mm, 2 * a + u + 1)
                    for m in range(KC):
                        s = dve.scalar_tensor_tensor(X[:, m, half(u)], PS[:, 2 * m + u, :], bias_o[:, a, m:m + 1],
                                                     X[:, m, half(u)], ALU.add, ALU.add)
                    s.then_inc(x_out, 1)

            def above(vals, e):
                shape = [P, 2 * NT, e, e]
                gt = cmp_a[:, 0:2 * NT * e * e].rearrange("p (n i j) -> p n i j", i=e, j=e)
                link(dve.tensor_tensor(gt, vals.unsqueeze(2).to_broadcast(shape), vals.unsqueeze(3).to_broadcast(shape),
                                       ALU.is_gt))

            def equal(vals, e):
                shape = [P, 2 * NT, e, e]
                eq = cmp_b[:, 0:2 * NT * e * e].rearrange("p (n i j) -> p n i j", i=e, j=e)
                link(dve.tensor_tensor(eq, vals.unsqueeze(2).to_broadcast(shape), vals.unsqueeze(3).to_broadcast(shape),
                                       ALU.is_equal))

            def earlier(e):
                shape = [P, 2 * NT, e, e]
                eq = cmp_b[:, 0:2 * NT * e * e].rearrange("p (n i j) -> p n i j", i=e, j=e)
                link(dve.tensor_tensor(eq, eq, tri[:, 0:e, 0:e].unsqueeze(1).to_broadcast(shape), ALU.mult))

            def before(e):
                n = 2 * NT * e * e
                link(dve.tensor_tensor(cmp_a[:, 0:n], cmp_a[:, 0:n], cmp_b[:, 0:n], ALU.add))

            def chosen(e, k, sel):
                n = 2 * NT * e * e
                link(dve.tensor_reduce(sel, cmp_a[:, 0:n].rearrange("p (n i j) -> p n i j", i=e, j=e), AX_X, ALU.add))
                link(dve.tensor_scalar(sel, sel, float(k), None, ALU.is_lt))

            def route_scores(fi):
                logits = PS[:, 2, 0:2 * NT * E].rearrange("p (n e) -> p n e", e=E)
                dve.wait_ge(r_mm, 1 if fi == 0 else 2)
                if fi == 0:
                    link(dve.tensor_reduce(r_s, logits, AX_X, ALU.max))
                    dve.tensor_tensor(r_lg, logits, r_s.unsqueeze(2).to_broadcast([P, 2 * NT, E]),
                                      ALU.subtract).then_inc(r_sub, 1)
                    dve.wait_ge(r_act, 1)
                    return r_ex
                groups = [v.rearrange("p n (g e) -> p n g e", g=4) for v in (r_ex, r_m)]
                dve.wait_ge(r_act, 2)
                link(dve.tensor_reduce(r_g, groups[0], AX_X, ALU.max))
                above(r_g, 4)
                equal(r_g, 4)
                earlier(4)
                before(4)
                chosen(4, 2, r_gs)
                link(dve.tensor_tensor(groups[1], groups[0], r_gs.unsqueeze(3).to_broadcast([P, 2 * NT, 4, 4]),
                                       ALU.mult))
                return r_m

            def route_weights(fi):
                link(dve.tensor_tensor(r_m, r_ex, r_sel, ALU.mult))
                link(dve.tensor_reduce(r_s, r_m, AX_X, ALU.add))
                link(dve.reciprocal(r_r, r_s))
                link(dve.tensor_scalar(r_r, r_r, TOPK / (TOPK + 1.0) if fi == 0 else 1.0, None, ALU.mult))
                link(dve.tensor_tensor(r_m, r_m, r_r.unsqueeze(2).to_broadcast([P, 2 * NT, E]), ALU.mult))
                dve.transpose(r_T, r_m.rearrange("p n e -> p (n e)")).then_inc(cw_ok, 1)

            def ffn(fi, p):
                n, cb = FFN_CHUNKS[fi], CHUNK_BASE[fi]
                routed, mx = FFN_ROUTED[fi], FFN_MX[fi]

                def gate(c, u, free):
                    m = 2 * (cb + c) + u
                    dve.wait_ge(sil, m + 1)
                    if not free:
                        dve.wait_ge(g_lo, m - 1)
                    dst = qg_b if mx else g_t
                    dve.tensor_tensor(dst[:, u, :], sil_t[:, u, :], PS[:, 5 + 2 * u, :], ALU.mult).then_inc(gm, 1)
                    if mx:
                        dve.wait_ge(gm, m + 1)
                        quant_front(dve, link, qg_b[:, u, :], qg_a[:, u, :], qg_b[:, u, :],
                                    qs[:, u]).then_inc(qg_f, 1)

                def quant_end(c, u):
                    m = 2 * c + u
                    dve.wait_ge(qg_r, m + 1)
                    if c:
                        dve.wait_ge(g_lo, 2 * cb + m - 1)
                    dve.transpose(g_t[:, u, :], qg_a[:, u, :]).then_inc(g_q, 1)

                def g_rest(c, u):
                    dve.wait_ge(g_hi, 2 * (cb + c) + u + 1)
                    dve.tensor_tensor(g_lo_t[:, u, :], g_t[:, u, :], f32(g_hi_t[:, u, :]),
                                      ALU.subtract).then_inc(g_lo, 1)

                layernorm(p, mx)
                if mx:
                    for c in range(n):
                        gate(c, 0, True)
                        if c:
                            quant_end(c - 1, 1)
                            g_rest(c - 1, 0)
                        gate(c, 1, True)
                        quant_end(c, 0)
                        if c:
                            g_rest(c - 1, 1)
                    quant_end(n - 1, 1)
                    g_rest(n - 1, 0)
                    g_rest(n - 1, 1)
                else:
                    if routed:
                        vals = route_scores(fi)
                    gate(0, 0, True)
                    if routed:
                        above(vals, E)
                    gate(0, 1, True)
                    g_rest(0, 0)
                    if routed:
                        equal(vals, E)
                    gate(1, 0, False)
                    g_rest(0, 1)
                    if routed:
                        earlier(E)
                    gate(1, 1, False)
                    g_rest(1, 0)
                    if routed:
                        before(E)
                        chosen(E, TOPK, r_sel)
                        route_weights(fi)

                    def chunk(c):
                        gate(c, 0, False)
                        g_rest(c - 1, 1)
                        gate(c, 1, False)
                        g_rest(c, 0)

                    loop_end, tail = pairs(n)
                    with dve.Fori(1, loop_end) as i:
                        chunk(2 * i)
                        chunk(2 * i + 1)
                    for c in tail:
                        chunk(c)
                    g_rest(n - 1, 1)
                if p + 1 < len(PHASES) and PHASES[p + 1][0] == "rope":
                    rope_weights_lo(PHASES[p + 1][1])
                for u in range(2):
                    dve.wait_ge(o_mm, 2 * (cb + n) - 1 + u)
                    for m in range(KC):
                        s = dve.tensor_tensor(X[:, m, half(u)], PS[:, 2 * m + u, :], X[:, m, half(u)], ALU.add)
                    s.then_inc(x_out, 1)

            def gqa(p):
                dve.wait_ge(l_mk, 16)
                link(dve.tensor_scalar(mbias.rearrange("p b k -> p (b k)"), mask8, MASKED, -MASKED,
                                       ALU.mult, ALU.add))
                layernorm(p, False)

                def mx_front(g, s, i):
                    dve.wait_ge(qw_ld[s], 16 * (i + 1))
                    quant_front(dve, chain(dve, qw_1, 6 * g), qw_in[:, s, :], qw_a[:, s, :], qw_b[:, s, :],
                                qw_s[:, s]).then_inc(qw_f, 1)

                def mx_end(g, s):
                    dve.wait_ge(qw_r, g + 1)
                    dve.transpose(qw_b[:, s, :], qw_a[:, s, :]).then_inc(qw_t, 1)
                    dve.wait_ge(qw_t, g + 1)
                    dst = qw[:, g, :] if isinstance(g, int) else \
                        qw[:, bass.ds(g, 1), :].rearrange("p a n -> p (a n)")
                    dve.tensor_copy(dst, qw_b[:, s, :]).then_inc(qw_ok, 1)

                def v_masked(g, s):
                    dve.wait_ge(lv_mm, g + 1)
                    dve.tensor_tensor(lv_t[:, s], PS[:, 6:8, :].rearrange("p a (b d) -> p (a b) d", d=D2),
                                      mcol[:].unsqueeze(2).to_broadcast([P, B, D2]), ALU.mult).then_inc(lv_ev, 1)

                def head(g, s, i, first=False, last=False):
                    for u in range(2):
                        dve.wait_ge(l_lg, 2 * g + u + 1)
                        dve.tensor_tensor(
                            ls_t[:, u], PS[:, 4 + 2 * u:6 + 2 * u, :].rearrange("p a (b h k) -> p (a b) h k", b=2, h=2),
                            mbias[:, 4 * u:4 * u + 4, :].unsqueeze(2).to_broadcast([P, 4, 2, S]),
                            ALU.add).then_inc(l_add, 1)
                    for u in range(2):
                        n = 2 * g + u
                        v = ls_t[:, u].rearrange("p b h k -> p (b h) k")
                        dve.wait_ge(l_add, n + 1)
                        dve.tensor_reduce(l_mx[:, u, :], v, AX_X, ALU.max).then_inc(l_max, 1)
                        dve.wait_ge(l_max, n + 1)
                        dve.tensor_tensor(v, v, l_mx[:, u, :].unsqueeze(2).to_broadcast([P, 8, S]),
                                          ALU.subtract).then_inc(l_sub, 1)
                    for u in range(2):
                        n = 2 * g + u
                        dve.wait_ge(l_exp, n + 1)
                        dve.tensor_reduce(l_sm[:, u, :], ls_t[:, u].rearrange("p b h k -> p (b h) k"), AX_X,
                                          ALU.add).then_inc(l_sum, 1)
                        dve.wait_ge(l_sum, n + 1)
                        dve.reciprocal(l_rc[:, u, :], l_sm[:, u, :]).then_inc(l_rcp, 1)
                    if not first:
                        mx_end(g - 1, 1 - s)
                    if not last:
                        v_masked(g + 1, 1 - s)
                    mx_front(g, s, i)
                    for u in range(2):
                        dve.wait_ge(l_ohi, 2 * g + u + 1)
                        dve.tensor_tensor(
                            lo_lo_t[:, :, half(u)].rearrange("p h (b t) -> p b h t", b=4),
                            PS[:, 4 + 2 * u:6 + 2 * u, :].rearrange("p a (b h t) -> p (a b) h t", b=2, h=2),
                            f32(lo_hi_t[:, :, half(u)]).rearrange("p h (b t) -> p b h t", b=4),
                            ALU.subtract).then_inc(l_olo, 1)

                v_masked(0, 0)
                head(0, 0, 0, first=True)
                head(1, 1, 0)
                with dve.Fori(1, 3) as i:
                    head(2 * i, 0, i)
                    head(2 * i + 1, 1, i)
                head(6, 0, 3)
                head(7, 1, 3, last=True)
                mx_end(G2 - 1, 1)
                for u in range(2):
                    dve.wait_ge(l_out, 15 + u)
                    for m in range(KC):
                        s = dve.tensor_tensor(X[:, m, half(u)], PS[:, 2 * m + u, :], X[:, m, half(u)], ALU.add)
                    s.then_inc(x_out, 1)

            for p, (kind, i) in enumerate(PHASES):
                if kind == "rope":
                    rope(i, p)
                elif kind == "ffn":
                    ffn(i, p)
                else:
                    gqa(p)


def laid_out(i):
    import numpy as np

    f4 = np.float32
    n = {k: np.asarray(v) for k, v in i.items()}

    def chunks(w):
        return w.reshape(-1, P, w.shape[1]).transpose(1, 0, 2)

    def packed(w1, w3, w2):
        c = w1.shape[1] // P
        a, b = (chunks(w).reshape(P, KC, c, P).transpose(2, 0, 1, 3).reshape(c, P, D) for w in (w1, w3))
        return np.ascontiguousarray(np.concatenate([a, b, w2.reshape(c, P, D)], 2))

    def padded(w, axis):
        pad = [(0, 0), (0, 0)]
        pad[axis] = (0, -w.shape[axis] % P)
        return np.pad(w, pad)

    swap = np.arange(D) ^ 1
    rope = []
    for l in (0, 2, 3):
        q, kv, o = n[f"L{l}_xattn_Wq"], n[f"L{l}_xattn_Wkv"], n[f"L{l}_xattn_Wout"]
        rope.append(np.concatenate([chunks(q).reshape(P, -1), chunks(q[:, swap]).reshape(P, -1), kv[:, :D],
                                    kv[:, :D][:, swap], kv[:, D:], chunks(o).reshape(P, -1)], 1))
    w0 = packed(np.concatenate([n["L0_ffn_ws1"], n["L0_ffn_we1"].transpose(1, 0, 2).reshape(D, -1)], 1),
                np.concatenate([n["L0_ffn_ws3"], n["L0_ffn_we3"].transpose(1, 0, 2).reshape(D, -1)], 1),
                np.concatenate([n["L0_ffn_ws2"], n["L0_ffn_we2"].reshape(-1, D)], 0))
    w1 = packed(n["L1_ffn_gate_w"].T, n["L1_ffn_up_w"].T, n["L1_ffn_down_w"].T)
    w2 = packed(n["L2_ffn_w_gate"].T, n["L2_ffn_w_up"].T, n["L2_ffn_w_down"].T)
    w3 = packed(padded(np.concatenate([n["L3_ffn_Ws1"], n["L3_ffn_W1"].reshape(-1, D)], 0).T, 1),
                padded(np.concatenate([n["L3_ffn_Ws3"], n["L3_ffn_W3"].reshape(-1, D)], 0).T, 1),
                padded(np.concatenate([n["L3_ffn_Ws2"].T, n["L3_ffn_W2"].transpose(0, 2, 1).reshape(-1, D)], 0), 0))
    gqa = []
    for g in range(G2):
        q = n["L1_xattn_Wq"][:, g * D:(g + 1) * D]
        k, v = (n[f"L1_xattn_{x}"][:, g * D2:(g + 1) * D2] for x in ("Wk", "Wv"))
        gqa.append(np.concatenate([chunks(q).reshape(P, -1), k, v,
                                   chunks(n["L1_xattn_Wo"][g * D:(g + 1) * D]).reshape(P, -1)], 1))
    p = np.arange(P)
    cols = np.zeros((P, 8), f4)
    cols[:, 0] = np.where((p % 4) // 2 == 0, 1.0, 10000.0 ** -0.5)
    cols[:, 1] = np.where(p % 2 == 0, -1.0, 1.0)
    for j in range(4):
        cols[:, 2 + j] = (p % 32) // HD == j
    cols[:, 6] = LN_EPS
    tri = np.tile(np.tril(np.ones((E, E), f4), -1).reshape(1, -1), (P, 1))
    pos = n["fside_BxSx2_0"].reshape(T, 2).T
    mask = n["mask_BxS2_bf1"].view(np.uint8)
    return dict(
        x_t=n["x"].reshape(T, D).T, ctx_t=n["ctx_1024"].reshape(T, P).T,
        pos_rows=pos[(p % HD) // 4], mask_row=mask.reshape(1, T), mask_col=mask.T,
        rope_w=np.stack(rope), rope_b=np.stack([n[f"L{l}_xattn_bout"].reshape(KC, P).T for l in (0, 2, 3)]),
        router_w=np.stack([chunks(n["L0_ffn_w_router"]), chunks(n["L3_ffn_gate_w"].T)]),
        ffn_w0=w0, ffn_w1=w1, ffn_w2=w2, ffn_w3=w3, gqa_w=np.stack(gqa),
        cols=cols, ident_in=np.eye(P, dtype=f4), tri_in=tri)


def kernel(**inputs):
    import numpy as np
    import concourse.bacc as bacc
    from concourse.bass_utils import run_bass_kernel_spmd

    nc = bacc.Bacc("TRN2", target_bir_lowering=False, num_devices=1)
    arrays = {f"in_{k}": np.ascontiguousarray(v) for k, v in laid_out(inputs).items()}
    args = [nc.dram_tensor(k, v.shape, mybir.dt.from_np(v.dtype), kind="ExternalInput").ap()
            for k, v in arrays.items()]
    args.append(nc.dram_tensor("out_t", (D, T), F32, kind="ExternalOutput").ap())
    build(nc, *args)
    r = run_bass_kernel_spmd(nc, [arrays], core_ids=[0])
    return np.ascontiguousarray(r.results[0]["out_t"].T).reshape(B, S, D)
```
